# Optimizing a Trainium2 kernel written in Bass

```python
import numpy as np
import jax
import jax.numpy as jnp

def _softmax(x, axis=-1):
    return jax.nn.softmax(x, axis=axis)

def _gelu(x):
    return jax.nn.gelu(x, approximate=True)

def _silu(x):
    return jax.nn.silu(x)

def _sigmoid(x):
    return jax.nn.sigmoid(x)

def _layernorm(x, axis=-1, eps=1e-05):
    m = jnp.mean(x, axis=axis, keepdims=True)
    v = jnp.var(x, axis=axis, keepdims=True)
    return (x - m) / jnp.sqrt(v + eps)

def _scatter_add(tgt, idx, src, axis=0):
    return tgt.at[idx].add(src)

def _segment_sum(src, seg, n):
    return jax.ops.segment_sum(src, seg, n)
kernel_name = 'mk_gnn_ffn_d4_gnn_r8_f8bee3'

def setup_inputs(seed: int=0):
    np.random.seed(seed)
    _w = jnp.asarray

    def _rec_inputs():
        import jax
        import jax.numpy as jnp
        _gk = jax.random.key(seed)
        x = -0.001003 + 1 * jax.random.normal(jax.random.fold_in(_gk, 1), (256, 768), jnp.float32)
        _s = jax.random.randint(jax.random.fold_in(_gk, 2), (2048,), 0, 256, jnp.int32)
        _d = jax.random.randint(jax.random.fold_in(_gk, 3), (2048,), 0, 256, jnp.int32)
        _loop = jnp.arange(256, dtype=jnp.int32)
        src = jnp.concatenate([_s, _d, _loop])
        dst = jnp.concatenate([_d, _s, _loop])
        _o = jnp.argsort(dst, stable=True)
        src = src[_o]
        dst = dst[_o]
        edge_type_3 = jax.random.randint(jax.random.fold_in(_gk, 13), (4352,), 0, 3, jnp.int32)
        return (x, src, dst, edge_type_3)
    x, src, dst, edge_type_3 = _rec_inputs()

    def _L0_gnn_setup():
        import jax, jax.numpy as jnp
        import numpy as np
        NUM_RELATIONS = 3

        def _rgcn(x, W_rel, W_root, bias, src, dst, etype):
            n = x.shape[0]
            xr = jnp.einsum('ni,rio->rno', x, W_rel)
            msg = xr[etype, src]
            out = x @ W_root + bias
            for r in range(NUM_RELATIONS):
                m = etype == r
                s = jax.ops.segment_sum(jnp.where(m[:, None], msg, 0.0), dst, num_segments=n)
                c = jax.ops.segment_sum(m.astype(x.dtype), dst, num_segments=n)
                out = out + s / jnp.maximum(c, 1.0)[:, None]
            return out

        def _gate(h, q, Wg, bg, Wq, bq):
            B, L, F = q.shape
            N = h.shape[0] // B
            h3 = h.reshape(B, N, F)
            hg = jnp.einsum('bnf,gf->bng', h3, Wg[:, :F])
            qg = jnp.einsum('blf,gf->blg', q, Wg[:, F:]) + bg
            attn = jax.nn.sigmoid(hg[:, :, None, :] + qg[:, None, :, :])
            qi = jnp.einsum('bnlf,blf->bnf', attn, q)
            alpha = jax.nn.sigmoid(jnp.einsum('bnf,gf->bng', h3, Wq[:, :F]) + jnp.einsum('bnf,gf->bng', qi, Wq[:, F:]) + bq)
            hn = alpha * jnp.tanh(qi) + (1.0 - alpha) * h3
            return hn.reshape(B * N, F)
        key = jax.random.key(seed)
        ks = jax.random.split(key, 16)
        F = 768
        BN, E, B, L = (256, 8192, 8, 64)
        s = 0.02
        return {'x': jax.random.normal(ks[0], (BN, F), jnp.float32), 'edge_index': jax.random.randint(ks[1], (2, E), 0, BN), 'edge_type': jax.random.randint(ks[2], (E,), 0, NUM_RELATIONS), 'query_embs': jax.random.normal(ks[3], (B, L, F), jnp.float32), 'W_rel1': jax.random.normal(ks[4], (NUM_RELATIONS, F, F), jnp.float32) * s, 'W_root1': jax.random.normal(ks[5], (F, F), jnp.float32) * s, 'b1': jnp.zeros((F,), jnp.float32), 'W_rel2': jax.random.normal(ks[6], (NUM_RELATIONS, F, F), jnp.float32) * s, 'W_root2': jax.random.normal(ks[7], (F, F), jnp.float32) * s, 'b2': jnp.zeros((F,), jnp.float32), 'Wg': jax.random.normal(ks[8], (F, 2 * F), jnp.float32) * s, 'bg': jnp.zeros((F,), jnp.float32), 'Wq': jax.random.normal(ks[9], (F, 2 * F), jnp.float32) * s, 'bq': jnp.zeros((F,), jnp.float32)}
    _L0_gnn_all = _L0_gnn_setup()
    _L0_gnn_in = {k: v for k, v in _L0_gnn_all.items() if k in ('query_embs', 'W_rel1', 'W_root1', 'b1', 'W_rel2', 'W_root2', 'b2', 'Wg', 'bg', 'Wq', 'bq')}
    del _L0_gnn_all

    def _L0_ffn_setup():
        import jax, jax.numpy as jnp
        import numpy as np
        key = jax.random.key(seed)
        k1, k2 = jax.random.split(key)
        B, S, D_IN, D_OUT = (4, 1024, 768, 768)
        x = jax.random.normal(k1, (B, S, D_IN), dtype=jnp.float32)
        weight = jax.random.normal(k2, (D_OUT, D_IN), dtype=jnp.float32) * (1.0 / jnp.sqrt(D_OUT))
        return {'x': x, 'weight': weight}
    _L0_ffn_all = _L0_ffn_setup()
    _L0_ffn_in = {k: v for k, v in _L0_ffn_all.items() if k in ('weight',)}
    del _L0_ffn_all

    def _L1_gnn_setup():
        import jax, jax.numpy as jnp
        import numpy as np
        N = 6250
        E = 31250
        H = 12
        D = 64
        NEG_SLOPE = 0.2
        key = jax.random.key(seed)
        k1, k2, k3, k4, k5, k6, k7 = jax.random.split(key, 7)
        h = jax.random.normal(k1, (N, H * D), dtype=jnp.float32)
        src = jnp.concatenate([jnp.arange(N, dtype=jnp.int32), jax.random.randint(k2, (E - N,), 0, N, dtype=jnp.int32)])
        dst = jnp.concatenate([jnp.arange(N, dtype=jnp.int32), jax.random.randint(k3, (E - N,), 0, N, dtype=jnp.int32)])
        xav = 1.414 / np.sqrt(D)
        W_fc = jax.random.normal(k4, (D, D), dtype=jnp.float32) * xav
        attn_l = jax.random.normal(k5, (H, D), dtype=jnp.float32) * 0.15
        attn_r = jax.random.normal(k6, (H, D), dtype=jnp.float32) * 0.15
        W_res = jax.random.normal(k7, (D, D), dtype=jnp.float32) * xav
        return {'h': h, 'W_fc': W_fc, 'attn_l': attn_l, 'attn_r': attn_r, 'W_res': W_res, 'src': src, 'dst': dst}
    _L1_gnn_all = _L1_gnn_setup()
    _L1_gnn_in = {k: v for k, v in _L1_gnn_all.items() if k in ('W_fc', 'attn_l', 'attn_r', 'W_res')}
    del _L1_gnn_all

    def _L1_ffn_setup():
        import math
        import jax, jax.numpy as jnp
        import numpy as np
        B, L, D = (8, 512, 768)
        E = 16
        TOP_K = 2
        F_EXP = 4 * D
        F_SH = F_EXP * 2 // 4
        key = jax.random.key(seed)
        ks = jax.random.split(key, 8)
        s = lambda fan_in: 1.0 / math.sqrt(fan_in)
        return {'hidden_states': jax.random.normal(ks[0], (B, L, D), jnp.float32), 'gate_weight': jax.random.uniform(ks[1], (E, D), jnp.float32, -s(D), s(D)), 'Wg': jax.random.uniform(ks[2], (E, F_EXP, D), jnp.float32, -s(D), s(D)), 'Wu': jax.random.uniform(ks[3], (E, F_EXP, D), jnp.float32, -s(D), s(D)), 'Wd': jax.random.uniform(ks[4], (E, D, F_EXP), jnp.float32, -s(F_EXP), s(F_EXP)), 'Ws_g': jax.random.uniform(ks[5], (F_SH, D), jnp.float32, -s(D), s(D)), 'Ws_u': jax.random.uniform(ks[6], (F_SH, D), jnp.float32, -s(D), s(D)), 'Ws_d': jax.random.uniform(ks[7], (D, F_SH), jnp.float32, -s(F_SH), s(F_SH))}
    _L1_ffn_all = _L1_ffn_setup()
    _L1_ffn_in = {k: v for k, v in _L1_ffn_all.items() if k in ('gate_weight', 'Wg', 'Wu', 'Wd', 'Ws_g', 'Ws_u', 'Ws_d')}
    del _L1_ffn_all

    def _L2_gnn_setup():
        import jax, jax.numpy as jnp
        import numpy as np
        N = 2500
        DEG = 16
        E = N * DEG
        H = 12
        DIN = 64
        DOUT = 64
        NEG_SLOPE = 0.2
        key = jax.random.key(seed)
        k_h, k_src, k_w, k_al, k_ar, k_wr = jax.random.split(key, 6)
        std = 1.414 * np.sqrt(2.0 / (DIN + DOUT))
        h = jax.random.normal(k_h, (N, H * DIN), dtype=jnp.float32)
        src = jax.random.randint(k_src, (E,), 0, N, dtype=jnp.int64)
        dst = jnp.repeat(jnp.arange(N, dtype=jnp.int64), DEG)
        W = jax.random.normal(k_w, (DOUT, DIN), dtype=jnp.float32) * std
        attn_l = jax.random.normal(k_al, (1, H, DOUT), dtype=jnp.float32) * std
        attn_r = jax.random.normal(k_ar, (1, H, DOUT), dtype=jnp.float32) * std
        W_res = jax.random.normal(k_wr, (DOUT, DIN), dtype=jnp.float32) * std
        return {'h': h, 'src': src, 'dst': dst, 'W': W, 'attn_l': attn_l, 'attn_r': attn_r, 'W_res': W_res}
    _L2_gnn_all = _L2_gnn_setup()
    _L2_gnn_in = {k: v for k, v in _L2_gnn_all.items() if k in ('W', 'attn_l', 'attn_r', 'W_res')}
    del _L2_gnn_all

    def _L2_ffn_setup():
        import jax, jax.numpy as jnp
        import numpy as np
        E = 8
        K = 2
        D = 768
        F = 4 * D
        key = jax.random.key(seed)
        ks = jax.random.split(key, 10)
        s_exp = 0.02
        return {'x': jax.random.normal(ks[0], (4, 1024, D), jnp.float32), 'W1': jax.random.normal(ks[1], (E, F, D), jnp.float32) * s_exp, 'b1': jax.random.normal(ks[2], (E, F), jnp.float32) * s_exp, 'W2': jax.random.normal(ks[3], (E, D, F), jnp.float32) * s_exp, 'b2': jax.random.normal(ks[4], (E, D), jnp.float32) * s_exp, 'Wr1': jax.random.normal(ks[5], (D, D), jnp.float32) * s_exp, 'br1': jax.random.normal(ks[6], (D,), jnp.float32) * s_exp, 'Wr2': jax.random.normal(ks[7], (E, D), jnp.float32) * s_exp, 'br2': jax.random.normal(ks[8], (E,), jnp.float32) * s_exp}
    _L2_ffn_all = _L2_ffn_setup()
    _L2_ffn_in = {k: v for k, v in _L2_ffn_all.items() if k in ('W1', 'b1', 'W2', 'b2', 'Wr1', 'br1', 'Wr2', 'br2')}
    del _L2_ffn_all

    def _L3_gnn_setup():
        import jax, jax.numpy as jnp
        import numpy as np
        N_NODES = 1250
        N_EDGES = 12500
        DIM = 768
        key = jax.random.key(seed)
        k1, k2, k3, k4 = jax.random.split(key, 4)
        x = jax.random.normal(k1, (N_NODES, DIM), dtype=jnp.float32)
        edge_index = jax.random.randint(k2, (2, N_EDGES), 0, N_NODES, dtype=jnp.int32)
        W = jax.random.normal(k3, (DIM, DIM), dtype=jnp.float32) / np.sqrt(DIM)
        b = jnp.zeros((DIM,), dtype=jnp.float32)
        return {'x': x, 'edge_index': edge_index, 'W': W, 'b': b}
    _L3_gnn_all = _L3_gnn_setup()
    _L3_gnn_in = {k: v for k, v in _L3_gnn_all.items() if k in ('W', 'b')}
    del _L3_gnn_all

    def _L3_ffn_setup():
        import jax, jax.numpy as jnp
        import numpy as np
        D_MODEL = 768
        D_FF = 384
        NUM_EXPERTS = 8
        EXPERT_CAPACITY = 1024
        key = jax.random.key(seed)
        k0, k1, k2, k3 = jax.random.split(key, 4)
        hidden_states = jax.random.normal(k0, (2, 1024, D_MODEL), dtype=jnp.float32)
        router_w = jax.random.normal(k1, (D_MODEL, NUM_EXPERTS), dtype=jnp.float32) * D_MODEL ** (-0.5)
        wi = jax.random.normal(k2, (NUM_EXPERTS, D_MODEL, D_FF), dtype=jnp.float32) * D_MODEL ** (-0.5)
        wo = jax.random.normal(k3, (NUM_EXPERTS, D_FF, D_MODEL), dtype=jnp.float32) * D_FF ** (-0.5)
        return {'hidden_states': hidden_states, 'router_w': router_w, 'wi': wi, 'wo': wo}
    _L3_ffn_all = _L3_ffn_setup()
    _L3_ffn_in = {k: v for k, v in _L3_ffn_all.items() if k in ('router_w', 'wi', 'wo')}
    del _L3_ffn_all
    return {'x': x, 'src': src, 'dst': dst, 'edge_type_3': edge_type_3, 'L0_gnn_query_embs': _L0_gnn_in['query_embs'], 'L0_gnn_W_rel1': _L0_gnn_in['W_rel1'], 'L0_gnn_W_root1': _L0_gnn_in['W_root1'], 'L0_gnn_b1': _L0_gnn_in['b1'], 'L0_gnn_W_rel2': _L0_gnn_in['W_rel2'], 'L0_gnn_W_root2': _L0_gnn_in['W_root2'], 'L0_gnn_b2': _L0_gnn_in['b2'], 'L0_gnn_Wg': _L0_gnn_in['Wg'], 'L0_gnn_bg': _L0_gnn_in['bg'], 'L0_gnn_Wq': _L0_gnn_in['Wq'], 'L0_gnn_bq': _L0_gnn_in['bq'], 'L0_ffn_weight': _L0_ffn_in['weight'], 'L1_gnn_W_fc': _L1_gnn_in['W_fc'], 'L1_gnn_attn_l': _L1_gnn_in['attn_l'], 'L1_gnn_attn_r': _L1_gnn_in['attn_r'], 'L1_gnn_W_res': _L1_gnn_in['W_res'], 'L1_ffn_gate_weight': _L1_ffn_in['gate_weight'], 'L1_ffn_Wg': _L1_ffn_in['Wg'], 'L1_ffn_Wu': _L1_ffn_in['Wu'], 'L1_ffn_Wd': _L1_ffn_in['Wd'], 'L1_ffn_Ws_g': _L1_ffn_in['Ws_g'], 'L1_ffn_Ws_u': _L1_ffn_in['Ws_u'], 'L1_ffn_Ws_d': _L1_ffn_in['Ws_d'], 'L2_gnn_W': _L2_gnn_in['W'], 'L2_gnn_attn_l': _L2_gnn_in['attn_l'], 'L2_gnn_attn_r': _L2_gnn_in['attn_r'], 'L2_gnn_W_res': _L2_gnn_in['W_res'], 'L2_ffn_W1': _L2_ffn_in['W1'], 'L2_ffn_b1': _L2_ffn_in['b1'], 'L2_ffn_W2': _L2_ffn_in['W2'], 'L2_ffn_b2': _L2_ffn_in['b2'], 'L2_ffn_Wr1': _L2_ffn_in['Wr1'], 'L2_ffn_br1': _L2_ffn_in['br1'], 'L2_ffn_Wr2': _L2_ffn_in['Wr2'], 'L2_ffn_br2': _L2_ffn_in['br2'], 'L3_gnn_W': _L3_gnn_in['W'], 'L3_gnn_b': _L3_gnn_in['b'], 'L3_ffn_router_w': _L3_ffn_in['router_w'], 'L3_ffn_wi': _L3_ffn_in['wi'], 'L3_ffn_wo': _L3_ffn_in['wo']}

def reference(x, src, dst, edge_type_3, L0_gnn_query_embs, L0_gnn_W_rel1, L0_gnn_W_root1, L0_gnn_b1, L0_gnn_W_rel2, L0_gnn_W_root2, L0_gnn_b2, L0_gnn_Wg, L0_gnn_bg, L0_gnn_Wq, L0_gnn_bq, L0_ffn_weight, L1_gnn_W_fc, L1_gnn_attn_l, L1_gnn_attn_r, L1_gnn_W_res, L1_ffn_gate_weight, L1_ffn_Wg, L1_ffn_Wu, L1_ffn_Wd, L1_ffn_Ws_g, L1_ffn_Ws_u, L1_ffn_Ws_d, L2_gnn_W, L2_gnn_attn_l, L2_gnn_attn_r, L2_gnn_W_res, L2_ffn_W1, L2_ffn_b1, L2_ffn_W2, L2_ffn_b2, L2_ffn_Wr1, L2_ffn_br1, L2_ffn_Wr2, L2_ffn_br2, L3_gnn_W, L3_gnn_b, L3_ffn_router_w, L3_ffn_wi, L3_ffn_wo):
    import jax
    import jax.numpy as jnp

    def _L0_gnn_ref(x, edge_index, edge_type, query_embs, W_rel1, W_root1, b1, W_rel2, W_root2, b2, Wg, bg, Wq, bq):
        import jax, jax.numpy as jnp
        import numpy as np
        NUM_RELATIONS = 3

        def _rgcn(x, W_rel, W_root, bias, src, dst, etype):
            n = x.shape[0]
            xr = jnp.einsum('ni,rio->rno', x, W_rel)
            msg = xr[etype, src]
            out = x @ W_root + bias
            for r in range(NUM_RELATIONS):
                m = etype == r
                s = jax.ops.segment_sum(jnp.where(m[:, None], msg, 0.0), dst, num_segments=n)
                c = jax.ops.segment_sum(m.astype(x.dtype), dst, num_segments=n)
                out = out + s / jnp.maximum(c, 1.0)[:, None]
            return out

        def _gate(h, q, Wg, bg, Wq, bq):
            B, L, F = q.shape
            N = h.shape[0] // B
            h3 = h.reshape(B, N, F)
            hg = jnp.einsum('bnf,gf->bng', h3, Wg[:, :F])
            qg = jnp.einsum('blf,gf->blg', q, Wg[:, F:]) + bg
            attn = jax.nn.sigmoid(hg[:, :, None, :] + qg[:, None, :, :])
            qi = jnp.einsum('bnlf,blf->bnf', attn, q)
            alpha = jax.nn.sigmoid(jnp.einsum('bnf,gf->bng', h3, Wq[:, :F]) + jnp.einsum('bnf,gf->bng', qi, Wq[:, F:]) + bq)
            hn = alpha * jnp.tanh(qi) + (1.0 - alpha) * h3
            return hn.reshape(B * N, F)
        src, dst = (edge_index[0], edge_index[1])
        h = jax.nn.relu(_rgcn(x, W_rel1, W_root1, b1, src, dst, edge_type))
        h = _gate(h, query_embs, Wg, bg, Wq, bq)
        h = jax.nn.relu(_rgcn(h, W_rel2, W_root2, b2, src, dst, edge_type))
        h = _gate(h, query_embs, Wg, bg, Wq, bq)
        return h

    def _L0_ffn_ref(x, weight):
        import jax, jax.numpy as jnp
        import numpy as np
        w_bin = jnp.sign(weight)
        return jnp.einsum('bsi,oi->bso', x, w_bin)

    def _L1_gnn_ref(h, W_fc, attn_l, attn_r, W_res, src, dst):
        import jax, jax.numpy as jnp
        import numpy as np
        N = 6250
        E = 31250
        H = 12
        D = 64
        NEG_SLOPE = 0.2
        n = h.shape[0]
        hh = h.reshape(n, H, D)
        ft = jnp.einsum('nhd,ed->nhe', hh, W_fc)
        a1 = jnp.einsum('nhd,hd->nh', ft, attn_l)
        a2 = jnp.einsum('nhd,hd->nh', ft, attn_r)
        e = jax.nn.leaky_relu(a1[src] + a2[dst], negative_slope=NEG_SLOPE)
        m = jax.ops.segment_max(e, dst, num_segments=n)
        ee = jnp.exp(e - m[dst])
        denom = jax.ops.segment_sum(ee, dst, num_segments=n)
        alpha = ee / denom[dst]
        agg = jax.ops.segment_sum(alpha[:, :, None] * ft[src], dst, num_segments=n)
        res = jnp.einsum('nhd,ed->nhe', hh, W_res)
        return jax.nn.relu((res + agg).reshape(n, H * D))

    def _L1_ffn_ref(hidden_states, gate_weight, Wg, Wu, Wd, Ws_g, Ws_u, Ws_d):
        import math
        import jax, jax.numpy as jnp
        import numpy as np
        B, L, D = (8, 512, 768)
        E = 16
        TOP_K = 2
        F_EXP = 4 * D
        F_SH = F_EXP * 2 // 4
        b, l, d = hidden_states.shape
        n = b * l
        x = hidden_states.reshape(n, d)
        scores = jax.nn.sigmoid(x @ gate_weight.T)
        capacity = math.ceil(n / E * TOP_K)
        topk_score, topk_ids = jax.lax.top_k(scores.T, capacity)
        xg = x[topk_ids]
        gate = jax.nn.silu(jnp.einsum('ecd,efd->ecf', xg, Wg))
        up = jnp.einsum('ecd,efd->ecf', xg, Wu)
        out = jnp.einsum('ecf,edf->ecd', gate * up, Wd)
        out = out * topk_score[..., None]
        y = jnp.zeros((n, d), x.dtype).at[topk_ids.reshape(-1)].add(out.reshape(-1, d))
        y = y.reshape(b, l, d)
        shared = jax.nn.silu(hidden_states @ Ws_g.T) * (hidden_states @ Ws_u.T) @ Ws_d.T
        return y + shared

    def _L2_gnn_ref(h, src, dst, W, attn_l, attn_r, W_res):
        import jax, jax.numpy as jnp
        import numpy as np
        N = 2500
        DEG = 16
        E = N * DEG
        H = 12
        DIN = 64
        DOUT = 64
        NEG_SLOPE = 0.2
        n = h.shape[0]
        hv = h.reshape(n, H, DIN)
        ft = jnp.einsum('nhd,od->nho', hv, W)
        a1 = jnp.sum(ft * attn_l, axis=-1)
        a2 = jnp.sum(ft * attn_r, axis=-1)
        e = jax.nn.leaky_relu(a1[src] + a2[dst], negative_slope=NEG_SLOPE)
        m = jax.ops.segment_max(e, dst, num_segments=n)
        m = jnp.where(jnp.isfinite(m), m, 0.0)
        w = jnp.exp(e - m[dst])
        denom = jax.ops.segment_sum(w, dst, num_segments=n)
        alpha = w / jnp.maximum(denom[dst], 1e-16)
        msg = alpha[:, :, None] * ft[src]
        agg = jax.ops.segment_sum(msg, dst, num_segments=n)
        res = jnp.einsum('nhd,od->nho', hv, W_res)
        out = jax.nn.relu((agg + res).reshape(n, H * DOUT))
        return out

    def _L2_ffn_ref(x, W1, b1, W2, b2, Wr1, br1, Wr2, br2):
        import jax, jax.numpy as jnp
        import numpy as np
        E = 8
        K = 2
        D = 768
        F = 4 * D
        h = jax.nn.relu(jnp.einsum('bsd,hd->bsh', x, Wr1) + br1)
        score = jnp.einsum('bsd,ed->bse', h, Wr2) + br2
        _, idx = jax.lax.top_k(score, K)
        mask = (jax.nn.one_hot(idx, E) > 0).any(axis=-2)
        w = jax.nn.softmax(jnp.where(mask, score, -jnp.inf), axis=-1)
        out = jnp.zeros_like(x)
        for e in range(E):
            mid = jax.nn.relu(jnp.einsum('bsd,fd->bsf', x, W1[e]) + b1[e])
            ye = jnp.einsum('bsf,df->bsd', mid, W2[e]) + b2[e]
            out = out + w[..., e:e + 1] * ye
        return out

    def _L3_gnn_ref(x, edge_index, W, b):
        import jax, jax.numpy as jnp
        import numpy as np
        N_NODES = 1250
        N_EDGES = 12500
        DIM = 768
        n = x.shape[0]
        loop = jnp.arange(n, dtype=edge_index.dtype)
        src = jnp.concatenate([edge_index[0], loop])
        dst = jnp.concatenate([edge_index[1], loop])
        deg = jax.ops.segment_sum(jnp.ones_like(dst, dtype=x.dtype), dst, num_segments=n)
        deg_inv_sqrt = jnp.where(deg > 0, jax.lax.rsqrt(deg), 0.0)
        norm = deg_inv_sqrt[src] * deg_inv_sqrt[dst]
        h = x @ W
        msg = h[src] * norm[:, None]
        out = jax.ops.segment_sum(msg, dst, num_segments=n)
        return out + b

    def _L3_ffn_ref(hidden_states, router_w, wi, wo):
        import jax, jax.numpy as jnp
        import numpy as np
        D_MODEL = 768
        D_FF = 384
        NUM_EXPERTS = 8
        EXPERT_CAPACITY = 1024
        B, S, d = hidden_states.shape
        E = router_w.shape[1]
        x = hidden_states.reshape(-1, d)
        logits = x.astype(jnp.float32) @ router_w.astype(jnp.float32)
        probs = jax.nn.softmax(logits, axis=-1).astype(x.dtype)
        p = jnp.max(probs, axis=-1)
        e_idx = jnp.argmax(probs, axis=-1)
        mask = jax.nn.one_hot(e_idx, E, dtype=x.dtype)
        token_priority = jnp.cumsum(mask[:, None, :], axis=-2)[:, 0, :]
        mask = mask * (token_priority <= EXPERT_CAPACITY).astype(x.dtype)
        combine = mask * p[:, None]

        def body(acc, ew):
            Wi_e, Wo_e, w_e = ew
            h = jax.nn.relu(x @ Wi_e) @ Wo_e
            return (acc + w_e[:, None] * h, None)
        out, _ = jax.lax.scan(body, jnp.zeros_like(x), (wi, wo, combine.T))
        return out.reshape(B, S, d)
    edge_index = jnp.stack([src, dst])
    x = x + _L0_gnn_ref(_layernorm(x, axis=-1), edge_index, edge_type_3, L0_gnn_query_embs, L0_gnn_W_rel1, L0_gnn_W_root1, L0_gnn_b1, L0_gnn_W_rel2, L0_gnn_W_root2, L0_gnn_b2, L0_gnn_Wg, L0_gnn_bg, L0_gnn_Wq, L0_gnn_bq)
    x = x + _L0_ffn_ref(_layernorm(x, axis=-1)[None], L0_ffn_weight)[0]
    x = x + _L1_gnn_ref(_layernorm(x, axis=-1), L1_gnn_W_fc, L1_gnn_attn_l, L1_gnn_attn_r, L1_gnn_W_res, src, dst)
    x = x + _L1_ffn_ref(_layernorm(x, axis=-1)[None], L1_ffn_gate_weight, L1_ffn_Wg, L1_ffn_Wu, L1_ffn_Wd, L1_ffn_Ws_g, L1_ffn_Ws_u, L1_ffn_Ws_d)[0]
    x = x + _L2_gnn_ref(_layernorm(x, axis=-1), src, dst, L2_gnn_W, L2_gnn_attn_l, L2_gnn_attn_r, L2_gnn_W_res)
    x = x + _L2_ffn_ref(_layernorm(x, axis=-1)[None], L2_ffn_W1, L2_ffn_b1, L2_ffn_W2, L2_ffn_b2, L2_ffn_Wr1, L2_ffn_br1, L2_ffn_Wr2, L2_ffn_br2)[0]
    x = x + _L3_gnn_ref(_layernorm(x, axis=-1), edge_index, L3_gnn_W, L3_gnn_b)
    x = x + _L3_ffn_ref(_layernorm(x, axis=-1)[None], L3_ffn_router_w, L3_ffn_wi, L3_ffn_wo)[0]
    return x

_drawn_inputs = setup_inputs


def setup_inputs(seed=0):
    import zlib

    import numpy as np

    out = dict(_drawn_inputs(seed))
    spreads = {'L0_gnn_b1': (0.0, 0.688),
     'L0_gnn_b2': (0.0, 0.1),
     'L0_gnn_bg': (0.0, 0.538),
     'L0_gnn_bq': (0.0, 0.678),
     'L3_gnn_b': (0.0, 2.0)}
    factors = {'L1_gnn_W_fc': 2.778,
     'L1_gnn_attn_l': 3.096,
     'L1_gnn_attn_r': 8.0,
     'L1_ffn_gate_weight': 8.0,
     'L1_ffn_Wg': 8.0,
     'L1_ffn_Wu': 8.0,
     'L1_ffn_Wd': 8.0,
     'L1_ffn_Ws_g': 8.0,
     'L1_ffn_Ws_u': 8.0,
     'L1_ffn_Ws_d': 8.0,
     'L2_gnn_W': 2.843,
     'L2_gnn_attn_l': 2.837,
     'L2_gnn_attn_r': 28.44,
     'L2_ffn_W1': 7.479,
     'L2_ffn_b1': 44.667,
     'L2_ffn_W2': 6.139,
     'L2_ffn_b2': 64.0,
     'L2_ffn_Wr1': 7.792,
     'L2_ffn_br1': 8.0,
     'L2_ffn_Wr2': 6.999,
     'L2_ffn_br2': 29.703,
     'L3_gnn_W': 6.308,
     'L3_ffn_router_w': 7.191,
     'L3_ffn_wi': 7.935,
     'L3_ffn_wo': 6.608,
     'L2_gnn_W_res': 3.156}
    for name, (base, spread) in spreads.items():
        noise = np.random.default_rng([zlib.crc32(name.encode()), seed]).standard_normal(out[name].shape)
        drawn = base * np.exp(spread * noise) if base else spread * noise
        out[name] = jnp.asarray(drawn.astype(out[name].dtype))
    for name, factor in factors.items():
        out[name] = (out[name] * factor).astype(out[name].dtype)
    return out
```

```python
from contextlib import ExitStack

import concourse.bass as bass
from concourse import mybir

ALU = mybir.AluOpType
ACT = mybir.ActivationFunctionType
AX = mybir.AxisListType
F32 = mybir.dt.float32
BF16 = mybir.dt.bfloat16
I32 = mybir.dt.int32

P = 128
N = 256
NH = N // P
D = 768
KD = D // P
HD = D // 2
EDGES = 4352
EC = EDGES // P
REL = 3
B, NB, L = 8, 32, 64
HEADS, HE = 12, 64
HG = 3
E1, SLOTS, FT1 = 16, 32, 24
E2, FT2 = 8, 24
E3, FT3 = 8, 3
SH_FT = 12
UB = 36
UW = UB * P
RING = 4
EPS = 1e-5
FAR = -1e30

U_QG = 0
U_RG1 = 1
U_GT1 = U_RG1 + 4
U_RG2 = U_GT1 + 3
U_GT2 = U_RG2 + 4
U_FF0 = U_GT2 + 3
U_SH = U_FF0 + 1
U_E1 = U_SH + SH_FT // 2
U_R2 = U_E1 + E1 * FT1 // 2
U_E2 = U_R2 + 1
U_L3G = U_E2 + E2 * FT2 // 3
U_E3 = U_L3G + 1
UNITS = U_E3 + E3
STAGE_UNITS = [U_FF0, U_SH, U_SH, U_R2, U_R2, U_L3G, U_E3, UNITS]
STAGES = 8

SMALL = {}
_at = 0
for _n, _w in (("b1", KD), ("b2", KD), ("bg", KD), ("bq", KD), ("br1", KD), ("fb1", E2 * FT2),
               ("gate", KD * E1), ("wr2", KD * E2), ("rw", KD * E3),
               ("fc1", HE), ("res1", HE), ("al1", KD), ("ar1", KD),
               ("fc2", HE), ("res2", HE), ("al2", KD), ("ar2", KD)):
    SMALL[_n] = (_at, _w)
    _at += _w
SMALL_W = _at


class Chain:

    def __init__(self, eng, sem):
        self.eng, self.sem, self.count, self.past = eng, sem, 0, 0

    def __call__(self, ins):
        self.count += 1
        ins.then_inc(self.sem, 1)
        self.eng.wait_ge(self.sem, self.past + self.count)
        return ins

    def enter(self, i, steps):
        self.first, self.steps = self.count, steps
        self.past = i * steps

    def leave(self, trips):
        assert self.count - self.first == self.steps, (self.count - self.first, self.steps)
        self.count += self.steps * (trips - 1)
        self.past = 0


def build(nc, weights, small, edges, xin, qT, rows8, row1, out):
    ctx = ExitStack()
    with ctx:
        sems = {}

        def sem(name):
            if name not in sems:
                sems[name] = ctx.enter_context(nc.semaphore(name))
            return sems[name]

        def sb(name, shape, dt=F32):
            return ctx.enter_context(nc.sbuf_tensor(name, shape, dt))

        ps = ctx.enter_context(nc.psum_tensor("ps", [P, 8, 512], F32))
        ring = sb("ring", [P, RING, UW])
        x = sb("x", [P, NH, D])
        xn = sb("xn", [P, NH, D])
        xT = sb("xT", [P, KD, N])
        adj = sb("adj", [P, NH, REL * N])
        cT = sb("cT", [P, NH, N])
        cN = sb("cN", [P, NH, N])
        far = sb("far", [P, NH, N])
        gcn = sb("gcn", [P, NH, N])
        scratch = sb("scratch", [P, 8192])
        qTs = sb("qTs", [P, KD, B * L])
        qgT = sb("qgT", [P, KD, B * L])
        hT = sb("hT", [P, KD, N])
        hgT = sb("hgT", [P, KD, N])
        qiT = sb("qiT", [P, KD, N])
        iota = sb("iota", [P, REL * N])
        ident = sb("ident", [P, P])
        ones = sb("ones", [P, P])
        sm = sb("sm", [P, SMALL_W])
        edi = sb("edi", [P, 3, EC], I32)
        edf = sb("edf", [P, 4, EC])
        b2r = sb("b2r", [E2, D])
        rw1 = sb("rw1", [1, D + E2])
        epst = sb("epst", [P, 1])
        bnst = sb("bnst", [P, NH, 2, 6])
        mv = sb("mv", [P, NH, 2])
        sd = sb("sd", [P, NH])
        rs = sb("rs", [P, NH])
        deg = sb("deg", [P, NH])
        dis = sb("dis", [P, NH])
        low = sb("low", [P, E2, E2])
        a2 = sb("a2", [P, NH, HEADS])
        hm = sb("hm", [P, 4, HG, NH])
        rden = sb("rden", [P, NH, HEADS])
        sc1 = sb("sc1", [P, NH, E1])
        cnt = sb("cnt", [P, 3, NH, E1])
        rk = sb("rk", [P, 2, NH, E2, E2])
        rt = sb("rt", [P, 6, NH, E2])
        rsm = sb("rsm", [P, 4, NH])
        wT8 = sb("wT8", [E2, N])

        def S(name):
            a, w = SMALL[name]
            return sm[:, a:a + w]

        def view(t, off, *shape):
            n = 1
            for s in shape:
                n *= s
            f = t[:, off:off + n]
            if len(shape) == 1:
                return f
            names = "abcd"[:len(shape)]
            return f.rearrange(f"p ({' '.join(names)}) -> p {' '.join(names)}", **dict(zip(names[1:], shape[1:])))

        qflat = qTs[:, :, :].rearrange("p a b -> p (a b)")
        gflat = qgT[:, :, :].rearrange("p a b -> p (a b)")

        def nat(h):
            return ps[:, 4 + 2 * h:6 + 2 * h, 0:HD]

        def halves(t, h):
            return t[:, h, :].rearrange("p (a b) -> p a b", a=2)

        def feat(bank):
            return ps[:, bank:bank + 3, :].rearrange("p a (b n) -> p (a b) n", b=2)

        def unit(u):
            return ring[:, u % RING, :]

        def unit_done(eng, u):
            eng.wait_ge(sem(f"slot{u % RING}_used"), u // RING + 1)

        FT1_AT = 2 * HG * NH * N + 2 * NH * N
        RES_AT = FT1_AT + NH * HEADS * (HE + 1)
        assert RES_AT + NH * D <= 8192

        def pwT():
            return view(qiT[:, :, :].rearrange("p a b -> p (a b)"), 0, 4, N)

        def onehots(c):
            b = scratch[:, 0:2048].bitcast(BF16)
            o = (c % 4) * 1024
            return b[:, o:o + N], b[:, o + N:o + N + REL * N]

        units = STAGE_UNITS[STAGES - 1]
        block = ctx.enter_context(nc.Block())

        @block.sync
        def _(sp):
            sp.dma_start(edi[:, :, :], edges).then_inc(sem("edges_in"), 16)
            sp.dma_start(x[:, :, :], xin).then_inc(sem("x_in"), 16)
            sp.dma_start(sm[:, :], small).then_inc(sem("small_in"), 16)
            sp.dma_start(qTs[:, :, :], qT).then_inc(sem("q_in"), 16)
            if STAGES >= 6:
                sp.dma_start(b2r[:, :], rows8).then_inc(sem("rows_in"), 16)
                sp.dma_start(rw1[:, :], row1).then_inc(sem("row1_in"), 16)
            for s in range(min(RING, units)):
                sp.dma_start(ring[:, s, :], weights[s]).then_inc(sem(f"slot{s}_full"), 16)
            rounds, rest = divmod(units, RING)
            if rounds > 1:
                with sp.Fori(1, rounds) as r:
                    for s in range(RING):
                        sp.wait_ge(sem(f"slot{s}_used"), r)
                        sp.dma_start(ring[:, s, :], weights[bass.ds(r * RING + s, 1)].rearrange("o p n -> (o p) n")
                                     ).then_inc(sem(f"slot{s}_full"), 16)
            if rounds:
                for s in range(rest):
                    sp.wait_ge(sem(f"slot{s}_used"), rounds)
                    sp.dma_start(ring[:, s, :], weights[rounds * RING + s]).then_inc(sem(f"slot{s}_full"), 16)
            sp.wait_ge(sem("result"), 1)
            sp.dma_start(out, x[:, :, :]).then_inc(sem("stored"), 16)
            sp.wait_ge(sem("stored"), 16)

        @block.gpsimd
        def _(g):
            g.iota(iota[:, :], [[1, REL * N]], base=0, channel_multiplier=0,
                   allow_small_or_imprecise_dtypes=True).then_inc(sem("iota_set"), 1)
            g.memset(ident[:, :], 0.0).then_inc(sem("pool_set"), 1)
            g.memset(ones[:, :], 1.0).then_inc(sem("ones_set"), 1)
            g.memset(epst[:, :], EPS).then_inc(sem("ones_set"), 1)
            g.memset(low[:, :, :], 0.0).then_inc(sem("pool_set"), 1)
            g.wait_ge(sem("pool_set"), 2)
            g.affine_select(out=ident[:, :], in_=ident[:, :], compare_op=ALU.not_equal, fill=1.0, base=0,
                            pattern=[[-1, P]], channel_multiplier=1).then_inc(sem("ident_set"), 1)
            g.affine_select(out=low[:, :, :], in_=low[:, :, :], compare_op=ALU.is_ge, fill=1.0, base=0,
                            pattern=[[-1, E2], [1, E2]], channel_multiplier=0).then_inc(sem("low_set"), 1)

            def gate_sum(gate, c, par, wait):
                s = view(scratch, par * NB * L, NB, L)
                if wait is not None:
                    g.wait_ge(sem("gate_prod"), wait)
                g.tensor_tensor(s, hgf[:, bass.ds(c * NB, NB)].unsqueeze(2).to_broadcast([P, NB, L]),
                                gflat[:, bass.ds(c * L, L)].unsqueeze(1).to_broadcast([P, NB, L]),
                                ALU.add).then_inc(sem("gate_sum"), 1)

            hgf = hgT[:, :, :].rearrange("p a b -> p (a b)")
            CH = KD * B
            for gate in range(2):
                g.wait_ge(sem("hg_ready"), gate + 1)
                g.wait_ge(sem("qg_ready"), KD)
                gate_sum(gate, 0, 0, None)
                gate_sum(gate, 1, 1, None)
                with g.Fori(1, CH // 2) as i:
                    for par in range(2):
                        gate_sum(gate, i * 2 + par, par, i * 2 + (CH * gate + par - 1))

            if STAGES >= 4:
                lt = view(gflat, 0, NH, N)
                g.wait_ge(sem("ln_Tv"), 4)
                g.memset(lt, 1.0).then_inc(sem("lt_set"), 1)
                g.wait_ge(sem("lt_set"), 1)
                for h in range(NH):
                    g.affine_select(out=lt[:, h, :], in_=lt[:, h, :], compare_op=ALU.is_gt, fill=0.0, base=h * P,
                                    pattern=[[-1, N]], channel_multiplier=1).then_inc(sem("lt_set"), 1)
                g.wait_ge(sem("xsel_odd"), KD // 2)
                g.wait_ge(sem("xsel_even"), KD // 2)
                xsel = view(scratch, 0, KD, E1 * SLOTS)
                xe = [view(scratch, KD * E1 * SLOTS + p * KD * SLOTS, KD, SLOTS) for p in range(2)]
                with g.Fori(0, E1 // 2) as i:
                    for par in range(2):
                        g.wait_ge(sem("y1_free"), i * 2 + (par + 1))
                        g.tensor_copy(xe[par], xsel[:, :, bass.ds((i * 2 + par) * SLOTS, SLOTS)]
                                      ).then_inc(sem("xe_ready"), 1)

        @block.tensor
        def _(pe):
            mm = nc.tensor.matmul

            def arrived(u):
                pe.wait_ge(sem(f"slot{u % RING}_full"), 16 * (u // RING + 1))

            def used(u, last):
                last.then_inc(sem(f"slot{u % RING}_used"), 1)

            def product_T(u, bank, act, start, stop):
                w = unit(u)
                arrived(u)
                for n in range(KD):
                    for k in range(KD):
                        last = mm(feat(bank)[:, n, :], w[:, k * D + n * P:k * D + (n + 1) * P], act[:, k, :],
                                  start=start and k == 0 and n % 2 == 0, stop=stop and k == KD - 1,
                                  skip_group_check=True)
                used(u, last)
                return last

            def product_N(w, act, bias=None):
                for h in range(NH):
                    for j in range(2):
                        o = ps[:, 4 + 2 * h + j, 0:HD]
                        for k in range(KD):
                            last = mm(o, act[:, k, h * P:(h + 1) * P], w[:, k * D + j * HD:k * D + (j + 1) * HD],
                                      start=k == 0, stop=k == KD - 1 and bias is None)
                        if bias is not None:
                            last = mm(o, ones[0:1, :], bias[:, j * HD:(j + 1) * HD], start=False, stop=True)
                return last

            def layernorm_T(n):
                for h in range(NH):
                    pe.wait_ge(sem("ln_xn"), NH * n + h + 1)
                    for k in range(KD):
                        last = nc.tensor.transpose(feat(0)[:, k, h * P:(h + 1) * P],
                                                   xn[:, h, k * P:(k + 1) * P], ident[:, :])
                last.then_inc(sem("ln_tp"), 1)

            def normalised(n):
                pe.wait_ge(sem("ln_Ta"), n + 1)
                pe.wait_ge(sem("ln_Tv"), n + 1)

            pe.wait_ge(sem("ident_set"), 1)
            pe.wait_ge(sem("ones_set"), 2)
            layernorm_T(0)
            pe.wait_ge(sem("q_in"), 16)
            arrived(U_QG)
            w = unit(U_QG)
            for n in range(KD):
                if n >= 4:
                    pe.wait_ge(sem("qg_ready"), n - 3)
                for k in range(KD):
                    last = mm(ps[:, 4 + n % 4, :], w[:, k * D + n * P:k * D + (n + 1) * P], qTs[:, k, :],
                              start=k == 0, stop=k == KD - 1)
                if n < KD - 1:
                    last.then_inc(sem("qg_done"), 1)
            used(U_QG, last)

            def graph():
                for c in range(EC):
                    pe.wait_ge(sem("onehot_ready"), c + 1)
                    s_oh, k_oh = onehots(c)
                    for h in range(NH):
                        mm(ps[:, 2 * h, :], s_oh[:, h * P:(h + 1) * P], k_oh[:, 0:512],
                           start=c == 0, stop=c == EC - 1)
                        last = mm(ps[:, 2 * h + 1, 0:N], s_oh[:, h * P:(h + 1) * P], k_oh[:, 512:768],
                                  start=c == 0, stop=c == EC - 1)
                    last.then_inc(sem("onehot_used"), 1)
                pe.wait_ge(sem("adj_raw"), 1)
                for j in range(2):
                    for h in range(NH):
                        last = mm(ps[:, j, 0:HD], ones[:, :], adj[:, h, j * HD:(j + 1) * HD],
                                  start=h == 0, stop=h == NH - 1)
                last.then_inc(sem("relcount"), 1)
                pe.wait_ge(sem("cT_ready"), 1)
                for dh in range(NH):
                    for sh in range(NH):
                        last = nc.tensor.transpose(ps[:, 2, dh * N + sh * P:dh * N + (sh + 1) * P],
                                                   cT[:, sh, dh * P:(dh + 1) * P], ident[:, :])
                last.then_inc(sem("cN_tp"), 1)
                pe.wait_ge(sem("dis_ready"), 1)
                for h in range(NH):
                    last = nc.tensor.transpose(ps[:, 3, h * P:(h + 1) * P],
                                               dis[:, h:h + 1].to_broadcast([P, P]), ident[:, :])
                last.then_inc(sem("disrow"), 1)

            def rgcn(r, u0, actN, actT):
                product_T(u0, 4, actT, True, False)
                if r == 0:
                    graph()
                    pe.wait_ge(sem("adj_ready"), 1)
                    pe.wait_ge(sem("gcn_ready"), 1)
                for j in range(KD):
                    if j >= 2:
                        pe.wait_ge(sem("g_copied_a"), KD * r + j - 1)
                        pe.wait_ge(sem("g_copied_v"), KD * r + j - 1)
                    bk = 2 * (j % 2)
                    for h in range(NH):
                        mm(ps[:, bk, :], actN[:, h, j * P:(j + 1) * P], adj[:, h, 0:512],
                           start=h == 0, stop=h == NH - 1)
                    for h in range(NH):
                        last = mm(ps[:, bk + 1, 0:N], actN[:, h, j * P:(j + 1) * P], adj[:, h, 512:768],
                                  start=h == 0, stop=h == NH - 1)
                    last.then_inc(sem("g_done"), 1)
                pe.wait_ge(sem("g_copied_a"), KD * (r + 1))
                pe.wait_ge(sem("g_copied_v"), KD * (r + 1))
                for rel in range(REL):
                    product_T(u0 + 1 + rel, 4, view(scratch, rel * KD * N, KD, N), False, rel == REL - 1)

            def gate(r, u0):
                pe.wait_ge(sem("hT_ready"), r + 1)
                product_T(u0, 0, hT, True, True)
                product_T(u0 + 1, 4, hT, True, False)
                pe.wait_ge(sem("qi_ready"), (r + 1) * KD * B // 2)
                product_T(u0 + 2, 4, qiT, False, True)
                pe.wait_ge(sem("hn_ready"), r + 1)
                for h in range(NH):
                    for k in range(KD):
                        last = nc.tensor.transpose(ps[:, 4 + 2 * h + k // 3, (k % 3) * P:(k % 3 + 1) * P],
                                                   hT[:, k, h * P:(h + 1) * P], ident[:, :])
                last.then_inc(sem("hn_nat"), 1)

            normalised(0)
            pe.wait_ge(sem("qg_ready"), KD)
            rgcn(0, U_RG1, xn, xT)
            gate(0, U_GT1)
            pe.wait_ge(sem("hnat_ready"), 1)
            rgcn(1, U_RG2, xn, hT)
            gate(1, U_GT2)

            if STAGES >= 2:
                layernorm_T(1)
                arrived(U_FF0)
                normalised(1)
                pe.wait_ge(sem("sign_ready"), 1)
                last = product_N(unit(U_FF0), xT)
                used(U_FF0, last)

            def gat(n, lnidx):
                layernorm_T(lnidx)
                normalised(lnidx)
                pe.wait_ge(sem("gat_w"), n + 1)
                bd = view(gflat, 0, 2, P)
                for i, s in ((0, "ft"), (1, "res")):
                    if i:
                        pe.wait_ge(sem("ft_ready"), n + 1)
                    for h in range(NH):
                        for k in range(KD):
                            last = mm(ps[:, 4 + 2 * h + k // 3, (k % 3) * P:(k % 3 + 1) * P],
                                      xT[:, k, h * P:(h + 1) * P], bd[:, i, :], start=True, stop=True)
                    last.then_inc(sem(f"{s}_done"), 1)
                for k in range(KD):
                    last = mm(feat(0)[:, k, :], bd[:, 0, :], xT[:, k, :], start=True, stop=True)
                last.then_inc(sem("ftT_done"), 1)
                pe.wait_ge(sem("ftT_ready"), n + 1)
                al = view(gflat, 2 * P, KD, 2)
                ar = view(gflat, 2 * P + 2 * KD, KD, 2)
                for h in range(NH):
                    for k in range(KD):
                        last = mm(ps[:, 3, h * HEADS + 2 * k:h * HEADS + 2 * k + 2], hT[:, k, h * P:(h + 1) * P],
                                  ar[:, k, :], start=True, stop=True)
                last.then_inc(sem("a2_done"), 1)
                pe.wait_ge(sem("a2_ready"), n + 1)
                pe.wait_ge(sem("res_ready"), n + 1)
                for gi in range(HEADS // HG):
                    G = n * (HEADS // HG) + gi
                    if gi:
                        pe.wait_ge(sem("arow_taken"), G)
                    for q in range(HG):
                        h = gi * HG + q
                        last = mm(ps[:, q // 2, (q % 2) * N:(q % 2 + 1) * N],
                                  al[:, h // 2, h % 2:h % 2 + 1].to_broadcast([P, P]), hT[:, h // 2, :],
                                  start=True, stop=True)
                    last.then_inc(sem("arow_done"), 1)
                    pe.wait_ge(sem("att_ready"), G + 1)
                    s = view(scratch, (gi % 2) * HG * NH * N, HG, NH, N)

                    def turn(q):
                        h = gi * HG + q
                        M = n * HEADS + h
                        if h >= 2:
                            pe.wait_ge(sem("wT_ready"), M - 1)
                        for sh in range(NH):
                            for dh in range(NH):
                                last = nc.tensor.transpose(ps[:, 2 + h % 2, sh * N + dh * P:sh * N + (dh + 1) * P],
                                                           s[:, q, dh, sh * P:(sh + 1) * P], ident[:, :])
                        last.then_inc(sem("wT_done"), 1)

                    def collect(q):
                        h = gi * HG + q
                        pe.wait_ge(sem("wT_ready"), n * HEADS + h + 1)
                        wt = view(scratch, 2 * HG * NH * N + (h % 2) * NH * N, NH, N)
                        for dh in range(NH):
                            c = (h % 6) * (HE + 1)
                            for sh in range(NH):
                                last = mm(ps[:, 4 + 2 * dh + h // 6, c:c + HE + 1], wt[:, sh, dh * P:(dh + 1) * P],
                                          ft1[:, sh, h, :], start=sh == 0, stop=sh == NH - 1)
                        last.then_inc(sem("head_done"), 1)

                    ft1 = view(scratch, FT1_AT, NH, HEADS, HE + 1)
                    turn(0)
                    for q in range(HG):
                        if q + 1 < HG:
                            turn(q + 1)
                        collect(q)

            if STAGES >= 3:
                gat(0, 2)

            if STAGES >= 4:
                layernorm_T(3)
                normalised(3)
                for h in range(NH):
                    for k in range(KD):
                        last = mm(ps[:, 3, h * E1:(h + 1) * E1], xT[:, k, h * P:(h + 1) * P],
                                  S("gate")[:, k * E1:(k + 1) * E1], start=k == 0, stop=k == KD - 1)
                last.then_inc(sem("score_done"), 1)
                pe.wait_ge(sem("score_ready"), 1)
                for e in range(E1):
                    if e >= 4:
                        pe.wait_ge(sem("rank_taken"), e - 3)
                    for h in range(NH):
                        last = nc.tensor.transpose(ps[:, e % 4, h * P:(h + 1) * P],
                                                   sc1[:, h, e:e + 1].to_broadcast([P, P]), ident[:, :])
                    last.then_inc(sem("srow_done"), 1)
                pe.wait_ge(sem("onehot1_ready"), 1)
                p1 = view(qflat, 0, NH, E1 * SLOTS)
                for k in range(KD):
                    if k >= 2:
                        pe.wait_ge(sem("xsel_odd" if k % 2 else "xsel_even"), k // 2)
                    for h in range(NH):
                        last = mm(ps[:, k % 2, :], xn[:, h, k * P:(k + 1) * P], p1[:, h, :],
                                  start=h == 0, stop=h == NH - 1)
                    last.then_inc(sem("xsel_done"), 1)
                pe.wait_ge(sem("pw_ready"), 1)
                for gi in range(4):
                    for h in range(NH):
                        last = nc.tensor.transpose(ps[:, 2 + gi // 2, (gi % 2) * N + h * P:(gi % 2) * N + (h + 1) * P],
                                                   p1[:, h, gi * P:(gi + 1) * P], ident[:, :])
                last.then_inc(sem("pwT_done"), 1)

                hs = [view(scratch, 6656 + p * N, N) for p in range(4)]

                def sh_down(f):
                    u = U_SH + f // 2
                    wd = unit(u)[:, (f % 2) * 18 * P + 12 * P:(f % 2) * 18 * P + 18 * P]
                    pe.wait_ge(sem("sh_act"), f + 1)
                    for h in range(NH):
                        for j in range(2):
                            last = mm(ps[:, 4 + 2 * h + j, 0:HD], hs[f % 4][:, h * P:(h + 1) * P],
                                      wd[:, j * HD:(j + 1) * HD], start=f == 0, stop=f == SH_FT - 1)
                    if f % 2:
                        used(u, last)

                pe.wait_ge(sem("pwT_ready"), 1)
                for f in range(SH_FT):
                    u = U_SH + f // 2
                    w = unit(u)[:, (f % 2) * 18 * P:(f % 2) * 18 * P + 12 * P]
                    if f % 2 == 0:
                        arrived(u)
                    if f == 0:
                        pe.wait_ge(sem("xsel_odd"), KD // 2)
                        pe.wait_ge(sem("xsel_even"), KD // 2)
                    for i in range(2):
                        for k in range(KD):
                            last = mm(ps[:, f % 4, i * N:(i + 1) * N], w[:, (i * KD + k) * P:(i * KD + k + 1) * P],
                                      xT[:, k, :], start=k == 0, stop=k == KD - 1)
                    last.then_inc(sem("sh_gu"), 1)
                    if f:
                        sh_down(f - 1)
                sh_down(SH_FT - 1)

                xe = [view(scratch, KD * E1 * SLOTS + p * KD * SLOTS, KD, SLOTS) for p in range(2)]
                he = [view(scratch, KD * E1 * SLOTS + 2 * KD * SLOTS + p * 2 * SLOTS, 2, SLOTS) for p in range(2)]
                NU = FT1 // 2
                BODY = 2 * NU
                assert BODY % RING == 0
                with pe.Fori(0, E1 // 2) as i:
                    def e_down(par, v):
                        U = par * NU + v
                        pe.wait_ge(sem("e1_act"), i * BODY + (U + 1))
                        if v == 0:
                            pe.wait_ge(sem("y1_free"), i * 2 + (par + 1))
                        slot = (U_E1 + U) % RING
                        for ft in range(2):
                            wd = ring[:, slot, ft * 18 * P + 12 * P:ft * 18 * P + 18 * P]
                            for k in range(KD):
                                last = mm(ps[:, 2 + par, k * SLOTS:(k + 1) * SLOTS], wd[:, k * P:(k + 1) * P],
                                          he[U % 2][:, ft, :], start=v == 0 and ft == 0 and k == 0,
                                          stop=v == NU - 1 and ft == 1, skip_group_check=True)
                        last.then_inc(sem(f"slot{slot}_used"), 1)

                    for par in range(2):
                        pe.wait_ge(sem("xe_ready"), i * 2 + (par + 1))
                        for v in range(NU):
                            U = par * NU + v
                            slot = (U_E1 + U) % RING
                            pe.wait_ge(sem(f"slot{slot}_full"),
                                       i * (16 * BODY // RING) + 16 * ((U_E1 + U) // RING + 1))
                            for ft in range(2):
                                for gu in range(2):
                                    for k in range(KD):
                                        b = ft * 18 + gu * KD + k
                                        last = mm(ps[:, U % 2, (ft * 2 + gu) * SLOTS:(ft * 2 + gu + 1) * SLOTS],
                                                  ring[:, slot, b * P:(b + 1) * P], xe[par][:, k, :],
                                                  start=k == 0, stop=k == KD - 1)
                            last.then_inc(sem("gu1_done"), 1)
                            if v:
                                e_down(par, v - 1)
                        e_down(par, NU - 1)
                yT = view(gflat, 0, KD, E1 * SLOTS)
                yn = view(qflat, 0, 4, D)
                pe.wait_ge(sem("y1_free"), E1 + 2)
                for gi in range(4):
                    if gi >= 2:
                        pe.wait_ge(sem("yn_ready"), gi - 1)
                    for k in range(KD):
                        last = nc.tensor.transpose(ps[:, 2 * (gi % 2) + k // 3, (k % 3) * P:(k % 3 + 1) * P],
                                                   yT[:, k, gi * P:(gi + 1) * P], ident[:, :])
                    last.then_inc(sem("yn_done"), 1)
                pe.wait_ge(sem("yn_ready"), 4)
                for h in range(NH):
                    for j in range(2):
                        for gi in range(4):
                            last = mm(ps[:, 4 + 2 * h + j, 0:HD], pwT()[:, gi, h * P:(h + 1) * P],
                                      yn[:, gi, j * HD:(j + 1) * HD], start=gi == 0, stop=gi == 3)
                last.then_inc(sem("combine_done"), 1)

            if STAGES >= 5:
                gat(1, 4)

            def dense(tag, u0, experts, unroll, upe, fpu):
                fe = upe * fpu
                body_u, body_f = unroll * upe, unroll * fe
                assert body_u % RING == 0 and body_f % 4 == 0
                mid = [view(scratch, p * N, N) for p in range(4)]
                with pe.Fori(0, experts // unroll) as i:
                    def down(F):
                        U, ft, q = F // fpu, F % fpu, F // fe
                        slot = (u0 + U) % RING
                        pe.wait_ge(sem(f"{tag}_mid"), i * body_f + (F + 1))
                        if F % fe == 0:
                            pe.wait_ge(sem(f"{tag}_yfree"), i * unroll + (q + 1))
                        wd = ring[:, slot, (ft * 12 + KD) * P:(ft * 12 + 12) * P]
                        for h in range(NH):
                            for j in range(2):
                                last = mm(ps[:, 4 + 2 * h + j, 0:HD], mid[F % 4][:, h * P:(h + 1) * P],
                                          wd[:, j * HD:(j + 1) * HD], start=F % fe == 0, stop=F % fe == fe - 1)
                        if ft == fpu - 1:
                            last.then_inc(sem(f"slot{slot}_used"), 1)

                    for F in range(body_f):
                        U, ft = F // fpu, F % fpu
                        slot = (u0 + U) % RING
                        if ft == 0:
                            pe.wait_ge(sem(f"slot{slot}_full"),
                                       i * (16 * body_u // RING) + 16 * ((u0 + U) // RING + 1))
                        for k in range(KD):
                            last = mm(ps[:, F % 4, 0:N], ring[:, slot, (ft * 12 + k) * P:(ft * 12 + k + 1) * P],
                                      xT[:, k, :], start=k == 0, stop=k == KD - 1)
                        last.then_inc(sem(f"{tag}_up"), 1)
                        if F:
                            down(F - 1)
                    down(body_f - 1)

            def scores(act, w, bias, name):
                for h in range(NH):
                    for k in range(KD):
                        last = mm(ps[:, 3, h * E2:(h + 1) * E2], act[:, k, h * P:(h + 1) * P],
                                  w[:, k * E2:(k + 1) * E2], start=k == 0, stop=k == KD - 1 and bias is None)
                    if bias is not None:
                        last = mm(ps[:, 3, h * E2:(h + 1) * E2], ones[0:1, :], bias, start=False, stop=True)
                last.then_inc(sem(name), 1)

            if STAGES >= 6:
                layernorm_T(5)
                normalised(5)
                product_T(U_R2, 0, xT, True, True)
                pe.wait_ge(sem("r2_ready"), 1)
                pe.wait_ge(sem("row1_in"), 16)
                pe.wait_ge(sem("rows_in"), 16)
                scores(hT, S("wr2"), rw1[:, D:D + E2], "score2_done")
                pe.wait_ge(sem("w2_ready"), 1)
                for h in range(NH):
                    last = nc.tensor.transpose(ps[0:E2, 2, h * P:(h + 1) * P], rt[:, 5, h, :], ident[:, :])
                last.then_inc(sem("w2T_done"), 1)
                pe.wait_ge(sem("w2T_ready"), 1)
                for h in range(NH):
                    for j in range(2):
                        last = mm(ps[:, 4 + 2 * h + j, 0:HD], wT8[:, h * P:(h + 1) * P],
                                  b2r[:, j * HD:(j + 1) * HD], start=True, stop=True)
                last.then_inc(sem("b2_done"), 1)
                dense("e2", U_E2, E2, 1, FT2 // 3, 3)

            if STAGES >= 7:
                layernorm_T(6)
                for k in range(KD):
                    if k == 0:
                        normalised(6)
                    for h in range(NH):
                        last = mm(feat(0)[:, k, :], xn[:, h, k * P:(k + 1) * P], gcn[:, h, :],
                                  start=h == 0, stop=h == NH - 1)
                last.then_inc(sem("agg3_done"), 1)
                pe.wait_ge(sem("agg3_ready"), 1)
                arrived(U_L3G)
                last = product_N(unit(U_L3G), hT, rw1[:, 0:D])
                used(U_L3G, last)

            if STAGES >= 8:
                layernorm_T(7)
                normalised(7)
                scores(xT, S("rw"), None, "score3_done")
                pe.wait_ge(sem("w3_ready"), 1)
                dense("e3", U_E3, E3, 4, 1, 3)

        @block.scalar
        def _(act):
            A = nc.scalar.activation

            def layernorm(n):
                act.wait_ge(sem("ln_var"), n + 1)
                if n == 0:
                    act.wait_ge(sem("ones_set"), 2)
                A(sd[:, :], mv[:, :, 1], ACT.Sqrt, bias=epst[:, 0:1]).then_inc(sem("ln_sd"), 1)
                act.wait_ge(sem("ln_tp"), n + 1)
                A(xT[:, 0:4, :], feat(0)[:, 0:4, :], ACT.Copy).then_inc(sem("ln_Ta"), 1)

            layernorm(0)
            act.wait_ge(sem("small_in"), 16)
            for n in range(KD):
                if n < KD - 1:
                    act.wait_ge(sem("qg_done"), n + 1)
                else:
                    unit_done(act, U_QG)
                A(qgT[:, n, :], ps[:, 4 + n % 4, :], ACT.Identity, bias=S("bg")[:, n:n + 1]).then_inc(sem("qg_ready"), 1)
            act.wait_ge(sem("deg_ready"), 1)
            A(dis[:, :], deg[:, :], ACT.Sqrt).then_inc(sem("deg_sqrt"), 1)

            for r in range(2):
                for j in range(KD):
                    act.wait_ge(sem("g_done"), KD * r + j + 1)
                    A(view(scratch, 0, REL, KD, N)[:, 0:2, j, :],
                      ps[:, 2 * (j % 2), :].rearrange("p (a b) -> p a b", a=2), ACT.Copy).then_inc(sem("g_copied_a"), 1)
                unit_done(act, (U_RG1, U_RG2)[r] + 3)
                for n in range(KD):
                    last = A(hT[:, n, :], feat(4)[:, n, :], ACT.Relu, bias=S(f"b{r + 1}")[:, n:n + 1])
                last.then_inc(sem("hT_ready"), 1)
                unit_done(act, (U_GT1, U_GT2)[r])
                A(hgT[:, :, :], feat(0), ACT.Copy).then_inc(sem("hg_ready"), 1)
                CH = KD * B
                with act.Fori(0, CH // 2) as i:
                    for par in range(2):
                        s = view(scratch, par * NB * L, NB * L)
                        act.wait_ge(sem("gate_sum"), i * 2 + (CH * r + par + 1))
                        A(s, s, ACT.Sigmoid).then_inc(sem("gate_sig"), 1)
                unit_done(act, (U_GT1, U_GT2)[r] + 2)
                for n in range(KD):
                    last = A(hgT[:, n, :], feat(4)[:, n, :], ACT.Sigmoid, bias=S("bq")[:, n:n + 1])
                last.then_inc(sem("alpha_ready"), 1)
                A(qiT[:, :, :], qiT[:, :, :], ACT.Tanh).then_inc(sem("alpha_ready"), 1)
                if r == 0:
                    act.wait_ge(sem("hn_nat"), 1)
                    A(xn[:, :, :].rearrange("p h (a b) -> p (h a) b", a=2), ps[:, 4:8, 0:HD], ACT.Copy
                      ).then_inc(sem("hnat_ready"), 1)

            if STAGES >= 2:
                layernorm(1)
                act.wait_ge(sem(f"slot{U_FF0 % RING}_full"), 16 * (U_FF0 // RING + 1))
                A(unit(U_FF0), unit(U_FF0), ACT.Sign).then_inc(sem("sign_ready"), 1)

            def gat(n, lnidx):
                layernorm(lnidx)
                act.wait_ge(sem("ft_done"), n + 1)
                ft1 = view(scratch, FT1_AT, NH, HEADS, HE + 1)
                act.wait_ge(sem("gat_w"), n + 1)
                for h in range(NH):
                    last = A(ft1[:, h, :, 0:HE].rearrange("p (a b) e -> p a b e", a=2),
                             nat(h).rearrange("p a (b e) -> p a b e", e=HE), ACT.Copy)
                last.then_inc(sem("ft_ready"), 1)
                act.wait_ge(sem("ftT_done"), n + 1)
                A(hT[:, :, :], feat(0), ACT.Copy).then_inc(sem("ftT_ready"), 1)
                act.wait_ge(sem("res_done"), n + 1)
                A(view(scratch, RES_AT, 2 * NH, HD), ps[:, 4:8, 0:HD], ACT.Copy).then_inc(sem("res_ready"), 1)
                for gi in range(HEADS // HG):
                    G = n * (HEADS // HG) + gi
                    s = view(scratch, (gi % 2) * HG * NH * N, HG, NH, N)
                    act.wait_ge(sem("arow_taken"), G + 1)
                    act.wait_ge(sem("a2_ready"), n + 1)
                    for q in range(HG):
                        for dh in range(NH):
                            last = A(s[:, q, dh, :], s[:, q, dh, :], ACT.Identity,
                                     bias=a2[:, dh, gi * HG + q:gi * HG + q + 1])
                    last.then_inc(sem("att_sum"), 1)
                    act.wait_ge(sem("hmax_ready"), G + 1)
                    for q in range(HG):
                        for dh in range(NH):
                            last = A(s[:, q, dh, :], s[:, q, dh, :], ACT.Exp, bias=hm[:, 3, q, dh:dh + 1])
                    last.then_inc(sem("att_exp"), 1)
                    for q in range(HG):
                        h = gi * HG + q
                        act.wait_ge(sem("wT_done"), n * HEADS + h + 1)
                        if h >= 2:
                            act.wait_ge(sem("head_done"), n * HEADS + h - 1)
                        A(view(scratch, 2 * HG * NH * N + (h % 2) * NH * N, NH * N), ps[:, 2 + h % 2, :],
                          ACT.Copy).then_inc(sem("wT_ready"), 1)

            if STAGES >= 3:
                gat(0, 2)

            if STAGES >= 4:
                layernorm(3)
                act.wait_ge(sem("score_done"), 1)
                A(sc1[:, :, :].rearrange("p a b -> p (a b)"), ps[:, 3, 0:NH * E1], ACT.Sigmoid
                  ).then_inc(sem("score_ready"), 1)
                xsel = view(scratch, 0, KD, E1 * SLOTS)
                for k in range(0, KD, 2):
                    act.wait_ge(sem("xsel_done"), k + 1)
                    A(xsel[:, k, :], ps[:, k % 2, :], ACT.Copy).then_inc(sem("xsel_even"), 1)
                act.wait_ge(sem("pwT_done"), 1)
                A(pwT().rearrange("p a b -> p (a b)"), ps[:, 2:4, :].rearrange("p a b -> p (a b)"), ACT.Copy
                  ).then_inc(sem("pwT_ready"), 1)
                sg = [view(scratch, 7680 + p * N, N) for p in range(2)]
                for f in range(SH_FT):
                    act.wait_ge(sem("sh_gu"), f + 1)
                    if f >= 2:
                        act.wait_ge(sem("sh_act"), f - 1)
                    A(sg[f % 2], ps[:, f % 4, 0:N], ACT.Silu).then_inc(sem("sh_silu"), 1)
                se = [view(scratch, 7680 + p * 64, 2, SLOTS) for p in range(2)]
                act.wait_ge(sem("sh_act"), SH_FT)
                NU = FT1 // 2
                with act.Fori(0, E1 * NU // 2) as i:
                    for par in range(2):
                        act.wait_ge(sem("gu1_done"), i * 2 + (par + 1))
                        A(se[par], ps[:, par, 0:4 * SLOTS].rearrange("p (f g s) -> p f g s", f=2, g=2)[:, :, 0, :],
                          ACT.Silu).then_inc(sem("e1_silu"), 1)
                for gi in range(4):
                    act.wait_ge(sem("yn_done"), gi + 1)
                    A(view(qflat, 0, 4, 2, HD)[:, gi, :, :], ps[:, 2 * (gi % 2):2 * (gi % 2) + 2, 0:HD], ACT.Copy
                      ).then_inc(sem("yn_ready"), 1)

            if STAGES >= 5:
                gat(1, 4)

            def softmax_exp(name, done):
                act.wait_ge(sem(name), 1)
                for h in range(NH):
                    last = A(rt[:, 1, h, :], rt[:, 0, h, :], ACT.Exp, bias=rsm[:, 0, h:h + 1])
                last.then_inc(sem(done), 1)

            def dense(tag, experts, unroll, fe, biased):
                body_f = unroll * fe
                mid = [view(scratch, p * N, N) for p in range(4)]
                with act.Fori(0, experts // unroll) as i:
                    for F in range(body_f):
                        act.wait_ge(sem(f"{tag}_up"), i * body_f + (F + 1))
                        kw = {"bias": S("fb1")[:, bass.ds(i * fe + F, 1)]} if biased else {}
                        A(mid[F % 4], ps[:, F % 4, 0:N], ACT.Relu, **kw).then_inc(sem(f"{tag}_mid"), 1)

            if STAGES >= 6:
                layernorm(5)
                unit_done(act, U_R2)
                for n in range(KD):
                    last = A(hT[:, n, :], feat(0)[:, n, :], ACT.Relu, bias=S("br1")[:, n:n + 1])
                last.then_inc(sem("r2_ready"), 1)
                softmax_exp("max2_ready", "exp2")
                dense("e2", E2, 1, FT2, True)
            if STAGES >= 7:
                layernorm(6)
                act.wait_ge(sem("agg3_done"), 1)
                A(hT[:, :, :], feat(0), ACT.Copy).then_inc(sem("agg3_ready"), 1)
            if STAGES >= 8:
                layernorm(7)
                softmax_exp("max3_ready", "exp3")
                dense("e3", E3, 4, FT3, False)

        @block.vector
        def _(v):
            link = Chain(v, sem("dve_own"))
            tt, ts, stt = nc.vector.tensor_tensor, nc.vector.tensor_scalar, nc.vector.scalar_tensor_tensor
            copy, red = nc.vector.tensor_copy, nc.vector.tensor_reduce

            def layernorm(n):
                for h in range(NH):
                    for j in range(2):
                        last = nc.vector.bn_stats(bnst[:, h, j, :], x[:, h, j * HD:(j + 1) * HD])
                link(last)
                for h in range(NH):
                    last = nc.vector.bn_aggr(mv[:, h, :], bnst[:, h, :, :].rearrange("p a b -> p (a b)"))
                last.then_inc(sem("ln_var"), 1)
                v.wait_ge(sem("ln_sd"), n + 1)
                link(nc.vector.reciprocal(rs[:, :], sd[:, :]))
                for h in range(NH):
                    ts(xn[:, h, :], x[:, h, :], mv[:, h, 0:1], rs[:, h:h + 1], ALU.subtract, ALU.mult
                       ).then_inc(sem("ln_xn"), 1)
                v.wait_ge(sem("ln_tp"), n + 1)
                copy(xT[:, 4:6, :], feat(0)[:, 4:6, :]).then_inc(sem("ln_Tv"), 1)

            def residual():
                for h in range(NH):
                    last = tt(halves(x, h), nat(h), halves(x, h), ALU.add)
                link(last)

            v.wait_ge(sem("x_in"), 16)
            layernorm(0)
            v.wait_ge(sem("edges_in"), 16)
            link(copy(edf[:, 0:3, :], edi[:, :, :]))
            link(stt(edf[:, 3, :], edf[:, 2, :], float(N), edf[:, 1, :], ALU.mult, ALU.add))
            v.wait_ge(sem("iota_set"), 1)
            for c in range(EC):
                if c >= 4:
                    v.wait_ge(sem("onehot_used"), c - 3)
                s_oh, k_oh = onehots(c)
                ts(s_oh, iota[:, 0:N], edf[:, 0, c:c + 1], None, ALU.is_equal)
                ts(k_oh, iota[:, :], edf[:, 3, c:c + 1], None, ALU.is_equal).then_inc(sem("onehot_ready"), 1)
            v.wait_ge(sem("onehot_used"), EC)
            for h in range(NH):
                copy(adj[:, h, 0:512], ps[:, 2 * h, :])
                last = copy(adj[:, h, 512:768], ps[:, 2 * h + 1, 0:N])
            last.then_inc(sem("adj_raw"), 1)
            v.wait_ge(sem("adj_raw"), 1)
            link(tt(cT[:, :, :], adj[:, :, 0:N], adj[:, :, N:2 * N], ALU.add))
            tt(cT[:, :, :], cT[:, :, :], adj[:, :, 2 * N:3 * N], ALU.add).then_inc(sem("cT_ready"), 1)
            rcnt = view(scratch, 2048, 2, HD)
            v.wait_ge(sem("relcount"), 1)
            link(ts(rcnt, ps[:, 0:2, 0:HD], 1.0, None, ALU.max))
            link(nc.vector.reciprocal(rcnt, rcnt))
            for h in range(NH):
                last = tt(halves(adj, h), halves(adj, h), rcnt, ALU.mult)
            last.then_inc(sem("adj_ready"), 1)
            v.wait_ge(sem("cN_tp"), 1)
            link(copy(cN[:, :, :].rearrange("p a b -> p (a b)"), ps[:, 2, :]))
            ts(far[:, :, :], cN[:, :, :], 0.0, FAR, ALU.is_equal, ALU.mult)
            link(red(deg[:, :], cN[:, :, :], AX.X, ALU.add))
            ts(deg[:, :], deg[:, :], 1.0, None, ALU.add).then_inc(sem("deg_ready"), 1)
            v.wait_ge(sem("deg_sqrt"), 1)
            nc.vector.reciprocal(dis[:, :], dis[:, :]).then_inc(sem("dis_ready"), 1)
            link(copy(gcn[:, :, :], cT[:, :, :]))
            v.wait_ge(sem("ident_set"), 1)
            for h in range(NH):
                last = tt(gcn[:, h, h * P:(h + 1) * P], gcn[:, h, h * P:(h + 1) * P], ident[:, :], ALU.add)
            link(last)
            v.wait_ge(sem("disrow"), 1)
            for h in range(NH):
                last = stt(gcn[:, h, :], gcn[:, h, :], dis[:, h:h + 1], ps[:, 3, 0:N], ALU.mult, ALU.mult)
            last.then_inc(sem("gcn_ready"), 1)

            qif = qiT[:, :, :].rearrange("p a b -> p (a b)")
            CH = KD * B
            for r in range(2):
                for j in range(KD):
                    v.wait_ge(sem("g_done"), KD * r + j + 1)
                    copy(view(scratch, 0, REL, KD, N)[:, 2, j, :], ps[:, 2 * (j % 2) + 1, 0:N]
                         ).then_inc(sem("g_copied_v"), 1)
                with v.Fori(0, CH // 2) as i:
                    for par in range(2):
                        s = view(scratch, par * NB * L, NB, L)
                        p = view(scratch, (2 + par) * NB * L, NB, L)
                        v.wait_ge(sem("gate_sig"), i * 2 + (CH * r + par + 1))
                        tt(p, s, qflat[:, bass.ds((i * 2 + par) * L, L)].unsqueeze(1).to_broadcast([P, NB, L]),
                           ALU.mult).then_inc(sem("gate_prod"), 1)
                        v.wait_ge(sem("gate_prod"), i * 2 + (CH * r + par + 1))
                        last = red(qif[:, bass.ds((i * 2 + par) * NB, NB)], p, AX.X, ALU.add)
                    last.then_inc(sem("qi_ready"), 1)
                v.wait_ge(sem("alpha_ready"), 2 * (r + 1))
                link(tt(qiT[:, :, :], qiT[:, :, :], hT[:, :, :], ALU.subtract))
                link(tt(qiT[:, :, :], qiT[:, :, :], hgT[:, :, :], ALU.mult))
                tt(hT[:, :, :], hT[:, :, :], qiT[:, :, :], ALU.add).then_inc(sem("hn_ready"), 1)
            v.wait_ge(sem("hn_nat"), 2)
            residual()

            if STAGES >= 2:
                layernorm(1)
                unit_done(v, U_FF0)
                residual()

            def gat(n, lnidx):
                bd = view(gflat, 0, 2, P)
                al = view(gflat, 2 * P, KD, 2)
                ar = view(gflat, 2 * P + 2 * KD, KD, 2)
                ft1 = view(scratch, FT1_AT, NH, HEADS, HE + 1)
                link(nc.vector.memset(gflat[:, 0:2 * P + 4 * KD], 0.0))
                for q in range(2):
                    pr = slice(q * HE, (q + 1) * HE)
                    copy(bd[pr, 0, pr], S(f"fc{n + 1}")[pr, :])
                    copy(bd[pr, 1, pr], S(f"res{n + 1}")[pr, :])
                    copy(al[pr, :, q], S(f"al{n + 1}")[pr, :])
                    copy(ar[pr, :, q], S(f"ar{n + 1}")[pr, :])
                nc.vector.memset(ft1[:, :, :, HE], 1.0).then_inc(sem("gat_w"), 1)
                layernorm(lnidx)
                v.wait_ge(sem("a2_done"), n + 1)
                copy(a2[:, :, :].rearrange("p a b -> p (a b)"), ps[:, 3, 0:NH * HEADS]).then_inc(sem("a2_ready"), 1)
                v.wait_ge(sem("a2_ready"), n + 1)
                for gi in range(HEADS // HG):
                    G = n * (HEADS // HG) + gi
                    s = view(scratch, (gi % 2) * HG * NH * N, HG, NH, N)
                    if gi >= 2:
                        v.wait_ge(sem("head_done"), n * HEADS + (gi - 1) * HG)
                    v.wait_ge(sem("arow_done"), G + 1)
                    rows = ps[:, 0:2, :].rearrange("p a (b n) -> p (a b) n", b=2)
                    for dh in range(NH):
                        last = tt(s[:, :, dh, :], rows[:, 0:HG, :], far[:, dh:dh + 1, :].to_broadcast([P, HG, N]),
                                  ALU.add)
                    link(last)
                    red(hm[:, 0, :, :], s, AX.X, ALU.max).then_inc(sem("arow_taken"), 1)
                    v.wait_ge(sem("arow_taken"), G + 1)
                    link(tt(hm[:, 1, :, :], hm[:, 0, :, :],
                            a2[:, :, gi * HG:(gi + 1) * HG].rearrange("p a b -> p b a"), ALU.add))
                    link(ts(hm[:, 2, :, :], hm[:, 1, :, :], 0.2, None, ALU.mult))
                    link(tt(hm[:, 2, :, :], hm[:, 2, :, :], hm[:, 1, :, :], ALU.max))
                    if gi:
                        v.wait_ge(sem("att_exp"), G)
                    ts(hm[:, 3, :, :], hm[:, 2, :, :], -1.0, None, ALU.mult)
                    v.wait_ge(sem("att_sum"), G + 1)
                    sf = view(scratch, (gi % 2) * HG * NH * N, HG * NH * N)
                    stt(sf, sf, 0.2, sf, ALU.mult, ALU.max).then_inc(sem("hmax_ready"), 1)
                    v.wait_ge(sem("att_exp"), G + 1)
                    for q in range(HG):
                        last = tt(s[:, q, :, :], s[:, q, :, :], cN[:, :, :], ALU.mult)
                    last.then_inc(sem("att_ready"), 1)
                v.wait_ge(sem("head_done"), (n + 1) * HEADS)
                v.wait_ge(sem("res_ready"), n + 1)
                t = view(scratch, 0, NH, 2, HD)
                res = view(scratch, RES_AT, NH, 2, HD)
                for dh in range(NH):
                    agg = ps[:, 4 + 2 * dh:6 + 2 * dh, 0:6 * (HE + 1)].rearrange("p a (b e) -> p a b e", e=HE + 1)
                    rd = rden[:, dh, :].rearrange("p (a b) -> p a b", a=2)
                    link(ts(rd, agg[:, :, :, HE], 1e-16, None, ALU.max))
                    link(nc.vector.reciprocal(rd, rd))
                    for a in range(2):
                        last = tt(t[:, dh, a, :].rearrange("p (b e) -> p b e", e=HE), agg[:, a, :, 0:HE],
                                  rd[:, a, :].unsqueeze(2).to_broadcast([P, 6, HE]), ALU.mult)
                    link(last)
                    link(tt(t[:, dh, :, :], t[:, dh, :, :], res[:, dh, :, :], ALU.add))
                    link(stt(halves(x, dh), t[:, dh, :, :], 0.0, halves(x, dh), ALU.max, ALU.add))

            if STAGES >= 3:
                gat(0, 2)

            if STAGES >= 4:
                layernorm(3)
                v.wait_ge(sem("score_ready"), 1)
                v.wait_ge(sem("lt_set"), 1 + NH)
                lt = view(gflat, 0, NH, N)
                jk = view(gflat, 2 * N, 2, NH, 2, N)
                for e in range(E1):
                    if e >= 2:
                        v.wait_ge(sem("rank_taken"), e - 1)
                    v.wait_ge(sem("srow_done"), e + 1)
                    for h in range(NH):
                        row = ps[:, e % 4, 0:N]
                        ts(jk[:, e % 2, h, 0, :], row, sc1[:, h, e:e + 1], None, ALU.is_gt, ALU.add,
                           accum_out=cnt[:, 0, h, e:e + 1])
                        last = stt(jk[:, e % 2, h, 1, :], row, sc1[:, h, e:e + 1], lt[:, h, :], ALU.is_equal, ALU.mult,
                                   accum_out=cnt[:, 1, h, e:e + 1])
                    last.then_inc(sem("rank_taken"), 1)
                v.wait_ge(sem("rank_taken"), E1)
                link(tt(cnt[:, 2, :, :], cnt[:, 0, :, :], cnt[:, 1, :, :], ALU.add))
                p1 = view(qflat, 0, NH, E1, SLOTS)
                for h in range(NH):
                    last = tt(p1[:, h, :, :], iota[:, 0:SLOTS].unsqueeze(1).to_broadcast([P, E1, SLOTS]),
                              cnt[:, 2, h, :].unsqueeze(2).to_broadcast([P, E1, SLOTS]), ALU.is_equal)
                last.then_inc(sem("onehot1_ready"), 1)
                xsel = view(scratch, 0, KD, E1 * SLOTS)
                for k in range(1, KD, 2):
                    v.wait_ge(sem("xsel_done"), k + 1)
                    copy(xsel[:, k, :], ps[:, k % 2, :]).then_inc(sem("xsel_odd"), 1)
                for h in range(NH):
                    last = tt(p1[:, h, :, :], p1[:, h, :, :],
                              sc1[:, h, :].unsqueeze(2).to_broadcast([P, E1, SLOTS]), ALU.mult)
                last.then_inc(sem("pw_ready"), 1)
                hs = [view(scratch, 6656 + p * N, N) for p in range(4)]
                sg = [view(scratch, 7680 + p * N, N) for p in range(2)]
                for f in range(SH_FT):
                    v.wait_ge(sem("sh_silu"), f + 1)
                    tt(hs[f % 4], sg[f % 2], ps[:, f % 4, N:2 * N], ALU.mult).then_inc(sem("sh_act"), 1)
                unit_done(v, U_E1 - 1)
                residual()
                v.sem_inc(sem("y1_free"), 2)
                he = [view(scratch, KD * E1 * SLOTS + 2 * KD * SLOTS + p * 2 * SLOTS, 2, SLOTS) for p in range(2)]
                se = [view(scratch, 7680 + p * 64, 2, SLOTS) for p in range(2)]
                yT = view(gflat, 0, KD, E1 * SLOTS)
                NU = FT1 // 2
                with v.Fori(0, E1 // 2) as i:
                    for par in range(2):
                        for w in range(NU):
                            U = par * NU + w
                            v.wait_ge(sem("e1_silu"), i * (2 * NU) + (U + 1))
                            tt(he[U % 2], se[U % 2],
                               ps[:, U % 2, 0:4 * SLOTS].rearrange("p (f g s) -> p f g s", f=2, g=2)[:, :, 1, :],
                               ALU.mult).then_inc(sem("e1_act"), 1)
                        ul = U_E1 + par * NU + NU - 1
                        v.wait_ge(sem(f"slot{ul % RING}_used"), i * (2 * NU // RING) + (ul // RING + 1))
                        copy(yT[:, :, bass.ds((i * 2 + par) * SLOTS, SLOTS)],
                             ps[:, 2 + par, 0:KD * SLOTS].rearrange("p (k s) -> p k s", k=KD)
                             ).then_inc(sem("y1_free"), 1)
                v.wait_ge(sem("combine_done"), 1)
                residual()

            if STAGES >= 5:
                gat(1, 4)

            def route(sname, mname, ename, wname, keep, before):
                v.wait_ge(sem(sname), 1)
                link(copy(rt[:, 0, :, :].rearrange("p a b -> p (a b)"), ps[:, 3, 0:NH * E2]))
                link(red(rsm[:, 1, :], rt[:, 0, :, :], AX.X, ALU.max))
                ts(rsm[:, 0, :], rsm[:, 1, :], -1.0, None, ALU.mult).then_inc(sem(mname), 1)
                v.wait_ge(sem(ename), 1)

                def mask(src):
                    for h in range(NH):
                        a = src[:, h, :].unsqueeze(1).to_broadcast([P, E2, E2])
                        b = src[:, h, :].unsqueeze(2).to_broadcast([P, E2, E2])
                        tt(rk[:, 0, h, :, :], a, b, ALU.is_gt)
                        last = tt(rk[:, 1, h, :, :], a, b, ALU.is_equal)
                    link(last)
                    for h in range(NH):
                        last = tt(rk[:, 1, h, :, :], rk[:, 1, h, :, :], low[:, :, :], ALU.mult)
                    link(last)
                    link(tt(rk[:, 0, :, :, :], rk[:, 0, :, :, :], rk[:, 1, :, :, :], ALU.add))
                    link(red(rt[:, 2, :, :], rk[:, 0, :, :, :].rearrange("p h a b -> p (h a) b"), AX.X, ALU.add))
                    link(ts(rt[:, 2, :, :], rt[:, 2, :, :], float(keep), None, ALU.is_lt))

                v.wait_ge(sem("low_set"), 1)
                if before:
                    mask(rt[:, 0, :, :])
                    link(tt(rt[:, 1, :, :], rt[:, 1, :, :], rt[:, 2, :, :], ALU.mult))
                link(red(rsm[:, 2, :], rt[:, 1, :, :], AX.X, ALU.add))
                link(nc.vector.reciprocal(rsm[:, 3, :], rsm[:, 2, :]))
                last = tt(rt[:, 5, :, :], rt[:, 1, :, :], rsm[:, 3, :].unsqueeze(2).to_broadcast([P, NH, E2]), ALU.mult)
                if before:
                    last.then_inc(sem(wname), 1)
                    v.wait_ge(sem(wname), 1)
                else:
                    link(last)
                    mask(rt[:, 5, :, :])
                    tt(rt[:, 5, :, :], rt[:, 5, :, :], rt[:, 2, :, :], ALU.mult).then_inc(sem(wname), 1)
                    v.wait_ge(sem(wname), 1)

            def dense(tag, u0, experts, unroll, upe):
                v.sem_inc(sem(f"{tag}_yfree"), 1)
                with v.Fori(0, experts // unroll) as i:
                    for q in range(unroll):
                        ul = u0 + (q + 1) * upe - 1
                        v.wait_ge(sem(f"slot{ul % RING}_used"), i * (unroll * upe // RING) + (ul // RING + 1))
                        for h in range(NH):
                            last = stt(halves(x, h), nat(h), rt[:, 5, h, bass.ds(i * unroll + q, 1)], halves(x, h),
                                       ALU.mult, ALU.add)
                        last.then_inc(sem(f"{tag}_yfree"), 1)
                        v.wait_ge(sem(f"{tag}_yfree"), i * unroll + (q + 2))

            if STAGES >= 6:
                layernorm(5)
                route("score2_done", "max2_ready", "exp2", "w2_ready", 2, True)
                v.wait_ge(sem("w2T_done"), 1)
                copy(wT8[:, :], ps[0:E2, 2, 0:N]).then_inc(sem("w2T_ready"), 1)
                v.wait_ge(sem("b2_done"), 1)
                residual()
                dense("e2", U_E2, E2, 1, FT2 // 3)
            if STAGES >= 7:
                layernorm(6)
                unit_done(v, U_L3G)
                residual()
            if STAGES >= 8:
                layernorm(7)
                route("score3_done", "max3_ready", "exp3", "w3_ready", 1, False)
                dense("e3", U_E3, E3, 4, 1)
            nc.vector.memset(rsm[:, :, :], 0.0).then_inc(sem("result"), 1)


def kernel(**inputs):
    import numpy as np
    import concourse.bacc as bacc
    from concourse.bass_utils import run_bass_kernel_spmd

    a = {k: np.asarray(v) for k, v in inputs.items()}

    def rows(w):
        return w.reshape(KD, P, -1).transpose(1, 0, 2).reshape(P, -1)

    def cols(b):
        return b.reshape(-1, P).T

    def twice(w):
        return np.concatenate([w.T, w.T])

    weights = np.empty((UNITS, P, UW), np.float32)

    def put(u, w):
        weights[u] = rows(w)

    wg, wq = a["L0_gnn_Wg"], a["L0_gnn_Wq"]
    put(U_QG, wg[:, D:].T)
    for r, (ur, ug) in enumerate(((U_RG1, U_GT1), (U_RG2, U_GT2))):
        put(ur, a[f"L0_gnn_W_root{r + 1}"])
        for rel in range(REL):
            put(ur + 1 + rel, a[f"L0_gnn_W_rel{r + 1}"][rel])
        put(ug, wg[:, :D].T)
        put(ug + 1, wq[:, :D].T)
        put(ug + 2, wq[:, D:].T)
    put(U_FF0, a["L0_ffn_weight"].T)

    def up_blocks(w, f):
        return w.reshape(w.shape[0], -1, f, P, KD, P).transpose(0, 1, 5, 2, 4, 3)

    def down_blocks(w, f):
        return w.reshape(w.shape[0], KD, P, -1, f, P).transpose(0, 3, 5, 4, 1, 2)

    def gated(u, wg, wu, wd):
        o = weights[u:u + wg.shape[0] * wg.shape[1] // (2 * P)].reshape(wg.shape[0], -1, P, 2, 18, P)
        o[:, :, :, :, 0:6] = up_blocks(wg, 2)
        o[:, :, :, :, 6:12] = up_blocks(wu, 2)
        o[:, :, :, :, 12:18] = down_blocks(wd, 2)

    gated(U_SH, a["L1_ffn_Ws_g"][None], a["L1_ffn_Ws_u"][None], a["L1_ffn_Ws_d"][None])
    gated(U_E1, a["L1_ffn_Wg"], a["L1_ffn_Wu"], a["L1_ffn_Wd"])
    put(U_R2, a["L2_ffn_Wr1"].T)
    o = weights[U_E2:U_L3G].reshape(E2, -1, P, 3, 12, P)
    o[:, :, :, :, 0:6] = up_blocks(a["L2_ffn_W1"], 3)
    o[:, :, :, :, 6:12] = down_blocks(a["L2_ffn_W2"], 3)
    put(U_L3G, a["L3_gnn_W"])
    o = weights[U_E3:UNITS].reshape(E3, 1, P, 3, 12, P)
    o[:, :, :, :, 0:6] = up_blocks(a["L3_ffn_wi"].transpose(0, 2, 1), 3)
    o[:, :, :, :, 6:12] = down_blocks(a["L3_ffn_wo"].transpose(0, 2, 1), 3)

    small = np.concatenate([
        cols(a["L0_gnn_b1"]), cols(a["L0_gnn_b2"]), cols(a["L0_gnn_bg"]), cols(a["L0_gnn_bq"]),
        cols(a["L2_ffn_br1"]), cols(a["L2_ffn_b1"].reshape(-1)),
        rows(a["L1_ffn_gate_weight"].T), rows(a["L2_ffn_Wr2"].T), rows(a["L3_ffn_router_w"]),
        twice(a["L1_gnn_W_fc"]), twice(a["L1_gnn_W_res"]), cols(a["L1_gnn_attn_l"].reshape(-1)),
        cols(a["L1_gnn_attn_r"].reshape(-1)),
        twice(a["L2_gnn_W"]), twice(a["L2_gnn_W_res"]), cols(a["L2_gnn_attn_l"].reshape(-1)),
        cols(a["L2_gnn_attn_r"].reshape(-1))], axis=1)
    arrays = {
        "weights": weights[:STAGE_UNITS[STAGES - 1]],
        "small": small,
        "edges": np.stack([a["src"], a["dst"], a["edge_type_3"]]).reshape(3, P, EC).transpose(1, 0, 2),
        "x": a["x"].reshape(NH, P, D).transpose(1, 0, 2),
        "qT": a["L0_gnn_query_embs"].reshape(B * L, KD, P).transpose(2, 1, 0),
        "rows8": a["L2_ffn_b2"],
        "row1": np.concatenate([a["L3_gnn_b"], a["L2_ffn_br2"]])[None],
    }
    nc = bacc.Bacc("TRN2", target_bir_lowering=False, num_devices=1)
    arrays = {f"in_{k}": np.ascontiguousarray(v) for k, v in arrays.items()}
    aps = [nc.dram_tensor(k, v.shape, mybir.dt.from_np(v.dtype), kind="ExternalInput").ap() for k, v in arrays.items()]
    out = nc.dram_tensor("out", (P, NH, D), F32, kind="ExternalOutput").ap()
    build(nc, *aps, out)
    r = run_bass_kernel_spmd(nc, [arrays], core_ids=[0])
    return r.results[0]["out"].transpose(1, 0, 2).reshape(N, D)
```

```python
from contextlib import ExitStack

import concourse.bass as bass
from concourse import mybir

ALU = mybir.AluOpType
ACT = mybir.ActivationFunctionType
AX = mybir.AxisListType
F32 = mybir.dt.float32
BF16 = mybir.dt.bfloat16
I32 = mybir.dt.int32

P = 128
N = 256
NH = N // P
D = 768
KD = D // P
HD = D // 2
EDGES = 4352
EC = EDGES // P
REL = 3
B, NB, L = 8, 32, 64
HEADS, HE = 12, 64
HG = 3
E1, SLOTS, FT1 = 16, 32, 24
E2, FT2 = 8, 24
CAP2 = P
E3, FT3 = 8, 3
SH_FT = 12
UB = 36
UW = UB * P
RING = 4
EPS = 1e-5
FAR = -1e30

U_QG = 0
U_RG1 = 1
U_GT1 = U_RG1 + 4
U_RG2 = U_GT1 + 3
U_GT2 = U_RG2 + 4
U_FF0 = U_GT2 + 3
U_SH = U_FF0 + 1
U_E1 = U_SH + SH_FT // 2
U_R2 = U_E1 + E1 * FT1 // 2
U_E2 = U_R2 + 1
U_L3G = U_E2 + E2 * FT2 // 3
U_E3 = U_L3G + 1
UNITS = U_E3 + E3
STAGE_UNITS = [U_FF0, U_SH, U_SH, U_R2, U_R2, U_L3G, U_E3, UNITS]
STAGES = 8

SMALL = {}
_at = 0
for _n, _w in (("b1", KD), ("b2", KD), ("bg", KD), ("bq", KD), ("br1", KD), ("fb1", E2 * FT2),
               ("gate", KD * E1), ("wr2", KD * E2), ("rw", KD * E3),
               ("fc1", HE), ("res1", HE), ("al1", KD), ("ar1", KD),
               ("fc2", HE), ("res2", HE), ("al2", KD), ("ar2", KD)):
    SMALL[_n] = (_at, _w)
    _at += _w
SMALL_W = _at


class Chain:

    def __init__(self, eng, sem):
        self.eng, self.sem, self.count, self.past = eng, sem, 0, 0

    def __call__(self, ins):
        self.count += 1
        ins.then_inc(self.sem, 1)
        self.eng.wait_ge(self.sem, self.past + self.count)
        return ins

    def enter(self, i, steps):
        self.first, self.steps = self.count, steps
        self.past = i * steps

    def leave(self, trips):
        assert self.count - self.first == self.steps, (self.count - self.first, self.steps)
        self.count += self.steps * (trips - 1)
        self.past = 0


def build(nc, weights, small, edges, xin, qT, rows8, row1, out):
    ctx = ExitStack()
    with ctx:
        sems = {}

        def sem(name):
            if name not in sems:
                sems[name] = ctx.enter_context(nc.semaphore(name))
            return sems[name]

        def sb(name, shape, dt=F32):
            return ctx.enter_context(nc.sbuf_tensor(name, shape, dt))

        ps = ctx.enter_context(nc.psum_tensor("ps", [P, 8, 512], F32))
        ring = sb("ring", [P, RING, UW])
        x = sb("x", [P, NH, D])
        xn = sb("xn", [P, NH, D])
        xT = sb("xT", [P, KD, N])
        adj = sb("adj", [P, NH, REL * N])
        cT = sb("cT", [P, NH, N])
        cN = sb("cN", [P, NH, N])
        far = sb("far", [P, NH, N])
        gcn = sb("gcn", [P, NH, N])
        scratch = sb("scratch", [P, 8192])
        qTs = sb("qTs", [P, KD, B * L])
        gate_in = sb("gate_in", [P, KD * B * L + KD * N])
        qgT = gate_in[:, 0:KD * B * L].rearrange("p (a b) -> p a b", a=KD)
        hgT = gate_in[:, KD * B * L:].rearrange("p (a b) -> p a b", a=KD)
        hT = sb("hT", [P, KD, N])
        qiT = sb("qiT", [P, KD, N])
        iota = sb("iota", [P, REL * N])
        ident = sb("ident", [P, P])
        ones = sb("ones", [P, P])
        sm = sb("sm", [P, SMALL_W])
        edi = sb("edi", [P, 3, EC], I32)
        edf = sb("edf", [P, 4, EC])
        b2r = sb("b2r", [E2, D])
        rw1 = sb("rw1", [1, D + E2])
        epst = sb("epst", [P, 1])
        bnst = sb("bnst", [P, NH, 2, 6])
        mv = sb("mv", [P, NH, 2])
        sd = sb("sd", [P, NH])
        rs = sb("rs", [P, NH])
        deg = sb("deg", [P, NH])
        dis = sb("dis", [P, NH])
        low = sb("low", [P, E2, E2])
        a2 = sb("a2", [P, NH, HEADS])
        hm = sb("hm", [P, 4, HG, NH])
        rden = sb("rden", [P, NH, HEADS])
        sc1 = sb("sc1", [P, NH, E1])
        cnt = sb("cnt", [P, 3, NH, E1])
        rk = sb("rk", [P, 2, NH, E2, E2])
        rt = sb("rt", [P, 6, NH, E2])
        rsm = sb("rsm", [P, 4, NH])
        wT8 = sb("wT8", [E2, N])
        tri = sb("tri", [P, P])
        over = sb("over", [P, 2], I32)
        ovw = gate_in

        def S(name):
            a, w = SMALL[name]
            return sm[:, a:a + w]

        def view(t, off, *shape):
            n = 1
            for s in shape:
                n *= s
            f = t[:, off:off + n]
            if len(shape) == 1:
                return f
            names = "abcd"[:len(shape)]
            return f.rearrange(f"p ({' '.join(names)}) -> p {' '.join(names)}", **dict(zip(names[1:], shape[1:])))

        qflat = qTs[:, :, :].rearrange("p a b -> p (a b)")
        gflat = gate_in[:, 0:KD * B * L]

        def nat(h):
            return ps[:, 4 + 2 * h:6 + 2 * h, 0:HD]

        def halves(t, h):
            return t[:, h, :].rearrange("p (a b) -> p a b", a=2)

        def feat(bank):
            return ps[:, bank:bank + 3, :].rearrange("p a (b n) -> p (a b) n", b=2)

        def unit(u):
            return ring[:, u % RING, :]

        def unit_done(eng, u):
            eng.wait_ge(sem(f"slot{u % RING}_used"), u // RING + 1)

        FT1_AT = 2 * HG * NH * N + 2 * NH * N
        RES_AT = FT1_AT + NH * HEADS * (HE + 1)
        assert RES_AT + NH * D <= 8192

        xsel2 = view(scratch, 0, KD, E2 * CAP2)
        xsel2c = view(scratch, 0, KD, 2, E2 * CAP2 // 2)
        o = KD * E2 * CAP2
        mid2 = [view(scratch, o + p * CAP2, CAP2) for p in range(2)]
        pe_in2 = view(scratch, o + 2 * CAP2, NH, CAP2)
        pwe2 = view(scratch, o + 2 * CAP2 + NH * CAP2, N)
        y2 = view(scratch, o + 2 * CAP2 + NH * CAP2 + N, D)
        assert o + 2 * CAP2 + NH * CAP2 + N + D <= 8192
        p2 = view(qflat, 0, NH, E2, CAP2)
        p2f = view(qflat, 0, NH, E2 * CAP2)
        UPE2 = FT2 // 3

        def overflow(eng, body):
            eng.wait_ge(sem("over_ready"), 1)
            most = eng.value_load(over[0:1, 0:1], min_val=0, max_val=N)
            with eng.If(most > CAP2):
                body()

        xsel = view(scratch, 0, KD, E1 * SLOTS)
        p1f = view(qflat, 0, NH, E1 * SLOTS)
        o = KD * E1 * SLOTS
        xe = [view(scratch, o + p * KD * SLOTS, KD, SLOTS) for p in range(2)]
        o += 2 * KD * SLOTS
        pe_in = [view(scratch, o + p * NH * P, NH, 4, SLOTS) for p in range(2)]
        o += 2 * NH * P
        pwe = view(scratch, o, N)
        e_silu = view(scratch, o + N, P)
        e_h = view(scratch, o + N + P, P)
        e_hT = view(scratch, o + N + 2 * P, P)
        e_y = view(scratch, o + N + 3 * P, D)
        assert o + N + 3 * P + D <= 6656
        GROUPS = FT1 // 4

        def onehots(c):
            b = scratch[:, 0:2048].bitcast(BF16)
            o = (c % 4) * 1024
            return b[:, o:o + N], b[:, o + N:o + N + REL * N]

        units = STAGE_UNITS[STAGES - 1]
        block = ctx.enter_context(nc.Block())

        @block.sync
        def _(sp):
            sp.dma_start(edi[:, :, :], edges).then_inc(sem("edges_in"), 16)
            sp.dma_start(x[:, :, :], xin).then_inc(sem("x_in"), 16)
            sp.dma_start(sm[:, :], small).then_inc(sem("small_in"), 16)
            sp.dma_start(qTs[:, :, :], qT).then_inc(sem("q_in"), 16)
            if STAGES >= 6:
                sp.dma_start(b2r[:, :], rows8).then_inc(sem("rows_in"), 16)
                sp.dma_start(rw1[:, :], row1).then_inc(sem("row1_in"), 16)
            for s in range(min(RING, units)):
                sp.dma_start(ring[:, s, :], weights[s]).then_inc(sem(f"slot{s}_full"), 16)
            rounds, rest = divmod(units, RING)
            if rounds > 1:
                with sp.Fori(1, rounds) as r:
                    for s in range(RING):
                        sp.wait_ge(sem(f"slot{s}_used"), r)
                        sp.dma_start(ring[:, s, :], weights[bass.ds(r * RING + s, 1)].rearrange("o p n -> (o p) n")
                                     ).then_inc(sem(f"slot{s}_full"), 16)
            if rounds:
                for s in range(rest):
                    sp.wait_ge(sem(f"slot{s}_used"), rounds)
                    sp.dma_start(ring[:, s, :], weights[rounds * RING + s]).then_inc(sem(f"slot{s}_full"), 16)
            sp.wait_ge(sem("result"), 1)
            sp.dma_start(out, x[:, :, :]).then_inc(sem("stored"), 16)
            sp.wait_ge(sem("stored"), 16)

        @block.gpsimd
        def _(g):
            g.iota(iota[:, :], [[1, REL * N]], base=0, channel_multiplier=0,
                   allow_small_or_imprecise_dtypes=True).then_inc(sem("iota_set"), 1)
            g.memset(ident[:, :], 0.0).then_inc(sem("pool_set"), 1)
            g.memset(ones[:, :], 1.0).then_inc(sem("ones_set"), 1)
            g.memset(epst[:, :], EPS).then_inc(sem("ones_set"), 1)
            g.memset(low[:, :, :], 0.0).then_inc(sem("pool_set"), 1)
            g.wait_ge(sem("pool_set"), 2)
            g.affine_select(out=ident[:, :], in_=ident[:, :], compare_op=ALU.not_equal, fill=1.0, base=0,
                            pattern=[[-1, P]], channel_multiplier=1).then_inc(sem("ident_set"), 1)
            g.affine_select(out=low[:, :, :], in_=low[:, :, :], compare_op=ALU.is_ge, fill=1.0, base=0,
                            pattern=[[-1, E2], [1, E2]], channel_multiplier=0).then_inc(sem("low_set"), 1)

            g.memset(tri[:, :], 1.0).then_inc(sem("tri_init"), 1)
            g.wait_ge(sem("tri_init"), 1)
            g.affine_select(out=tri[:, :], in_=tri[:, :], compare_op=ALU.is_gt, fill=0.0, base=0,
                            pattern=[[1, P]], channel_multiplier=-1).then_inc(sem("tri_set"), 1)

            def gate_sum(gate, c, par, wait):
                s = view(scratch, par * NB * L, NB, L)
                if wait is not None:
                    g.wait_ge(sem("gate_prod"), wait)
                g.tensor_tensor(s, hgf[:, bass.ds(c * NB, NB)].unsqueeze(2).to_broadcast([P, NB, L]),
                                gflat[:, bass.ds(c * L, L)].unsqueeze(1).to_broadcast([P, NB, L]),
                                ALU.add).then_inc(sem("gate_sum"), 1)

            hgf = gate_in[:, KD * B * L:]
            CH = KD * B
            for gate in range(2):
                g.wait_ge(sem("hg_ready"), gate + 1)
                g.wait_ge(sem("qg_ready"), KD)
                gate_sum(gate, 0, 0, None)
                gate_sum(gate, 1, 1, None)
                with g.Fori(1, CH // 2) as i:
                    for par in range(2):
                        gate_sum(gate, i * 2 + par, par, i * 2 + (CH * gate + par - 1))

            if STAGES >= 4:
                lt = view(gflat, 0, NH, N)
                g.wait_ge(sem("ln_Tv"), 4)
                g.memset(lt, 1.0).then_inc(sem("lt_set"), 1)
                g.wait_ge(sem("lt_set"), 1)
                for h in range(NH):
                    g.affine_select(out=lt[:, h, :], in_=lt[:, h, :], compare_op=ALU.is_gt, fill=0.0, base=h * P,
                                    pattern=[[-1, N]], channel_multiplier=1).then_inc(sem("lt_set"), 1)
                g.wait_ge(sem("xsel_odd"), KD // 2)
                g.wait_ge(sem("xsel_even"), KD // 2)
                g.wait_ge(sem("pw_ready"), 1)

                def stage_expert(e, par):
                    g.tensor_copy(xe[par], xsel[:, :, bass.ds(e * SLOTS, SLOTS)])
                    for h in range(NH):
                        last = g.tensor_copy(pe_in[par][:, h, :, :], p1f[:, h, bass.ds(e * SLOTS, SLOTS)].unsqueeze(1)
                                             .to_broadcast([P, 4, SLOTS]))
                    last.then_inc(sem("xe_ready"), 1)

                for par in range(2):
                    stage_expert(par, par)
                with g.Fori(1, E1 // 2) as i:
                    for par in range(2):
                        g.wait_ge(sem("y1_ready"), i * 2 + (par - 1))
                        stage_expert(i * 2 + par, par)

            def experts2(t):
                g.wait_ge(sem("pw2_ready" + t), 1)
                g.tensor_copy(pe_in2, p2f[:, :, 0:CAP2]).then_inc(sem("stage2" + t), 1)
                if t:
                    fetch2(0)
                with g.Fori(1, E2) as i:
                    g.wait_ge(sem("turn2" + t), i)
                    g.tensor_copy(pe_in2, p2f[:, :, bass.ds(i * CAP2, CAP2)]).then_inc(sem("stage2" + t), 1)
                    if t:
                        fetch2(i)

            def fetch2(e):
                for U in range(UPE2):
                    g.wait_ge(sem("ovw_used"), e * UPE2 + (U + 1))
                    src = weights[U_E2 + U] if isinstance(e, int) else \
                        weights[bass.ds(e * UPE2 + (U_E2 + U), 1)].rearrange("o p n -> (o p) n")
                    g.dma_start(ovw[:, :], src).then_inc(sem("ovw_full"), 16)

            if STAGES >= 6:
                experts2("")
                overflow(g, lambda: experts2("_ov"))

        @block.tensor
        def _(pe):
            mm = nc.tensor.matmul

            def arrived(u):
                pe.wait_ge(sem(f"slot{u % RING}_full"), 16 * (u // RING + 1))

            def used(u, last):
                last.then_inc(sem(f"slot{u % RING}_used"), 1)

            def product_T(u, bank, act, start, stop):
                w = unit(u)
                arrived(u)
                for n in range(KD):
                    for k in range(KD):
                        last = mm(feat(bank)[:, n, :], w[:, k * D + n * P:k * D + (n + 1) * P], act[:, k, :],
                                  start=start and k == 0 and n % 2 == 0, stop=stop and k == KD - 1,
                                  skip_group_check=True)
                used(u, last)
                return last

            def product_N(w, act, bias=None):
                for h in range(NH):
                    for j in range(2):
                        o = ps[:, 4 + 2 * h + j, 0:HD]
                        for k in range(KD):
                            last = mm(o, act[:, k, h * P:(h + 1) * P], w[:, k * D + j * HD:k * D + (j + 1) * HD],
                                      start=k == 0, stop=k == KD - 1 and bias is None)
                        if bias is not None:
                            last = mm(o, ones[0:1, :], bias[:, j * HD:(j + 1) * HD], start=False, stop=True)
                return last

            def layernorm_T(n):
                for h in range(NH):
                    pe.wait_ge(sem("ln_xn"), NH * n + h + 1)
                    for k in range(KD):
                        last = nc.tensor.transpose(feat(0)[:, k, h * P:(h + 1) * P],
                                                   xn[:, h, k * P:(k + 1) * P], ident[:, :])
                last.then_inc(sem("ln_tp"), 1)

            def normalised(n):
                pe.wait_ge(sem("ln_Ta"), n + 1)
                pe.wait_ge(sem("ln_Tv"), n + 1)

            pe.wait_ge(sem("ident_set"), 1)
            pe.wait_ge(sem("ones_set"), 2)
            layernorm_T(0)
            pe.wait_ge(sem("q_in"), 16)
            arrived(U_QG)
            w = unit(U_QG)
            for n in range(KD):
                if n >= 4:
                    pe.wait_ge(sem("qg_ready"), n - 3)
                for k in range(KD):
                    last = mm(ps[:, 4 + n % 4, :], w[:, k * D + n * P:k * D + (n + 1) * P], qTs[:, k, :],
                              start=k == 0, stop=k == KD - 1)
                if n < KD - 1:
                    last.then_inc(sem("qg_done"), 1)
            used(U_QG, last)

            def graph():
                for c in range(EC):
                    pe.wait_ge(sem("onehot_ready"), c + 1)
                    s_oh, k_oh = onehots(c)
                    for h in range(NH):
                        mm(ps[:, 2 * h, :], s_oh[:, h * P:(h + 1) * P], k_oh[:, 0:512],
                           start=c == 0, stop=c == EC - 1)
                        last = mm(ps[:, 2 * h + 1, 0:N], s_oh[:, h * P:(h + 1) * P], k_oh[:, 512:768],
                                  start=c == 0, stop=c == EC - 1)
                    last.then_inc(sem("onehot_used"), 1)
                pe.wait_ge(sem("adj_raw"), 1)
                for j in range(2):
                    for h in range(NH):
                        last = mm(ps[:, j, 0:HD], ones[:, :], adj[:, h, j * HD:(j + 1) * HD],
                                  start=h == 0, stop=h == NH - 1)
                last.then_inc(sem("relcount"), 1)
                pe.wait_ge(sem("cT_ready"), 1)
                for dh in range(NH):
                    for sh in range(NH):
                        last = nc.tensor.transpose(ps[:, 2, dh * N + sh * P:dh * N + (sh + 1) * P],
                                                   cT[:, sh, dh * P:(dh + 1) * P], ident[:, :])
                last.then_inc(sem("cN_tp"), 1)
                pe.wait_ge(sem("dis_ready"), 1)
                for h in range(NH):
                    last = nc.tensor.transpose(ps[:, 3, h * P:(h + 1) * P],
                                               dis[:, h:h + 1].to_broadcast([P, P]), ident[:, :])
                last.then_inc(sem("disrow"), 1)

            def rgcn(r, u0, actN, actT):
                product_T(u0, 4, actT, True, False)
                if r == 0:
                    graph()
                    pe.wait_ge(sem("adj_ready"), 1)
                    pe.wait_ge(sem("gcn_ready"), 1)
                for j in range(KD):
                    if j >= 2:
                        pe.wait_ge(sem("g_copied_a"), KD * r + j - 1)
                        pe.wait_ge(sem("g_copied_v"), KD * r + j - 1)
                    bk = 2 * (j % 2)
                    for h in range(NH):
                        mm(ps[:, bk, :], actN[:, h, j * P:(j + 1) * P], adj[:, h, 0:512],
                           start=h == 0, stop=h == NH - 1)
                    for h in range(NH):
                        last = mm(ps[:, bk + 1, 0:N], actN[:, h, j * P:(j + 1) * P], adj[:, h, 512:768],
                                  start=h == 0, stop=h == NH - 1)
                    last.then_inc(sem("g_done"), 1)
                pe.wait_ge(sem("g_copied_a"), KD * (r + 1))
                pe.wait_ge(sem("g_copied_v"), KD * (r + 1))
                for rel in range(REL):
                    product_T(u0 + 1 + rel, 4, view(scratch, rel * KD * N, KD, N), False, rel == REL - 1)

            def gate(r, u0):
                pe.wait_ge(sem("hT_ready"), r + 1)
                product_T(u0, 0, hT, True, True)
                product_T(u0 + 1, 4, hT, True, False)
                pe.wait_ge(sem("qi_ready"), (r + 1) * KD * B // 2)
                product_T(u0 + 2, 4, qiT, False, True)
                pe.wait_ge(sem("hn_ready"), r + 1)
                for h in range(NH):
                    for k in range(KD):
                        last = nc.tensor.transpose(ps[:, 4 + 2 * h + k // 3, (k % 3) * P:(k % 3 + 1) * P],
                                                   hT[:, k, h * P:(h + 1) * P], ident[:, :])
                last.then_inc(sem("hn_nat"), 1)

            normalised(0)
            pe.wait_ge(sem("qg_ready"), KD)
            rgcn(0, U_RG1, xn, xT)
            gate(0, U_GT1)
            pe.wait_ge(sem("hnat_ready"), 1)
            rgcn(1, U_RG2, xn, hT)
            gate(1, U_GT2)

            if STAGES >= 2:
                layernorm_T(1)
                arrived(U_FF0)
                normalised(1)
                pe.wait_ge(sem("sign_ready"), 1)
                last = product_N(unit(U_FF0), xT)
                used(U_FF0, last)

            def gat(n, lnidx):
                layernorm_T(lnidx)
                normalised(lnidx)
                pe.wait_ge(sem("gat_w"), n + 1)
                bd = view(gflat, 0, 2, P)
                for i, s in ((0, "ft"), (1, "res")):
                    if i:
                        pe.wait_ge(sem("ft_ready"), n + 1)
                    for h in range(NH):
                        for k in range(KD):
                            last = mm(ps[:, 4 + 2 * h + k // 3, (k % 3) * P:(k % 3 + 1) * P],
                                      xT[:, k, h * P:(h + 1) * P], bd[:, i, :], start=True, stop=True)
                    last.then_inc(sem(f"{s}_done"), 1)
                for k in range(KD):
                    last = mm(feat(0)[:, k, :], bd[:, 0, :], xT[:, k, :], start=True, stop=True)
                last.then_inc(sem("ftT_done"), 1)
                pe.wait_ge(sem("ftT_ready"), n + 1)
                al = view(gflat, 2 * P, KD, 2)
                ar = view(gflat, 2 * P + 2 * KD, KD, 2)
                for h in range(NH):
                    for k in range(KD):
                        last = mm(ps[:, 3, h * HEADS + 2 * k:h * HEADS + 2 * k + 2], hT[:, k, h * P:(h + 1) * P],
                                  ar[:, k, :], start=True, stop=True)
                last.then_inc(sem("a2_done"), 1)
                pe.wait_ge(sem("a2_ready"), n + 1)
                pe.wait_ge(sem("res_ready"), n + 1)
                for gi in range(HEADS // HG):
                    G = n * (HEADS // HG) + gi
                    if gi:
                        pe.wait_ge(sem("arow_taken"), G)
                    for q in range(HG):
                        h = gi * HG + q
                        last = mm(ps[:, q // 2, (q % 2) * N:(q % 2 + 1) * N],
                                  al[:, h // 2, h % 2:h % 2 + 1].to_broadcast([P, P]), hT[:, h // 2, :],
                                  start=True, stop=True)
                    last.then_inc(sem("arow_done"), 1)
                    pe.wait_ge(sem("att_ready"), G + 1)
                    s = view(scratch, (gi % 2) * HG * NH * N, HG, NH, N)

                    def turn(q):
                        h = gi * HG + q
                        M = n * HEADS + h
                        if h >= 2:
                            pe.wait_ge(sem("wT_ready"), M - 1)
                        for sh in range(NH):
                            for dh in range(NH):
                                last = nc.tensor.transpose(ps[:, 2 + h % 2, sh * N + dh * P:sh * N + (dh + 1) * P],
                                                           s[:, q, dh, sh * P:(sh + 1) * P], ident[:, :])
                        last.then_inc(sem("wT_done"), 1)

                    def collect(q):
                        h = gi * HG + q
                        pe.wait_ge(sem("wT_ready"), n * HEADS + h + 1)
                        wt = view(scratch, 2 * HG * NH * N + (h % 2) * NH * N, NH, N)
                        for dh in range(NH):
                            c = (h % 6) * (HE + 1)
                            for sh in range(NH):
                                last = mm(ps[:, 4 + 2 * dh + h // 6, c:c + HE + 1], wt[:, sh, dh * P:(dh + 1) * P],
                                          ft1[:, sh, h, :], start=sh == 0, stop=sh == NH - 1)
                        last.then_inc(sem("head_done"), 1)

                    ft1 = view(scratch, FT1_AT, NH, HEADS, HE + 1)
                    turn(0)
                    for q in range(HG):
                        if q + 1 < HG:
                            turn(q + 1)
                        collect(q)

            if STAGES >= 3:
                gat(0, 2)

            if STAGES >= 4:
                layernorm_T(3)
                normalised(3)
                for h in range(NH):
                    for k in range(KD):
                        last = mm(ps[:, 3, h * E1:(h + 1) * E1], xT[:, k, h * P:(h + 1) * P],
                                  S("gate")[:, k * E1:(k + 1) * E1], start=k == 0, stop=k == KD - 1)
                last.then_inc(sem("score_done"), 1)
                pe.wait_ge(sem("score_ready"), 1)
                for e in range(E1):
                    if e >= 4:
                        pe.wait_ge(sem("rank_taken"), e - 3)
                    for h in range(NH):
                        last = nc.tensor.transpose(ps[:, e % 4, h * P:(h + 1) * P],
                                                   sc1[:, h, e:e + 1].to_broadcast([P, P]), ident[:, :])
                    last.then_inc(sem("srow_done"), 1)
                pe.wait_ge(sem("onehot1_ready"), 1)
                p1 = view(qflat, 0, NH, E1 * SLOTS)
                for k in range(KD):
                    if k >= 2:
                        pe.wait_ge(sem("xsel_odd" if k % 2 else "xsel_even"), k // 2)
                    for h in range(NH):
                        last = mm(ps[:, k % 2, :], xn[:, h, k * P:(k + 1) * P], p1[:, h, :],
                                  start=h == 0, stop=h == NH - 1)
                    last.then_inc(sem("xsel_done"), 1)
                hs = [view(scratch, 6656 + p * N, N) for p in range(4)]

                def sh_down(f):
                    u = U_SH + f // 2
                    wd = unit(u)[:, (f % 2) * 18 * P + 12 * P:(f % 2) * 18 * P + 18 * P]
                    pe.wait_ge(sem("sh_act"), f + 1)
                    for h in range(NH):
                        for j in range(2):
                            last = mm(ps[:, 4 + 2 * h + j, 0:HD], hs[f % 4][:, h * P:(h + 1) * P],
                                      wd[:, j * HD:(j + 1) * HD], start=f == 0, stop=f == SH_FT - 1,
                                      skip_group_check=True)
                    if f % 2:
                        used(u, last)

                for f in range(SH_FT):
                    u = U_SH + f // 2
                    w = unit(u)[:, (f % 2) * 18 * P:(f % 2) * 18 * P + 12 * P]
                    if f % 2 == 0:
                        arrived(u)
                    if f == 0:
                        pe.wait_ge(sem("xsel_odd"), KD // 2)
                        pe.wait_ge(sem("xsel_even"), KD // 2)
                    for i in range(2):
                        for k in range(KD):
                            last = mm(ps[:, f % 4, i * N:(i + 1) * N], w[:, (i * KD + k) * P:(i * KD + k + 1) * P],
                                      xT[:, k, :], start=k == 0, stop=k == KD - 1)
                    last.then_inc(sem("sh_gu"), 1)
                    if f:
                        sh_down(f - 1)
                sh_down(SH_FT - 1)

                BODY = 4 * GROUPS
                assert BODY % RING == 0
                with pe.Fori(0, E1 // 2) as i:
                    def slot_of(U):
                        return (U_E1 + U) % RING

                    def group(par, gi):
                        G = par * GROUPS + gi
                        done = i * (2 * GROUPS) + (G + 1)
                        for half in range(2):
                            U = 2 * G + half
                            pe.wait_ge(sem(f"slot{slot_of(U)}_full"),
                                       i * (16 * BODY // RING) + 16 * ((U_E1 + U) // RING + 1))
                            for kk in range(3):
                                for j in range(4):
                                    b = (kk * 4 + j) * 2 * P
                                    last = mm(ps[32 * j:32 * j + 32, 0, 0:2 * P], xe[par][:, 3 * half + kk, :],
                                              ring[:, slot_of(U), b:b + 2 * P], start=half == 0 and kk == 0,
                                              stop=half == 1 and kk == 2)
                        last.then_inc(sem("e1_gu"), 1)
                        pe.wait_ge(sem("e1_act"), done)
                        nc.tensor.transpose(ps[:, 1, 0:P], e_h, ident[:, :]).then_inc(sem("e1_turn"), 1)
                        pe.wait_ge(sem("e1_hT"), done)
                        for c in range(2):
                            for j in range(4):
                                U = 2 * G + j // 2
                                b = (24 + (j % 2) * KD) * P + c * HD
                                last = mm(ps[32 * j:32 * j + 32, 2 + c, 0:HD], e_hT[:, 32 * j:32 * j + 32],
                                          ring[:, slot_of(U), b:b + HD], start=gi == 0, stop=gi == GROUPS - 1)
                                if c and j % 2:
                                    last.then_inc(sem(f"slot{slot_of(U)}_used"), 1)

                    for par in range(2):
                        pe.wait_ge(sem("xe_ready"), i * 2 + (par + 1))
                        for h in range(NH):
                            last = nc.tensor.transpose(ps[:, 1, (h + 1) * P:(h + 2) * P],
                                                       pe_in[par][:, h, :, :].rearrange("p a b -> p (a b)"),
                                                       ident[:, :])
                        last.then_inc(sem("pwe_turn"), 1)
                        for gi in range(GROUPS):
                            group(par, gi)
                        pe.wait_ge(sem("pwe_ready"), i * 2 + (par + 1))
                        pe.wait_ge(sem("y1_ready"), i * 2 + (par + 1))
                        for h in range(NH):
                            for c in range(2):
                                last = mm(ps[:, 4 + 2 * h + c, 0:HD], pwe[:, h * P:(h + 1) * P],
                                          e_y[:, c * HD:(c + 1) * HD], start=False, stop=True,
                                          skip_group_check=True)
                        last.then_inc(sem("combined"), 1)

            if STAGES >= 5:
                gat(1, 4)

            def dense(tag, u0, experts, unroll, upe, fpu):
                fe = upe * fpu
                body_u, body_f = unroll * upe, unroll * fe
                assert body_u % RING == 0 and body_f % 4 == 0
                mid = [view(scratch, p * N, N) for p in range(4)]
                with pe.Fori(0, experts // unroll) as i:
                    def down(F):
                        U, ft, q = F // fpu, F % fpu, F // fe
                        slot = (u0 + U) % RING
                        pe.wait_ge(sem(f"{tag}_mid"), i * body_f + (F + 1))
                        if F % fe == 0:
                            pe.wait_ge(sem(f"{tag}_yfree"), i * unroll + (q + 1))
                        wd = ring[:, slot, (ft * 12 + KD) * P:(ft * 12 + 12) * P]
                        for h in range(NH):
                            for j in range(2):
                                last = mm(ps[:, 4 + 2 * h + j, 0:HD], mid[F % 4][:, h * P:(h + 1) * P],
                                          wd[:, j * HD:(j + 1) * HD], start=F % fe == 0, stop=F % fe == fe - 1)
                        if ft == fpu - 1:
                            last.then_inc(sem(f"slot{slot}_used"), 1)

                    for F in range(body_f):
                        U, ft = F // fpu, F % fpu
                        slot = (u0 + U) % RING
                        if ft == 0:
                            pe.wait_ge(sem(f"slot{slot}_full"),
                                       i * (16 * body_u // RING) + 16 * ((u0 + U) // RING + 1))
                        for k in range(KD):
                            last = mm(ps[:, F % 4, 0:N], ring[:, slot, (ft * 12 + k) * P:(ft * 12 + k + 1) * P],
                                      xT[:, k, :], start=k == 0, stop=k == KD - 1)
                        last.then_inc(sem(f"{tag}_up"), 1)
                        if F:
                            down(F - 1)
                    down(body_f - 1)

            def scores(act, w, bias, name):
                for h in range(NH):
                    for k in range(KD):
                        last = mm(ps[:, 3, h * E2:(h + 1) * E2], act[:, k, h * P:(h + 1) * P],
                                  w[:, k * E2:(k + 1) * E2], start=k == 0, stop=k == KD - 1 and bias is None)
                    if bias is not None:
                        last = mm(ps[:, 3, h * E2:(h + 1) * E2], ones[0:1, :], bias, start=False, stop=True)
                last.then_inc(sem(name), 1)

            if STAGES >= 6:
                layernorm_T(5)
                normalised(5)
                product_T(U_R2, 0, xT, True, True)
                pe.wait_ge(sem("r2_ready"), 1)
                pe.wait_ge(sem("row1_in"), 16)
                pe.wait_ge(sem("rows_in"), 16)
                scores(hT, S("wr2"), rw1[:, D:D + E2], "score2_done")
                pe.wait_ge(sem("w2_ready"), 1)
                for h in range(NH):
                    last = nc.tensor.transpose(ps[0:E2, 2, h * P:(h + 1) * P], rt[:, 5, h, :], ident[:, :])
                last.then_inc(sem("w2T_done"), 1)
                pe.wait_ge(sem("tri_set"), 1)
                for h in range(NH):
                    for hh in range(h + 1):
                        last = mm(ps[:, 3, h * E2:(h + 1) * E2], tri[:, :] if hh == h else ones[:, :],
                                  rt[:, 2, hh, :], start=hh == 0, stop=hh == h)
                for hh in range(NH):
                    last = mm(ps[:, 3, NH * E2:(NH + 1) * E2], ones[:, :], rt[:, 2, hh, :],
                              start=hh == 0, stop=hh == NH - 1)
                last.then_inc(sem("pos_done"), 1)

                def experts2(t):
                    if t:
                        pe.sem_inc(sem("ovw_used"), 1)
                    pe.wait_ge(sem("w2T_ready" + t), 1)
                    for h in range(NH):
                        for c in range(2):
                            mm(ps[:, 4 + 2 * h + c, 0:HD], wT8[:, h * P:(h + 1) * P],
                               b2r[:, c * HD:(c + 1) * HD], start=True, stop=False, skip_group_check=True)
                    pe.wait_ge(sem("onehot2_ready" + t), 1)
                    for k in range(KD):
                        for c in range(2):
                            if k:
                                pe.wait_ge(sem(("xsel2_a", "xsel2_v")[c] + t), k)
                            for h in range(NH):
                                last = mm(ps[:, c, :], xn[:, h, k * P:(k + 1) * P],
                                          p2f[:, h, c * 512:(c + 1) * 512], start=h == 0, stop=h == NH - 1)
                            last.then_inc(sem("xsel2_done" + t), 1)
                    pe.wait_ge(sem("xsel2_a" + t), KD)
                    pe.wait_ge(sem("xsel2_v" + t), KD)
                    with pe.Fori(0, E2) as i:
                        def unit2(U):
                            return ovw[:, :] if t else ring[:, (U_E2 + U) % RING, :]

                        def down(F):
                            U, ft = F // 3, F % 3
                            pe.wait_ge(sem("mid2" + t), i * FT2 + (F + 1))
                            for c in range(2):
                                b = (ft * 12 + KD) * P + c * HD
                                last = mm(ps[:, 2 + c, 0:HD], mid2[F % 2], unit2(U)[:, b:b + HD],
                                          start=F == 0, stop=F == FT2 - 1)
                                if F == FT2 - 1 and c == 0:
                                    last.then_inc(sem("y2_first" + t), 1)
                            if ft == 2:
                                last.then_inc(sem("ovw_used" if t else f"slot{(U_E2 + U) % RING}_used"), 1)

                        pe.wait_ge(sem("stage2" + t), i + 1)
                        for h in range(NH):
                            last = nc.tensor.transpose(ps[:, 1, (h + 1) * P:(h + 2) * P], pe_in2[:, h, :], ident[:, :])
                        last.then_inc(sem("turn2" + t), 1)
                        for F in range(FT2):
                            U, ft = F // 3, F % 3
                            if ft == 0 and t:
                                if F:
                                    down(F - 1)
                                pe.wait_ge(sem("ovw_full"), i * (16 * UPE2) + 16 * (U + 1))
                            elif ft == 0:
                                pe.wait_ge(sem(f"slot{(U_E2 + U) % RING}_full"),
                                           i * (16 * UPE2 // RING) + 16 * ((U_E2 + U) // RING + 1))
                            if F == 1:
                                pe.wait_ge(sem("pwe2_ready" + t), i + 1)
                            for k in range(KD):
                                b = (ft * 12 + k) * P
                                last = mm(ps[:, F % 2, 0:CAP2], unit2(U)[:, b:b + P],
                                          xsel2[:, k, bass.ds(i * CAP2, CAP2)], start=k == 0, stop=k == KD - 1)
                            last.then_inc(sem("up2" + t), 1)
                            if F and not (ft == 0 and t):
                                down(F - 1)
                        down(FT2 - 1)
                        for c in range(2):
                            pe.wait_ge(sem("y2_ready" + t), i * 2 + (c + 1))
                            for h in range(NH):
                                last = mm(ps[:, 4 + 2 * h + c, 0:HD], pwe2[:, h * P:(h + 1) * P],
                                          y2[:, c * HD:(c + 1) * HD], start=False, stop=True,
                                          skip_group_check=True)
                        last.then_inc(sem("combined2" + t), 1)

                experts2("")
                overflow(pe, lambda: experts2("_ov"))

            if STAGES >= 7:
                layernorm_T(6)
                for k in range(KD):
                    if k == 0:
                        normalised(6)
                    for h in range(NH):
                        last = mm(feat(0)[:, k, :], xn[:, h, k * P:(k + 1) * P], gcn[:, h, :],
                                  start=h == 0, stop=h == NH - 1)
                last.then_inc(sem("agg3_done"), 1)
                pe.wait_ge(sem("agg3_ready"), 1)
                arrived(U_L3G)
                last = product_N(unit(U_L3G), hT, rw1[:, 0:D])
                used(U_L3G, last)

            if STAGES >= 8:
                layernorm_T(7)
                normalised(7)
                scores(xT, S("rw"), None, "score3_done")
                pe.wait_ge(sem("w3_ready"), 1)
                dense("e3", U_E3, E3, 4, 1, 3)

        @block.scalar
        def _(act):
            A = nc.scalar.activation

            def layernorm(n):
                act.wait_ge(sem("ln_var"), n + 1)
                if n == 0:
                    act.wait_ge(sem("ones_set"), 2)
                A(sd[:, :], mv[:, :, 1], ACT.Sqrt, bias=epst[:, 0:1]).then_inc(sem("ln_sd"), 1)
                act.wait_ge(sem("ln_tp"), n + 1)
                A(xT[:, 0:4, :], feat(0)[:, 0:4, :], ACT.Copy).then_inc(sem("ln_Ta"), 1)

            layernorm(0)
            act.wait_ge(sem("small_in"), 16)
            for n in range(KD):
                if n < KD - 1:
                    act.wait_ge(sem("qg_done"), n + 1)
                else:
                    unit_done(act, U_QG)
                A(qgT[:, n, :], ps[:, 4 + n % 4, :], ACT.Identity, bias=S("bg")[:, n:n + 1]).then_inc(sem("qg_ready"), 1)
            act.wait_ge(sem("deg_ready"), 1)
            A(dis[:, :], deg[:, :], ACT.Sqrt).then_inc(sem("deg_sqrt"), 1)

            for r in range(2):
                for j in range(KD):
                    act.wait_ge(sem("g_done"), KD * r + j + 1)
                    A(view(scratch, 0, REL, KD, N)[:, 0:2, j, :],
                      ps[:, 2 * (j % 2), :].rearrange("p (a b) -> p a b", a=2), ACT.Copy).then_inc(sem("g_copied_a"), 1)
                unit_done(act, (U_RG1, U_RG2)[r] + 3)
                for n in range(KD):
                    last = A(hT[:, n, :], feat(4)[:, n, :], ACT.Relu, bias=S(f"b{r + 1}")[:, n:n + 1])
                last.then_inc(sem("hT_ready"), 1)
                unit_done(act, (U_GT1, U_GT2)[r])
                A(hgT[:, :, :], feat(0), ACT.Copy).then_inc(sem("hg_ready"), 1)
                CH = KD * B
                with act.Fori(0, CH // 2) as i:
                    for par in range(2):
                        s = view(scratch, par * NB * L, NB * L)
                        act.wait_ge(sem("gate_sum"), i * 2 + (CH * r + par + 1))
                        A(s, s, ACT.Sigmoid).then_inc(sem("gate_sig"), 1)
                unit_done(act, (U_GT1, U_GT2)[r] + 2)
                for n in range(KD):
                    last = A(hgT[:, n, :], feat(4)[:, n, :], ACT.Sigmoid, bias=S("bq")[:, n:n + 1])
                last.then_inc(sem("alpha_ready"), 1)
                A(qiT[:, :, :], qiT[:, :, :], ACT.Tanh).then_inc(sem("alpha_ready"), 1)
                if r == 0:
                    act.wait_ge(sem("hn_nat"), 1)
                    A(xn[:, :, :].rearrange("p h (a b) -> p (h a) b", a=2), ps[:, 4:8, 0:HD], ACT.Copy
                      ).then_inc(sem("hnat_ready"), 1)

            if STAGES >= 2:
                layernorm(1)
                act.wait_ge(sem(f"slot{U_FF0 % RING}_full"), 16 * (U_FF0 // RING + 1))
                A(unit(U_FF0), unit(U_FF0), ACT.Sign).then_inc(sem("sign_ready"), 1)

            def gat(n, lnidx):
                layernorm(lnidx)
                act.wait_ge(sem("ft_done"), n + 1)
                ft1 = view(scratch, FT1_AT, NH, HEADS, HE + 1)
                act.wait_ge(sem("gat_w"), n + 1)
                for h in range(NH):
                    last = A(ft1[:, h, :, 0:HE].rearrange("p (a b) e -> p a b e", a=2),
                             nat(h).rearrange("p a (b e) -> p a b e", e=HE), ACT.Copy)
                last.then_inc(sem("ft_ready"), 1)
                act.wait_ge(sem("ftT_done"), n + 1)
                A(hT[:, :, :], feat(0), ACT.Copy).then_inc(sem("ftT_ready"), 1)
                act.wait_ge(sem("res_done"), n + 1)
                A(view(scratch, RES_AT, 2 * NH, HD), ps[:, 4:8, 0:HD], ACT.Copy).then_inc(sem("res_ready"), 1)
                for gi in range(HEADS // HG):
                    G = n * (HEADS // HG) + gi
                    s = view(scratch, (gi % 2) * HG * NH * N, HG, NH, N)
                    act.wait_ge(sem("arow_taken"), G + 1)
                    act.wait_ge(sem("a2_ready"), n + 1)
                    for q in range(HG):
                        for dh in range(NH):
                            last = A(s[:, q, dh, :], s[:, q, dh, :], ACT.Identity,
                                     bias=a2[:, dh, gi * HG + q:gi * HG + q + 1])
                    last.then_inc(sem("att_sum"), 1)
                    act.wait_ge(sem("hmax_ready"), G + 1)
                    for q in range(HG):
                        for dh in range(NH):
                            last = A(s[:, q, dh, :], s[:, q, dh, :], ACT.Exp, bias=hm[:, 3, q, dh:dh + 1])
                    last.then_inc(sem("att_exp"), 1)
                    for q in range(HG):
                        h = gi * HG + q
                        act.wait_ge(sem("wT_done"), n * HEADS + h + 1)
                        if h >= 2:
                            act.wait_ge(sem("head_done"), n * HEADS + h - 1)
                        A(view(scratch, 2 * HG * NH * N + (h % 2) * NH * N, NH * N), ps[:, 2 + h % 2, :],
                          ACT.Copy).then_inc(sem("wT_ready"), 1)

            if STAGES >= 3:
                gat(0, 2)

            if STAGES >= 4:
                layernorm(3)
                act.wait_ge(sem("score_done"), 1)
                A(sc1[:, :, :].rearrange("p a b -> p (a b)"), ps[:, 3, 0:NH * E1], ACT.Sigmoid
                  ).then_inc(sem("score_ready"), 1)
                for k in range(0, KD, 2):
                    act.wait_ge(sem("xsel_done"), k + 1)
                    A(xsel[:, k, :], ps[:, k % 2, :], ACT.Copy).then_inc(sem("xsel_even"), 1)
                sg = [view(scratch, 7680 + p * N, N) for p in range(2)]
                for f in range(SH_FT):
                    act.wait_ge(sem("sh_gu"), f + 1)
                    if f >= 2:
                        act.wait_ge(sem("sh_act"), f - 1)
                    A(sg[f % 2], ps[:, f % 4, 0:N], ACT.Silu).then_inc(sem("sh_silu"), 1)
                with act.Fori(0, E1) as i:
                    act.wait_ge(sem("pwe_turn"), i + 1)
                    A(pwe, ps[:, 1, P:3 * P], ACT.Copy).then_inc(sem("pwe_ready"), 1)
                    for gi in range(GROUPS):
                        act.wait_ge(sem("e1_gu"), i * GROUPS + (gi + 1))
                        A(e_silu, ps[:, 0, 0:P], ACT.Silu).then_inc(sem("e1_silu"), 1)
                        act.wait_ge(sem("e1_turn"), i * GROUPS + (gi + 1))
                        A(e_hT, ps[:, 1, 0:P], ACT.Copy).then_inc(sem("e1_hT"), 1)

            if STAGES >= 5:
                gat(1, 4)

            def softmax_exp(name, done):
                act.wait_ge(sem(name), 1)
                for h in range(NH):
                    last = A(rt[:, 1, h, :], rt[:, 0, h, :], ACT.Exp, bias=rsm[:, 0, h:h + 1])
                last.then_inc(sem(done), 1)

            def dense(tag, experts, unroll, fe, biased):
                body_f = unroll * fe
                mid = [view(scratch, p * N, N) for p in range(4)]
                with act.Fori(0, experts // unroll) as i:
                    for F in range(body_f):
                        act.wait_ge(sem(f"{tag}_up"), i * body_f + (F + 1))
                        kw = {"bias": S("fb1")[:, bass.ds(i * fe + F, 1)]} if biased else {}
                        A(mid[F % 4], ps[:, F % 4, 0:N], ACT.Relu, **kw).then_inc(sem(f"{tag}_mid"), 1)

            if STAGES >= 6:
                layernorm(5)
                unit_done(act, U_R2)
                for n in range(KD):
                    last = A(hT[:, n, :], feat(0)[:, n, :], ACT.Relu, bias=S("br1")[:, n:n + 1])
                last.then_inc(sem("r2_ready"), 1)
                softmax_exp("max2_ready", "exp2")

                def experts2(t):
                    for k in range(KD):
                        act.wait_ge(sem("xsel2_done" + t), 2 * k + 1)
                        A(xsel2c[:, k, 0, :], ps[:, 0, :], ACT.Copy).then_inc(sem("xsel2_a" + t), 1)
                    with act.Fori(0, E2) as i:
                        act.wait_ge(sem("turn2" + t), i + 1)
                        A(pwe2, ps[:, 1, P:3 * P], ACT.Copy).then_inc(sem("pwe2_ready" + t), 1)
                        for F in range(FT2):
                            act.wait_ge(sem("up2" + t), i * FT2 + (F + 1))
                            A(mid2[F % 2], ps[:, F % 2, 0:CAP2], ACT.Relu,
                              bias=S("fb1")[:, bass.ds(i * FT2 + F, 1)]).then_inc(sem("mid2" + t), 1)

                experts2("")
                overflow(act, lambda: experts2("_ov"))
            if STAGES >= 7:
                layernorm(6)
                act.wait_ge(sem("agg3_done"), 1)
                A(hT[:, :, :], feat(0), ACT.Copy).then_inc(sem("agg3_ready"), 1)
            if STAGES >= 8:
                layernorm(7)
                softmax_exp("max3_ready", "exp3")
                dense("e3", E3, 4, FT3, False)

        @block.vector
        def _(v):
            link = Chain(v, sem("dve_own"))
            tt, ts, stt = nc.vector.tensor_tensor, nc.vector.tensor_scalar, nc.vector.scalar_tensor_tensor
            copy, red = nc.vector.tensor_copy, nc.vector.tensor_reduce

            def layernorm(n):
                for h in range(NH):
                    for j in range(2):
                        last = nc.vector.bn_stats(bnst[:, h, j, :], x[:, h, j * HD:(j + 1) * HD])
                link(last)
                for h in range(NH):
                    last = nc.vector.bn_aggr(mv[:, h, :], bnst[:, h, :, :].rearrange("p a b -> p (a b)"))
                last.then_inc(sem("ln_var"), 1)
                v.wait_ge(sem("ln_sd"), n + 1)
                link(nc.vector.reciprocal(rs[:, :], sd[:, :]))
                for h in range(NH):
                    ts(xn[:, h, :], x[:, h, :], mv[:, h, 0:1], rs[:, h:h + 1], ALU.subtract, ALU.mult
                       ).then_inc(sem("ln_xn"), 1)
                v.wait_ge(sem("ln_tp"), n + 1)
                copy(xT[:, 4:6, :], feat(0)[:, 4:6, :]).then_inc(sem("ln_Tv"), 1)

            def residual():
                for h in range(NH):
                    last = tt(halves(x, h), nat(h), halves(x, h), ALU.add)
                link(last)

            v.wait_ge(sem("x_in"), 16)
            layernorm(0)
            v.wait_ge(sem("edges_in"), 16)
            link(copy(edf[:, 0:3, :], edi[:, :, :]))
            link(stt(edf[:, 3, :], edf[:, 2, :], float(N), edf[:, 1, :], ALU.mult, ALU.add))
            v.wait_ge(sem("iota_set"), 1)
            for c in range(EC):
                if c >= 4:
                    v.wait_ge(sem("onehot_used"), c - 3)
                s_oh, k_oh = onehots(c)
                ts(s_oh, iota[:, 0:N], edf[:, 0, c:c + 1], None, ALU.is_equal)
                ts(k_oh, iota[:, :], edf[:, 3, c:c + 1], None, ALU.is_equal).then_inc(sem("onehot_ready"), 1)
            v.wait_ge(sem("onehot_used"), EC)
            for h in range(NH):
                copy(adj[:, h, 0:512], ps[:, 2 * h, :])
                last = copy(adj[:, h, 512:768], ps[:, 2 * h + 1, 0:N])
            last.then_inc(sem("adj_raw"), 1)
            v.wait_ge(sem("adj_raw"), 1)
            link(tt(cT[:, :, :], adj[:, :, 0:N], adj[:, :, N:2 * N], ALU.add))
            tt(cT[:, :, :], cT[:, :, :], adj[:, :, 2 * N:3 * N], ALU.add).then_inc(sem("cT_ready"), 1)
            rcnt = view(scratch, 2048, 2, HD)
            v.wait_ge(sem("relcount"), 1)
            link(ts(rcnt, ps[:, 0:2, 0:HD], 1.0, None, ALU.max))
            link(nc.vector.reciprocal(rcnt, rcnt))
            for h in range(NH):
                last = tt(halves(adj, h), halves(adj, h), rcnt, ALU.mult)
            last.then_inc(sem("adj_ready"), 1)
            v.wait_ge(sem("cN_tp"), 1)
            link(copy(cN[:, :, :].rearrange("p a b -> p (a b)"), ps[:, 2, :]))
            ts(far[:, :, :], cN[:, :, :], 0.0, FAR, ALU.is_equal, ALU.mult)
            link(red(deg[:, :], cN[:, :, :], AX.X, ALU.add))
            ts(deg[:, :], deg[:, :], 1.0, None, ALU.add).then_inc(sem("deg_ready"), 1)
            v.wait_ge(sem("deg_sqrt"), 1)
            nc.vector.reciprocal(dis[:, :], dis[:, :]).then_inc(sem("dis_ready"), 1)
            link(copy(gcn[:, :, :], cT[:, :, :]))
            v.wait_ge(sem("ident_set"), 1)
            for h in range(NH):
                last = tt(gcn[:, h, h * P:(h + 1) * P], gcn[:, h, h * P:(h + 1) * P], ident[:, :], ALU.add)
            link(last)
            v.wait_ge(sem("disrow"), 1)
            for h in range(NH):
                last = stt(gcn[:, h, :], gcn[:, h, :], dis[:, h:h + 1], ps[:, 3, 0:N], ALU.mult, ALU.mult)
            last.then_inc(sem("gcn_ready"), 1)

            qif = qiT[:, :, :].rearrange("p a b -> p (a b)")
            CH = KD * B
            for r in range(2):
                for j in range(KD):
                    v.wait_ge(sem("g_done"), KD * r + j + 1)
                    copy(view(scratch, 0, REL, KD, N)[:, 2, j, :], ps[:, 2 * (j % 2) + 1, 0:N]
                         ).then_inc(sem("g_copied_v"), 1)
                with v.Fori(0, CH // 2) as i:
                    for par in range(2):
                        s = view(scratch, par * NB * L, NB, L)
                        p = view(scratch, (2 + par) * NB * L, NB, L)
                        v.wait_ge(sem("gate_sig"), i * 2 + (CH * r + par + 1))
                        tt(p, s, qflat[:, bass.ds((i * 2 + par) * L, L)].unsqueeze(1).to_broadcast([P, NB, L]),
                           ALU.mult).then_inc(sem("gate_prod"), 1)
                        v.wait_ge(sem("gate_prod"), i * 2 + (CH * r + par + 1))
                        last = red(qif[:, bass.ds((i * 2 + par) * NB, NB)], p, AX.X, ALU.add)
                    last.then_inc(sem("qi_ready"), 1)
                v.wait_ge(sem("alpha_ready"), 2 * (r + 1))
                link(tt(qiT[:, :, :], qiT[:, :, :], hT[:, :, :], ALU.subtract))
                link(tt(qiT[:, :, :], qiT[:, :, :], hgT[:, :, :], ALU.mult))
                tt(hT[:, :, :], hT[:, :, :], qiT[:, :, :], ALU.add).then_inc(sem("hn_ready"), 1)
            v.wait_ge(sem("hn_nat"), 2)
            residual()

            if STAGES >= 2:
                layernorm(1)
                unit_done(v, U_FF0)
                residual()

            def gat(n, lnidx):
                bd = view(gflat, 0, 2, P)
                al = view(gflat, 2 * P, KD, 2)
                ar = view(gflat, 2 * P + 2 * KD, KD, 2)
                ft1 = view(scratch, FT1_AT, NH, HEADS, HE + 1)
                link(nc.vector.memset(gflat[:, 0:2 * P + 4 * KD], 0.0))
                for q in range(2):
                    pr = slice(q * HE, (q + 1) * HE)
                    copy(bd[pr, 0, pr], S(f"fc{n + 1}")[pr, :])
                    copy(bd[pr, 1, pr], S(f"res{n + 1}")[pr, :])
                    copy(al[pr, :, q], S(f"al{n + 1}")[pr, :])
                    copy(ar[pr, :, q], S(f"ar{n + 1}")[pr, :])
                nc.vector.memset(ft1[:, :, :, HE], 1.0).then_inc(sem("gat_w"), 1)
                layernorm(lnidx)
                v.wait_ge(sem("a2_done"), n + 1)
                copy(a2[:, :, :].rearrange("p a b -> p (a b)"), ps[:, 3, 0:NH * HEADS]).then_inc(sem("a2_ready"), 1)
                v.wait_ge(sem("a2_ready"), n + 1)
                for gi in range(HEADS // HG):
                    G = n * (HEADS // HG) + gi
                    s = view(scratch, (gi % 2) * HG * NH * N, HG, NH, N)
                    if gi >= 2:
                        v.wait_ge(sem("head_done"), n * HEADS + (gi - 1) * HG)
                    v.wait_ge(sem("arow_done"), G + 1)
                    rows = ps[:, 0:2, :].rearrange("p a (b n) -> p (a b) n", b=2)
                    for dh in range(NH):
                        last = tt(s[:, :, dh, :], rows[:, 0:HG, :], far[:, dh:dh + 1, :].to_broadcast([P, HG, N]),
                                  ALU.add)
                    link(last)
                    red(hm[:, 0, :, :], s, AX.X, ALU.max).then_inc(sem("arow_taken"), 1)
                    v.wait_ge(sem("arow_taken"), G + 1)
                    link(tt(hm[:, 1, :, :], hm[:, 0, :, :],
                            a2[:, :, gi * HG:(gi + 1) * HG].rearrange("p a b -> p b a"), ALU.add))
                    link(ts(hm[:, 2, :, :], hm[:, 1, :, :], 0.2, None, ALU.mult))
                    link(tt(hm[:, 2, :, :], hm[:, 2, :, :], hm[:, 1, :, :], ALU.max))
                    if gi:
                        v.wait_ge(sem("att_exp"), G)
                    ts(hm[:, 3, :, :], hm[:, 2, :, :], -1.0, None, ALU.mult)
                    v.wait_ge(sem("att_sum"), G + 1)
                    sf = view(scratch, (gi % 2) * HG * NH * N, HG * NH * N)
                    stt(sf, sf, 0.2, sf, ALU.mult, ALU.max).then_inc(sem("hmax_ready"), 1)
                    v.wait_ge(sem("att_exp"), G + 1)
                    for q in range(HG):
                        last = tt(s[:, q, :, :], s[:, q, :, :], cN[:, :, :], ALU.mult)
                    last.then_inc(sem("att_ready"), 1)
                v.wait_ge(sem("head_done"), (n + 1) * HEADS)
                v.wait_ge(sem("res_ready"), n + 1)
                t = view(scratch, 0, NH, 2, HD)
                res = view(scratch, RES_AT, NH, 2, HD)
                for dh in range(NH):
                    agg = ps[:, 4 + 2 * dh:6 + 2 * dh, 0:6 * (HE + 1)].rearrange("p a (b e) -> p a b e", e=HE + 1)
                    rd = rden[:, dh, :].rearrange("p (a b) -> p a b", a=2)
                    link(ts(rd, agg[:, :, :, HE], 1e-16, None, ALU.max))
                    link(nc.vector.reciprocal(rd, rd))
                    for a in range(2):
                        last = tt(t[:, dh, a, :].rearrange("p (b e) -> p b e", e=HE), agg[:, a, :, 0:HE],
                                  rd[:, a, :].unsqueeze(2).to_broadcast([P, 6, HE]), ALU.mult)
                    link(last)
                    link(tt(t[:, dh, :, :], t[:, dh, :, :], res[:, dh, :, :], ALU.add))
                    link(stt(halves(x, dh), t[:, dh, :, :], 0.0, halves(x, dh), ALU.max, ALU.add))

            if STAGES >= 3:
                gat(0, 2)

            if STAGES >= 4:
                layernorm(3)
                v.wait_ge(sem("score_ready"), 1)
                v.wait_ge(sem("lt_set"), 1 + NH)
                lt = view(gflat, 0, NH, N)
                jk = view(gflat, 2 * N, 2, NH, 2, N)
                for e in range(E1):
                    if e >= 2:
                        v.wait_ge(sem("rank_taken"), e - 1)
                    v.wait_ge(sem("srow_done"), e + 1)
                    for h in range(NH):
                        row = ps[:, e % 4, 0:N]
                        ts(jk[:, e % 2, h, 0, :], row, sc1[:, h, e:e + 1], None, ALU.is_gt, ALU.add,
                           accum_out=cnt[:, 0, h, e:e + 1])
                        last = stt(jk[:, e % 2, h, 1, :], row, sc1[:, h, e:e + 1], lt[:, h, :], ALU.is_equal, ALU.mult,
                                   accum_out=cnt[:, 1, h, e:e + 1])
                    last.then_inc(sem("rank_taken"), 1)
                v.wait_ge(sem("rank_taken"), E1)
                link(tt(cnt[:, 2, :, :], cnt[:, 0, :, :], cnt[:, 1, :, :], ALU.add))
                p1 = view(qflat, 0, NH, E1, SLOTS)
                for h in range(NH):
                    last = tt(p1[:, h, :, :], iota[:, 0:SLOTS].unsqueeze(1).to_broadcast([P, E1, SLOTS]),
                              cnt[:, 2, h, :].unsqueeze(2).to_broadcast([P, E1, SLOTS]), ALU.is_equal)
                last.then_inc(sem("onehot1_ready"), 1)
                for k in range(1, KD, 2):
                    v.wait_ge(sem("xsel_done"), k + 1)
                    copy(xsel[:, k, :], ps[:, k % 2, :]).then_inc(sem("xsel_odd"), 1)
                for h in range(NH):
                    last = tt(p1[:, h, :, :], p1[:, h, :, :],
                              sc1[:, h, :].unsqueeze(2).to_broadcast([P, E1, SLOTS]), ALU.mult)
                last.then_inc(sem("pw_ready"), 1)
                hs = [view(scratch, 6656 + p * N, N) for p in range(4)]
                sg = [view(scratch, 7680 + p * N, N) for p in range(2)]
                for f in range(SH_FT):
                    v.wait_ge(sem("sh_silu"), f + 1)
                    tt(hs[f % 4], sg[f % 2], ps[:, f % 4, N:2 * N], ALU.mult).then_inc(sem("sh_act"), 1)
                with v.Fori(0, E1) as i:
                    for gi in range(GROUPS):
                        v.wait_ge(sem("e1_silu"), i * GROUPS + (gi + 1))
                        tt(e_h, e_silu, ps[:, 0, P:2 * P], ALU.mult).then_inc(sem("e1_act"), 1)
                    ul = U_E1 + 2 * GROUPS - 1
                    v.wait_ge(sem(f"slot{ul % RING}_used"), i * (2 * GROUPS // RING) + (ul // RING + 1))
                    copy(e_y.rearrange("p (a b) -> p a b", a=2), ps[:, 2:4, 0:HD]).then_inc(sem("y1_ready"), 1)
                v.wait_ge(sem("combined"), E1)
                residual()

            if STAGES >= 5:
                gat(1, 4)

            def route(sname, mname, ename, wname, keep, before):
                v.wait_ge(sem(sname), 1)
                link(copy(rt[:, 0, :, :].rearrange("p a b -> p (a b)"), ps[:, 3, 0:NH * E2]))
                link(red(rsm[:, 1, :], rt[:, 0, :, :], AX.X, ALU.max))
                ts(rsm[:, 0, :], rsm[:, 1, :], -1.0, None, ALU.mult).then_inc(sem(mname), 1)
                v.wait_ge(sem(ename), 1)

                def mask(src):
                    for h in range(NH):
                        a = src[:, h, :].unsqueeze(1).to_broadcast([P, E2, E2])
                        b = src[:, h, :].unsqueeze(2).to_broadcast([P, E2, E2])
                        tt(rk[:, 0, h, :, :], a, b, ALU.is_gt)
                        last = tt(rk[:, 1, h, :, :], a, b, ALU.is_equal)
                    link(last)
                    for h in range(NH):
                        last = tt(rk[:, 1, h, :, :], rk[:, 1, h, :, :], low[:, :, :], ALU.mult)
                    link(last)
                    link(tt(rk[:, 0, :, :, :], rk[:, 0, :, :, :], rk[:, 1, :, :, :], ALU.add))
                    link(red(rt[:, 2, :, :], rk[:, 0, :, :, :].rearrange("p h a b -> p (h a) b"), AX.X, ALU.add))
                    link(ts(rt[:, 2, :, :], rt[:, 2, :, :], float(keep), None, ALU.is_lt))

                v.wait_ge(sem("low_set"), 1)
                if before:
                    mask(rt[:, 0, :, :])
                    link(tt(rt[:, 1, :, :], rt[:, 1, :, :], rt[:, 2, :, :], ALU.mult))
                link(red(rsm[:, 2, :], rt[:, 1, :, :], AX.X, ALU.add))
                link(nc.vector.reciprocal(rsm[:, 3, :], rsm[:, 2, :]))
                last = tt(rt[:, 5, :, :], rt[:, 1, :, :], rsm[:, 3, :].unsqueeze(2).to_broadcast([P, NH, E2]), ALU.mult)
                if before:
                    last.then_inc(sem(wname), 1)
                    v.wait_ge(sem(wname), 1)
                else:
                    link(last)
                    mask(rt[:, 5, :, :])
                    tt(rt[:, 5, :, :], rt[:, 5, :, :], rt[:, 2, :, :], ALU.mult).then_inc(sem(wname), 1)
                    v.wait_ge(sem(wname), 1)

            def dense(tag, u0, experts, unroll, upe):
                v.sem_inc(sem(f"{tag}_yfree"), 1)
                with v.Fori(0, experts // unroll) as i:
                    for q in range(unroll):
                        ul = u0 + (q + 1) * upe - 1
                        v.wait_ge(sem(f"slot{ul % RING}_used"), i * (unroll * upe // RING) + (ul // RING + 1))
                        for h in range(NH):
                            last = stt(halves(x, h), nat(h), rt[:, 5, h, bass.ds(i * unroll + q, 1)], halves(x, h),
                                       ALU.mult, ALU.add)
                        last.then_inc(sem(f"{tag}_yfree"), 1)
                        v.wait_ge(sem(f"{tag}_yfree"), i * unroll + (q + 2))

            if STAGES >= 6:
                layernorm(5)
                route("score2_done", "max2_ready", "exp2", "w2_ready", 2, True)
                v.wait_ge(sem("w2T_done"), 1)
                copy(wT8[:, :], ps[0:E2, 2, 0:N]).then_inc(sem("w2T_ready"), 1)
                v.wait_ge(sem("pos_done"), 1)
                link(stt(rt[:, 3, :, :].rearrange("p a b -> p (a b)"), rt[:, 2, :, :].rearrange("p a b -> p (a b)"),
                         -1024.0, ps[:, 3, 0:NH * E2], ALU.mult, ALU.add))
                link(ts(rt[:, 3, :, :], rt[:, 3, :, :], 1024.0, None, ALU.add))
                link(ts(rt[:, 4, :, :], rt[:, 3, :, :], -float(CAP2), None, ALU.add))
                link(red(rsm[:, 0, 0:1], ps[:, 3, NH * E2:(NH + 1) * E2], AX.X, ALU.max))
                copy(over[:, 0:1], rsm[:, 0, 0:1]).then_inc(sem("over_ready"), 1)

                def experts2(t, link):
                    q = rt[:, 4 if t else 3, :, :]
                    if t:
                        nc.vector.memset(wT8[:, :], 0.0).then_inc(sem("w2T_ready" + t), 1)
                    for h in range(NH):
                        last = tt(p2[:, h, :, :], iota[:, 0:CAP2].unsqueeze(1).to_broadcast([P, E2, CAP2]),
                                  q[:, h, :].unsqueeze(2).to_broadcast([P, E2, CAP2]), ALU.is_equal)
                    last.then_inc(sem("onehot2_ready" + t), 1)
                    for k in range(KD):
                        v.wait_ge(sem("xsel2_done" + t), 2 * k + 2)
                        copy(xsel2c[:, k, 1, :], ps[:, 1, :]).then_inc(sem("xsel2_v" + t), 1)
                    for h in range(NH):
                        last = tt(p2[:, h, :, :], p2[:, h, :, :],
                                  rt[:, 5, h, :].unsqueeze(2).to_broadcast([P, E2, CAP2]), ALU.mult)
                    last.then_inc(sem("pw2_ready" + t), 1)
                    with v.Fori(0, E2) as i:
                        v.wait_ge(sem("y2_first" + t), i + 1)
                        copy(y2[:, 0:HD], ps[:, 2, 0:HD]).then_inc(sem("y2_ready" + t), 1)
                        ul = U_E2 + UPE2 - 1
                        if t:
                            v.wait_ge(sem("ovw_used"), i * UPE2 + (UPE2 + 1))
                        else:
                            v.wait_ge(sem(f"slot{ul % RING}_used"), i * (UPE2 // RING) + (ul // RING + 1))
                        copy(y2[:, HD:D], ps[:, 3, 0:HD]).then_inc(sem("y2_ready" + t), 1)
                    v.wait_ge(sem("combined2" + t), E2)
                    for h in range(NH):
                        last = tt(halves(x, h), nat(h), halves(x, h), ALU.add)
                    link(last)

                experts2("", link)
                overflow(v, lambda: experts2("_ov", Chain(v, sem("dve_own_ov"))))
            if STAGES >= 7:
                layernorm(6)
                unit_done(v, U_L3G)
                residual()
            if STAGES >= 8:
                layernorm(7)
                route("score3_done", "max3_ready", "exp3", "w3_ready", 1, False)
                dense("e3", U_E3, E3, 4, 1)
            nc.vector.memset(rsm[:, :, :], 0.0).then_inc(sem("result"), 1)


def kernel(**inputs):
    import numpy as np
    import concourse.bacc as bacc
    from concourse.bass_utils import run_bass_kernel_spmd

    a = {k: np.asarray(v) for k, v in inputs.items()}

    def rows(w):
        return w.reshape(KD, P, -1).transpose(1, 0, 2).reshape(P, -1)

    def cols(b):
        return b.reshape(-1, P).T

    def twice(w):
        return np.concatenate([w.T, w.T])

    weights = np.empty((UNITS, P, UW), np.float32)

    def put(u, w):
        weights[u] = rows(w)

    wg, wq = a["L0_gnn_Wg"], a["L0_gnn_Wq"]
    put(U_QG, wg[:, D:].T)
    for r, (ur, ug) in enumerate(((U_RG1, U_GT1), (U_RG2, U_GT2))):
        put(ur, a[f"L0_gnn_W_root{r + 1}"])
        for rel in range(REL):
            put(ur + 1 + rel, a[f"L0_gnn_W_rel{r + 1}"][rel])
        put(ug, wg[:, :D].T)
        put(ug + 1, wq[:, :D].T)
        put(ug + 2, wq[:, D:].T)
    put(U_FF0, a["L0_ffn_weight"].T)

    def up_blocks(w, f):
        return w.reshape(w.shape[0], -1, f, P, KD, P).transpose(0, 1, 5, 2, 4, 3)

    def down_blocks(w, f):
        return w.reshape(w.shape[0], KD, P, -1, f, P).transpose(0, 3, 5, 4, 1, 2)

    def gated(u, wg, wu, wd):
        o = weights[u:u + wg.shape[0] * wg.shape[1] // (2 * P)].reshape(wg.shape[0], -1, P, 2, 18, P)
        o[:, :, :, :, 0:6] = up_blocks(wg, 2)
        o[:, :, :, :, 6:12] = up_blocks(wu, 2)
        o[:, :, :, :, 12:18] = down_blocks(wd, 2)

    gated(U_SH, a["L1_ffn_Ws_g"][None], a["L1_ffn_Ws_u"][None], a["L1_ffn_Ws_d"][None])
    o = weights[U_E1:U_R2].reshape(E1, FT1 // 4, 2, P, UB, P)
    for i, w in enumerate((a["L1_ffn_Wg"], a["L1_ffn_Wu"])):
        o[:, :, :, :, 0:24].reshape(E1, FT1 // 4, 2, P, 3, 4, 2, P)[..., i, :] = \
            w.reshape(E1, FT1 // 4, 4, P, 2, 3, P).transpose(0, 1, 4, 6, 5, 2, 3)
    o[:, :, :, :, 24:36] = a["L1_ffn_Wd"].reshape(E1, KD, P, FT1 // 4, 2, 2, P).transpose(0, 3, 4, 6, 5, 1, 2
        ).reshape(E1, FT1 // 4, 2, P, 12, P)
    put(U_R2, a["L2_ffn_Wr1"].T)
    o = weights[U_E2:U_L3G].reshape(E2, -1, P, 3, 12, P)
    o[:, :, :, :, 0:6] = up_blocks(a["L2_ffn_W1"], 3)
    o[:, :, :, :, 6:12] = down_blocks(a["L2_ffn_W2"], 3)
    put(U_L3G, a["L3_gnn_W"])
    o = weights[U_E3:UNITS].reshape(E3, 1, P, 3, 12, P)
    o[:, :, :, :, 0:6] = up_blocks(a["L3_ffn_wi"].transpose(0, 2, 1), 3)
    o[:, :, :, :, 6:12] = down_blocks(a["L3_ffn_wo"].transpose(0, 2, 1), 3)

    small = np.concatenate([
        cols(a["L0_gnn_b1"]), cols(a["L0_gnn_b2"]), cols(a["L0_gnn_bg"]), cols(a["L0_gnn_bq"]),
        cols(a["L2_ffn_br1"]), cols(a["L2_ffn_b1"].reshape(-1)),
        rows(a["L1_ffn_gate_weight"].T), rows(a["L2_ffn_Wr2"].T), rows(a["L3_ffn_router_w"]),
        twice(a["L1_gnn_W_fc"]), twice(a["L1_gnn_W_res"]), cols(a["L1_gnn_attn_l"].reshape(-1)),
        cols(a["L1_gnn_attn_r"].reshape(-1)),
        twice(a["L2_gnn_W"]), twice(a["L2_gnn_W_res"]), cols(a["L2_gnn_attn_l"].reshape(-1)),
        cols(a["L2_gnn_attn_r"].reshape(-1))], axis=1)
    arrays = {
        "weights": weights[:STAGE_UNITS[STAGES - 1]],
        "small": small,
        "edges": np.stack([a["src"], a["dst"], a["edge_type_3"]]).reshape(3, P, EC).transpose(1, 0, 2),
        "x": a["x"].reshape(NH, P, D).transpose(1, 0, 2),
        "qT": a["L0_gnn_query_embs"].reshape(B * L, KD, P).transpose(2, 1, 0),
        "rows8": a["L2_ffn_b2"],
        "row1": np.concatenate([a["L3_gnn_b"], a["L2_ffn_br2"]])[None],
    }
    nc = bacc.Bacc("TRN2", target_bir_lowering=False, num_devices=1)
    arrays = {f"in_{k}": np.ascontiguousarray(v) for k, v in arrays.items()}
    aps = [nc.dram_tensor(k, v.shape, mybir.dt.from_np(v.dtype), kind="ExternalInput").ap() for k, v in arrays.items()]
    out = nc.dram_tensor("out", (P, NH, D), F32, kind="ExternalOutput").ap()
    build(nc, *aps, out)
    r = run_bass_kernel_spmd(nc, [arrays], core_ids=[0])
    return r.results[0]["out"].transpose(1, 0, 2).reshape(N, D)
```

```python
from contextlib import ExitStack

import concourse.bass as bass
from concourse import mybir

ALU = mybir.AluOpType
ACT = mybir.ActivationFunctionType
AX = mybir.AxisListType
F32 = mybir.dt.float32
BF16 = mybir.dt.bfloat16
I32 = mybir.dt.int32

P = 128
N = 256
NH = N // P
D = 768
KD = D // P
HD = D // 2
EDGES = 4352
EC = EDGES // P
REL = 3
B, NB, L = 8, 32, 64
HEADS, HE = 12, 64
HG = 3
E1, SLOTS, FT1 = 16, 32, 24
E2, FT2 = 8, 24
CAP2 = P
E3, FT3 = 8, 3
CAP3 = P // 2
SH_FT = 12
SH_EARLY = 4
MIX = E1 // 2 - 1
SH_UNITS = (SH_FT - SH_EARLY) // 2
UB = 36
UW = UB * P
RING = 4
EPS = 1e-5
FAR = -1e30

U_QG = 0
U_RG1 = 1
U_GT1 = U_RG1 + 4
U_RG2 = U_GT1 + 3
U_GT2 = U_RG2 + 4
U_FF0 = U_GT2 + 3
U_SH = U_FF0 + 1
U_E1 = U_SH + SH_EARLY // 2
U_R2 = U_E1 + E1 * FT1 // 2 + SH_UNITS
U_E2 = U_R2 + 1
U_L3G = U_E2 + E2 * FT2 // 3
U_E3 = U_L3G + 1
UNITS = U_E3 + E3
GROUPS = FT1 // 4


def pair_unit(e, g):
    return U_E1 + 2 * (e * GROUPS + g) + (min(g, SH_UNITS) if e == MIX else SH_UNITS if e > MIX else 0)


def shared_unit(f):
    return U_SH + f // 2 if f < SH_EARLY else pair_unit(MIX, (f - SH_EARLY) // 2) + 2


SMALL = {}
_at = 0
for _n, _w in (("b1", KD), ("b2", KD), ("bg", KD), ("bq", KD), ("br1", KD), ("fb1", E2 * FT2),
               ("gate", KD * E1), ("wr2", KD * E2), ("rw", KD * E3),
               ("fc1", HE), ("res1", HE), ("al1", KD), ("ar1", KD),
               ("fc2", HE), ("res2", HE), ("al2", KD), ("ar2", KD)):
    SMALL[_n] = (_at, _w)
    _at += _w
SMALL_W = _at


class Chain:

    def __init__(self, eng, sem):
        self.eng, self.sem, self.count, self.past = eng, sem, 0, 0

    def __call__(self, ins):
        self.count += 1
        ins.then_inc(self.sem, 1)
        self.eng.wait_ge(self.sem, self.past + self.count)
        return ins

    def enter(self, i, steps):
        self.first, self.steps = self.count, steps
        self.past = i * steps

    def leave(self, trips):
        assert self.count - self.first == self.steps, (self.count - self.first, self.steps)
        self.count += self.steps * (trips - 1)
        self.past = 0


def build(nc, weights, small, edges, xin, qT, rows8, row1, out):
    ctx = ExitStack()
    with ctx:
        sems = {}

        def sem(name):
            if name not in sems:
                sems[name] = ctx.enter_context(nc.semaphore(name))
            return sems[name]

        def sb(name, shape, dt=F32):
            return ctx.enter_context(nc.sbuf_tensor(name, shape, dt))

        ps = ctx.enter_context(nc.psum_tensor("ps", [P, 8, 512], F32))
        ring = sb("ring", [P, RING, UW])
        x = sb("x", [P, NH, D])
        xn = sb("xn", [P, NH, D])
        xT = sb("xT", [P, KD, N])
        adj = sb("adj", [P, NH, REL * N])
        cT = sb("cT", [P, NH, N])
        cN = sb("cN", [P, NH, N])
        far = sb("far", [P, NH, N])
        gcn = sb("gcn", [P, NH, N])
        scratch = sb("scratch", [P, 8192])
        qTs = sb("qTs", [P, KD, B * L])
        gate_in = sb("gate_in", [P, KD * B * L + KD * N])
        qgT = gate_in[:, 0:KD * B * L].rearrange("p (a b) -> p a b", a=KD)
        hgT = gate_in[:, KD * B * L:].rearrange("p (a b) -> p a b", a=KD)
        hT = sb("hT", [P, KD, N])
        qiT = sb("qiT", [P, KD, N])
        iota = sb("iota", [P, REL * N])
        iota16 = sb("iota16", [P, REL * N], mybir.dt.float16)
        ident = sb("ident", [P, P])
        ones = sb("ones", [P, P])
        sm = sb("sm", [P, SMALL_W])
        edi = sb("edi", [P, 3, EC], I32)
        edf = sb("edf", [P, 4, EC])
        b2r = sb("b2r", [E2, D])
        rw1 = sb("rw1", [1, D + E2])
        epst = sb("epst", [P, 1])
        bnst = sb("bnst", [P, NH, 2, 6])
        mv = sb("mv", [P, NH, 2])
        sd = sb("sd", [P, NH])
        rs = sb("rs", [P, NH])
        deg = sb("deg", [P, NH])
        dis = sb("dis", [P, NH])
        low = sb("low", [P, E2, E2])
        a2 = sb("a2", [P, NH, HEADS])
        hm = sb("hm", [P, 2, 4, HG, NH])
        rden = sb("rden", [P, NH, HEADS])
        sc1 = sb("sc1", [P, NH, E1])
        cnt = sb("cnt", [P, 3, NH, E1])
        rk = sb("rk", [P, 2, NH, E2, E2])
        rt = sb("rt", [P, 6, NH, E2])
        rsm = sb("rsm", [P, 4, NH])
        wT8 = sb("wT8", [E2, N])
        tri = sb("tri", [P, P])
        over = sb("over", [P, 2], I32)
        ovw = gate_in

        def S(name):
            a, w = SMALL[name]
            return sm[:, a:a + w]

        def view(t, off, *shape):
            n = 1
            for s in shape:
                n *= s
            f = t[:, off:off + n]
            if len(shape) == 1:
                return f
            names = "abcd"[:len(shape)]
            return f.rearrange(f"p ({' '.join(names)}) -> p {' '.join(names)}", **dict(zip(names[1:], shape[1:])))

        qflat = qTs[:, :, :].rearrange("p a b -> p (a b)")
        gflat = gate_in[:, 0:KD * B * L]

        def turned(n):
            return n + 1 - (n >= 6)

        def nat(h):
            return ps[:, 4 + 2 * h:6 + 2 * h, 0:HD]

        def halves(t, h):
            return t[:, h, :].rearrange("p (a b) -> p a b", a=2)

        def feat(bank):
            return ps[:, bank:bank + 3, :].rearrange("p a (b n) -> p (a b) n", b=2)

        def unit(u):
            return ring[:, u % RING, :]

        def unit_done(eng, u):
            eng.wait_ge(sem(f"slot{u % RING}_used"), u // RING + 1)

        def att(gi):
            return view(scratch, gi * HG * NH * N, HG, NH, N)

        def att_T(h):
            return view(scratch, (HEADS + h % 2) * NH * N, NH, N)

        bd = view(gflat, 0, 2, P)
        al = view(gflat, 2 * P, KD, 2)
        ar = view(gflat, 2 * P + 2 * KD, KD, 2)
        ft1 = view(gflat, 2 * P + 4 * KD, NH, HEADS, HE + 1)

        xsel2 = view(scratch, 0, KD, E2 * CAP2)
        xsel2c = view(scratch, 0, KD, 2, E2 * CAP2 // 2)
        o = KD * E2 * CAP2
        mid2 = [view(scratch, o + p * CAP2, CAP2) for p in range(2)]
        pe_in2 = view(scratch, o + 2 * CAP2, NH, CAP2)
        pwe2 = view(scratch, o + 2 * CAP2 + NH * CAP2, N)
        y2 = view(scratch, o + 2 * CAP2 + NH * CAP2 + N, D)
        assert o + 2 * CAP2 + NH * CAP2 + N + D <= 8192
        p2 = view(qflat, 0, NH, E2, CAP2)
        p2f = view(qflat, 0, NH, E2 * CAP2)
        UPE2 = FT2 // 3

        def overflow(eng, body):
            eng.wait_ge(sem("most_ready"), 1)
            most = eng.value_load(over[0:1, 0:1], min_val=0, max_val=N)
            with eng.If(most > CAP2):
                body()

        PAIRS = E3 // 2
        xsel3 = view(scratch, 0, KD, E3 * CAP3)
        o = KD * E3 * CAP3
        h3 = [view(scratch, o + p * FT3 * P, FT3 * P) for p in range(2)]
        h3T = view(scratch, o + 2 * FT3 * P, FT3, P)
        y3 = view(scratch, o + 3 * FT3 * P, D)
        pw3T = view(scratch, o + 3 * FT3 * P + D, PAIRS, N)
        assert o + 3 * FT3 * P + D + PAIRS * N <= 8192
        p3 = view(qflat, 0, NH, E3, CAP3)
        p3f = view(qflat, 0, NH, E3 * CAP3)

        def either(eng, sparse, dense):
            eng.wait_ge(sem("most_ready"), 2)
            most = eng.value_load(over[0:1, 1:2], min_val=0, max_val=N)
            with eng.If(most > CAP3):
                dense()
            with eng.If(most <= CAP3):
                sparse()

        xsel = view(scratch, 0, KD, E1 * SLOTS)
        p1f = view(qflat, 0, NH, E1 * SLOTS)
        o = KD * E1 * SLOTS
        xe = [view(scratch, o + p * KD * SLOTS, KD, SLOTS) for p in range(2)]
        o += 2 * KD * SLOTS
        pe_in = [view(scratch, o + p * NH * P, NH, 4, SLOTS) for p in range(2)]
        o += 2 * NH * P
        pwe = view(scratch, o, N)
        e_silu = view(scratch, o + N, P)
        e_h = view(scratch, o + N + P, P)
        e_hT = view(scratch, o + N + 2 * P, P)
        e_y = view(scratch, o + N + 3 * P, D)
        assert o + N + 3 * P + D <= 6656

        LC = 8
        BLOCK_CH = L // LC
        BODY_CH = 2 * BLOCK_CH
        GATE_CH = KD * BLOCK_CH
        BUFS = 4

        def chunk(j):
            return view(scratch, (j % BUFS) * LC * N, LC, B, NB)

        def paired(j):
            return 1 + j % 2

        th = view(scratch, 0, KD, N)

        def node_rows(t, i, j, r0, r1):
            return t[:, bass.ds(i * 2 + j // BLOCK_CH, 1), :].rearrange("p o (b n) -> p (o b) n", b=B) \
                .unsqueeze(1).to_broadcast([P, r1 - r0, B, NB])

        def query_rows(t, i, j, r0, r1):
            l = (j % BLOCK_CH) * LC
            return t[:, bass.ds(i * 2 + j // BLOCK_CH, 1), :].rearrange("p o (b l) -> p l (o b)", b=B) \
                [:, l + r0:l + r1, :].unsqueeze(3).to_broadcast([P, r1 - r0, B, NB])

        def onehots(c):
            b = scratch[:, 0:2048].bitcast(BF16)
            o = (c % 4) * 1024
            return b[:, o:o + N], b[:, o + N:o + N + REL * N]

        block = ctx.enter_context(nc.Block())

        @block.sync
        def _(sp):
            sp.dma_start(edi[:, :, :], edges).then_inc(sem("edges_in"), 16)
            sp.dma_start(x[:, :, :], xin).then_inc(sem("x_in"), 16)
            sp.dma_start(sm[:, :], small).then_inc(sem("small_in"), 16)
            sp.dma_start(qTs[:, :, :], qT).then_inc(sem("q_in"), 16)
            sp.dma_start(b2r[:, :], rows8).then_inc(sem("rows_in"), 16)
            sp.dma_start(rw1[:, :], row1).then_inc(sem("rows_in"), 16)
            for s in range(RING):
                sp.dma_start(ring[:, s, :], weights[s]).then_inc(sem(f"slot{s}_full"), 16)
            rounds, rest = divmod(UNITS, RING)
            with sp.Fori(1, rounds) as r:
                for s in range(RING):
                    sp.wait_ge(sem(f"slot{s}_used"), r)
                    sp.dma_start(ring[:, s, :], weights[bass.ds(r * RING + s, 1)].rearrange("o p n -> (o p) n")
                                 ).then_inc(sem(f"slot{s}_full"), 16)
            for s in range(rest):
                sp.wait_ge(sem(f"slot{s}_used"), rounds)
                sp.dma_start(ring[:, s, :], weights[rounds * RING + s]).then_inc(sem(f"slot{s}_full"), 16)
            sp.wait_ge(sem("result"), 1)
            sp.dma_start(out, x[:, :, :]).then_inc(sem("stored"), 16)
            sp.wait_ge(sem("stored"), 16)

        @block.gpsimd
        def _(g):
            g.iota(iota[:, :], [[1, REL * N]], base=0, channel_multiplier=0,
                   allow_small_or_imprecise_dtypes=True).then_inc(sem("iota_set"), 1)
            g.memset(ident[:, :], 0.0).then_inc(sem("pool_set"), 1)
            g.memset(ones[:, :], 1.0).then_inc(sem("ones_set"), 1)
            g.memset(epst[:, :], EPS).then_inc(sem("ones_set"), 1)
            g.memset(low[:, :, :], 0.0).then_inc(sem("pool_set"), 1)
            g.memset(tri[:, :], 1.0).then_inc(sem("pool_set"), 1)
            g.wait_ge(sem("pool_set"), 3)
            g.affine_select(out=ident[:, :], in_=ident[:, :], compare_op=ALU.not_equal, fill=1.0, base=0,
                            pattern=[[-1, P]], channel_multiplier=1).then_inc(sem("ident_set"), 1)
            g.affine_select(out=low[:, :, :], in_=low[:, :, :], compare_op=ALU.is_ge, fill=1.0, base=0,
                            pattern=[[-1, E2], [1, E2]], channel_multiplier=0).then_inc(sem("low_tri_set"), 1)
            g.affine_select(out=tri[:, :], in_=tri[:, :], compare_op=ALU.is_gt, fill=0.0, base=0,
                            pattern=[[1, P]], channel_multiplier=-1).then_inc(sem("low_tri_set"), 1)

            for gate in range(2):
                g.wait_ge(sem("hg_ready"), gate + 1)
                g.wait_ge(sem("qg_ready"), KD)
                with g.Fori(0, GATE_CH // BODY_CH) as i:
                    for j in range(BODY_CH):
                        g.wait_ge(sem("gate_free"), i * BODY_CH + (GATE_CH * gate + j + 1))
                        g.tensor_tensor(chunk(j)[:, 1:LC, :, :], node_rows(hgT, i, j, 1, LC),
                                        query_rows(qgT, i, j, 1, LC), ALU.add).then_inc(sem("gate_sum"), 1)

            def gat(n):
                for gi in range(HEADS // HG):
                    g.wait_ge(sem("att_exp"), n * (HEADS // HG) + gi + 1)
                    g.tensor_tensor(att(gi), att(gi), cN[:, :, :].unsqueeze(1).to_broadcast([P, HG, NH, N]),
                                    ALU.mult).then_inc(sem("att_ready"), 1)

            gat(0)

            lt = view(gflat, 0, NH, N)
            g.wait_ge(sem("ln_Tv"), 4)
            g.memset(lt, 1.0).then_inc(sem("lt_set"), 1)
            g.wait_ge(sem("lt_set"), 1)
            for h in range(NH):
                g.affine_select(out=lt[:, h, :], in_=lt[:, h, :], compare_op=ALU.is_gt, fill=0.0, base=h * P,
                                pattern=[[-1, N]], channel_multiplier=1).then_inc(sem("lt_set"), 1)
            g.wait_ge(sem("xsel_odd"), KD // 2)
            g.wait_ge(sem("xsel_even"), KD // 2)
            g.wait_ge(sem("pw_ready"), 1)

            def stage_expert(e, par):
                g.tensor_copy(xe[par], xsel[:, :, bass.ds(e * SLOTS, SLOTS)])
                for h in range(NH):
                    last = g.tensor_copy(pe_in[par][:, h, :, :], p1f[:, h, bass.ds(e * SLOTS, SLOTS)].unsqueeze(1)
                                         .to_broadcast([P, 4, SLOTS]))
                last.then_inc(sem("xe_ready"), 1)

            for par in range(2):
                stage_expert(par, par)
            with g.Fori(1, E1 // 2) as i:
                for par in range(2):
                    g.wait_ge(sem("y1_ready"), i * 2 + (par - 1))
                    stage_expert(i * 2 + par, par)

            gat(1)

            def experts2(t):
                g.wait_ge(sem("pw2_ready" + t), 1)
                g.tensor_copy(pe_in2, p2f[:, :, 0:CAP2]).then_inc(sem("stage2" + t), 1)
                if t:
                    fetch2(0)
                with g.Fori(1, E2) as i:
                    g.wait_ge(sem("turn2" + t), i)
                    g.tensor_copy(pe_in2, p2f[:, :, bass.ds(i * CAP2, CAP2)]).then_inc(sem("stage2" + t), 1)
                    if t:
                        fetch2(i)

            def fetch2(e):
                for U in range(UPE2):
                    g.wait_ge(sem("ovw_used"), e * UPE2 + (U + 1))
                    src = weights[U_E2 + U] if isinstance(e, int) else \
                        weights[bass.ds(e * UPE2 + (U_E2 + U), 1)].rearrange("o p n -> (o p) n")
                    g.dma_start(ovw[:, :], src).then_inc(sem("ovw_full"), 16)

            experts2("")
            overflow(g, lambda: experts2("_ov"))

        @block.tensor
        def _(pe):
            mm = nc.tensor.matmul

            def arrived(u):
                pe.wait_ge(sem(f"slot{u % RING}_full"), 16 * (u // RING + 1))

            def used(u, last):
                last.then_inc(sem(f"slot{u % RING}_used"), 1)

            def product_T(u, bank, act, start, stop):
                w = unit(u)
                arrived(u)
                for n in range(KD):
                    for k in range(KD):
                        last = mm(feat(bank)[:, n, :], w[:, k * D + n * P:k * D + (n + 1) * P], act[:, k, :],
                                  start=start and k == 0 and n % 2 == 0, stop=stop and k == KD - 1,
                                  skip_group_check=True)
                used(u, last)
                return last

            def product_N(w, act, bias=None):
                for h in range(NH):
                    for j in range(2):
                        o = ps[:, 4 + 2 * h + j, 0:HD]
                        for k in range(KD):
                            last = mm(o, act[:, k, h * P:(h + 1) * P], w[:, k * D + j * HD:k * D + (j + 1) * HD],
                                      start=k == 0, stop=k == KD - 1 and bias is None)
                        if bias is not None:
                            last = mm(o, ones[0:1, :], bias[:, j * HD:(j + 1) * HD], start=False, stop=True)
                return last

            def layernorm_T(n):
                for h in range(NH):
                    pe.wait_ge(sem("ln_xn"), NH * n + h + 1)
                    for k in range(KD):
                        last = nc.tensor.transpose(feat(0)[:, k, h * P:(h + 1) * P],
                                                   xn[:, h, k * P:(k + 1) * P], ident[:, :])
                last.then_inc(sem("ln_tp"), 1)

            def normalised(n):
                pe.wait_ge(sem("ln_Ta"), turned(n))
                pe.wait_ge(sem("ln_Tv"), turned(n))

            pe.wait_ge(sem("ident_set"), 1)
            pe.wait_ge(sem("ones_set"), 2)

            def query_gate(n):
                if n == 0:
                    pe.wait_ge(sem("q_in"), 16)
                    arrived(U_QG)
                w = unit(U_QG)
                if n >= 4:
                    pe.wait_ge(sem("qg_ready"), n - 3)
                for k in range(KD):
                    last = mm(ps[:, 4 + n % 4, :], w[:, k * D + n * P:k * D + (n + 1) * P], qTs[:, k, :],
                              start=k == 0, stop=k == KD - 1)
                if n < KD - 1:
                    last.then_inc(sem("qg_done"), 1)
                else:
                    used(U_QG, last)

            def graph():
                for c in range(EC):
                    pe.wait_ge(sem("onehot_ready"), c + 1)
                    s_oh, k_oh = onehots(c)
                    for h in range(NH):
                        mm(ps[:, 2 * h, :], s_oh[:, h * P:(h + 1) * P], k_oh[:, 0:512],
                           start=c == 0, stop=c == EC - 1)
                        last = mm(ps[:, 2 * h + 1, 0:N], s_oh[:, h * P:(h + 1) * P], k_oh[:, 512:768],
                                  start=c == 0, stop=c == EC - 1)
                    last.then_inc(sem("onehot_used"), 1)
                query_gate(0)
                query_gate(1)
                pe.wait_ge(sem("counts_ready"), 1)
                for j in range(2):
                    for h in range(NH):
                        last = mm(ps[:, j, 0:HD], ones[:, :], adj[:, h, j * HD:(j + 1) * HD],
                                  start=h == 0, stop=h == NH - 1)
                last.then_inc(sem("graph_done"), 1)
                query_gate(2)
                query_gate(3)
                pe.wait_ge(sem("counts_ready"), 2)
                for dh in range(NH):
                    for sh in range(NH):
                        last = nc.tensor.transpose(ps[:, 2, dh * N + sh * P:dh * N + (sh + 1) * P],
                                                   cT[:, sh, dh * P:(dh + 1) * P], ident[:, :])
                last.then_inc(sem("graph_done"), 1)
                query_gate(4)
                query_gate(5)
                pe.wait_ge(sem("dis_ready"), 1)
                for h in range(NH):
                    last = nc.tensor.transpose(ps[:, 3, h * P:(h + 1) * P],
                                               dis[:, h:h + 1].to_broadcast([P, P]), ident[:, :])
                last.then_inc(sem("graph_done"), 1)

            def rgcn(r, u0, actN, actT):
                product_T(u0, 4, actT, True, False)
                if r == 0:
                    pe.wait_ge(sem("adj_ready"), 1)
                    pe.wait_ge(sem("gcn_ready"), 1)
                else:
                    pe.wait_ge(sem("hnat_ready"), 1)
                for j in range(KD):
                    if j >= 2:
                        pe.wait_ge(sem("g_copied_a"), KD * r + j - 1)
                        pe.wait_ge(sem("g_copied_v"), KD * r + j - 1)
                    bk = 2 * (j % 2)
                    for h in range(NH):
                        mm(ps[:, bk, :], actN[:, h, j * P:(j + 1) * P], adj[:, h, 0:512],
                           start=h == 0, stop=h == NH - 1)
                    for h in range(NH):
                        last = mm(ps[:, bk + 1, 0:N], actN[:, h, j * P:(j + 1) * P], adj[:, h, 512:768],
                                  start=h == 0, stop=h == NH - 1)
                    last.then_inc(sem("g_done"), 1)
                pe.wait_ge(sem("g_copied_a"), KD * (r + 1))
                pe.wait_ge(sem("g_copied_v"), KD * (r + 1))
                for rel in range(REL):
                    product_T(u0 + 1 + rel, 4, view(scratch, rel * KD * N, KD, N), False, rel == REL - 1)

            def gate(r, u0):
                pe.wait_ge(sem("hT_ready"), r + 1)
                product_T(u0, 0, hT, True, True)
                product_T(u0 + 1, 4, hT, True, False)
                pe.wait_ge(sem("hg_ready"), r + 1)
                if r == 0:
                    pe.sem_inc(sem("gate_free"), BUFS)
                with pe.Fori(0, GATE_CH // BODY_CH) as i:
                    for j in range(BODY_CH):
                        pe.wait_ge(sem("gate_ready"), i * BODY_CH + (GATE_CH * r + j + 1))
                        for l in range(LC - paired(j)):
                            last = mm(ps[:, bass.ds(i, 1), (j // BLOCK_CH) * N:(j // BLOCK_CH + 1) * N], ident[:, :],
                                      chunk(j)[:, l, :, :], start=j == 0 and l == 0,
                                      stop=j % BLOCK_CH == BLOCK_CH - 1 and l == LC - paired(j) - 1,
                                      skip_group_check=True)
                        last.then_inc(sem("gate_free"), 1)
                pe.wait_ge(sem("qi_ready"), r + 1)
                product_T(u0 + 2, 4, qiT, False, True)
                if r:
                    pe.wait_ge(sem("alpha_ready"), 2 * (r + 1))
                for k in range(KD):
                    if k % 3 == 0:
                        pe.wait_ge(sem("hn_ready"), 2 * r + k // 3 + 1)
                    for h in range(NH):
                        last = nc.tensor.transpose(ps[:, 4 * r + 2 * h + k // 3, (k % 3) * P:(k % 3 + 1) * P],
                                                   hT[:, k, h * P:(h + 1) * P], ident[:, :])
                last.then_inc(sem("hn_nat"), 1)

            graph()
            layernorm_T(0)
            normalised(0)
            pe.wait_ge(sem("qg_ready"), KD)
            rgcn(0, U_RG1, xn, xT)
            gate(0, U_GT1)
            rgcn(1, U_RG2, xn, hT)
            gate(1, U_GT2)

            layernorm_T(1)
            arrived(U_FF0)
            normalised(1)
            pe.wait_ge(sem("sign_ready"), 1)
            last = product_N(unit(U_FF0), xT)
            used(U_FF0, last)

            def gat(n, lnidx):
                layernorm_T(lnidx)
                normalised(lnidx)
                pe.wait_ge(sem("gat_w"), n + 1)
                for k in range(KD):
                    last = mm(feat(0)[:, k, :], bd[:, 0, :], xT[:, k, :], start=True, stop=True)
                last.then_inc(sem("ftT_done"), 1)

                def natural(i, s):
                    for h in range(NH):
                        for k in range(KD):
                            last = mm(ps[:, 4 + 2 * h + k // 3, (k % 3) * P:(k % 3 + 1) * P],
                                      xT[:, k, h * P:(h + 1) * P], bd[:, i, :], start=True, stop=True)
                    last.then_inc(sem(f"{s}_done"), 1)

                def rows(gi):
                    for q in range(HG):
                        h = gi * HG + q
                        last = mm(ps[:, q // 2, (q % 2) * N:(q % 2 + 1) * N],
                                  al[:, h // 2, h % 2:h % 2 + 1].to_broadcast([P, P]), hT[:, h // 2, :],
                                  start=True, stop=True)
                    last.then_inc(sem("arow_done"), 1)

                natural(0, "ft")
                pe.wait_ge(sem("ftT_ready"), n + 1)
                for h in range(NH):
                    for k in range(KD):
                        last = mm(ps[:, 3, h * HEADS + 2 * k:h * HEADS + 2 * k + 2], hT[:, k, h * P:(h + 1) * P],
                                  ar[:, k, :], start=True, stop=True)
                last.then_inc(sem("a2_done"), 1)
                rows(0)
                pe.wait_ge(sem("ft_ready"), n + 1)
                natural(1, "res")
                pe.wait_ge(sem("a2_ready"), n + 1)
                pe.wait_ge(sem("res_ready"), n + 1)

                def turn(h):
                    M = n * HEADS + h
                    if h >= 2:
                        pe.wait_ge(sem("wT_ready"), M - 1)
                    for sh in range(NH):
                        for dh in range(NH):
                            last = nc.tensor.transpose(ps[:, 2 + h % 2, sh * N + dh * P:sh * N + (dh + 1) * P],
                                                       att(h // HG)[:, h % HG, dh, sh * P:(sh + 1) * P], ident[:, :])
                    last.then_inc(sem("wT_done"), 1)

                def collect(h):
                    pe.wait_ge(sem("wT_ready"), n * HEADS + h + 1)
                    for dh in range(NH):
                        c = (h % 6) * (HE + 1)
                        for sh in range(NH):
                            last = mm(ps[:, 4 + 2 * dh + h // 6, c:c + HE + 1], att_T(h)[:, sh, dh * P:(dh + 1) * P],
                                      ft1[:, sh, h, :], start=sh == 0, stop=sh == NH - 1)
                    last.then_inc(sem("head_done"), 1)

                for gi in range(1, HEADS // HG):
                    pe.wait_ge(sem("arow_taken"), n * (HEADS // HG) + gi)
                    rows(gi)
                for gi in range(HEADS // HG):
                    G = n * (HEADS // HG) + gi
                    pe.wait_ge(sem("att_ready"), G + 1)
                    h = gi * HG
                    turn(h)
                    for q in range(HG):
                        if q + 1 < HG:
                            turn(h + q + 1)
                        collect(h + q)

            gat(0, 2)

            layernorm_T(3)
            normalised(3)
            for h in range(NH):
                for k in range(KD):
                    last = mm(ps[:, 3, h * E1:(h + 1) * E1], xT[:, k, h * P:(h + 1) * P],
                              S("gate")[:, k * E1:(k + 1) * E1], start=k == 0, stop=k == KD - 1)
            last.then_inc(sem("score_done"), 1)
            pe.wait_ge(sem("score_ready"), 1)
            hs = [view(scratch, 6656 + p * N, N) for p in range(4)]

            def score_row(e):
                if e >= 2:
                    pe.wait_ge(sem("rank_taken"), e - 1)
                for h in range(NH):
                    last = nc.tensor.transpose(ps[:, 2 + e % 2, h * P:(h + 1) * P],
                                               sc1[:, h, e:e + 1].to_broadcast([P, P]), ident[:, :])
                last.then_inc(sem("srow_done"), 1)

            def sh_gu(f, i):
                if f % 2 == 0 and i == 0:
                    arrived(shared_unit(f))
                b = (f % 2) * 18 * P + i * KD * P
                for k in range(KD):
                    last = mm(ps[:, f % 2, i * N:(i + 1) * N], unit(shared_unit(f))[:, b + k * P:b + (k + 1) * P],
                              xT[:, k, :], start=k == 0, stop=k == KD - 1)
                if i:
                    last.then_inc(sem("sh_gu"), 1)

            def sh_down(f, h):
                if h == 0:
                    pe.wait_ge(sem("sh_act"), f + 1)
                b = (f % 2) * 18 * P + 12 * P
                for j in range(2):
                    last = mm(ps[:, 4 + 2 * h + j, 0:HD], hs[f % 4][:, h * P:(h + 1) * P],
                              unit(shared_unit(f))[:, b + j * HD:b + (j + 1) * HD], start=f == 0, stop=f == SH_FT - 1,
                              skip_group_check=True)
                if f % 2 and h == NH - 1:
                    used(shared_unit(f), last)

            for f in range(SH_EARLY):
                for q in range(4):
                    score_row(4 * f + q)
                    if q < 2:
                        sh_gu(f, q)
                    elif f:
                        sh_down(f - 1, q - 2)
            for h in range(NH):
                sh_down(SH_EARLY - 1, h)
            pe.wait_ge(sem("onehot1_ready"), 1)
            p1 = view(qflat, 0, NH, E1 * SLOTS)
            for k in range(KD):
                if k >= 2:
                    pe.wait_ge(sem("xsel_odd" if k % 2 else "xsel_even"), k // 2)
                for h in range(NH):
                    last = mm(ps[:, 2 + k % 2, :], xn[:, h, k * P:(k + 1) * P], p1[:, h, :],
                              start=h == 0, stop=h == NH - 1)
                last.then_inc(sem("xsel_done"), 1)

            BODY = 4 * GROUPS
            assert BODY % RING == 0 and MIX % 2 == 1

            def experts1(i, after, mixed=False):

                def pair_at(par, gi):
                    return pair_unit(0, 0) + 2 * (par * GROUPS + gi) + after + \
                        (min(gi, SH_UNITS) if mixed and par else 0)

                def group(par, gi):
                    done = i * (2 * GROUPS) + (par * GROUPS + gi + 1)
                    for part in range(2):
                        u = pair_at(par, gi) + part
                        pe.wait_ge(sem(f"slot{u % RING}_full"), i * (16 * BODY // RING) + 16 * (u // RING + 1))
                        for kk in range(3):
                            for j in range(4):
                                b = (kk * 4 + j) * 2 * P
                                last = mm(ps[32 * j:32 * j + 32, 0, 0:2 * P], xe[par][:, 3 * part + kk, :],
                                          ring[:, u % RING, b:b + 2 * P], start=part == 0 and kk == 0,
                                          stop=part == 1 and kk == 2)
                    last.then_inc(sem("e1_gu"), 1)
                    pe.wait_ge(sem("e1_act"), done)
                    nc.tensor.transpose(ps[:, 1, 0:P], e_h, ident[:, :]).then_inc(sem("e1_turn"), 1)
                    pe.wait_ge(sem("e1_hT"), done)
                    for c in range(2):
                        for j in range(4):
                            u = pair_at(par, gi) + j // 2
                            b = (24 + (j % 2) * KD) * P + c * HD
                            last = mm(ps[32 * j:32 * j + 32, 2 + c, 0:HD], e_hT[:, 32 * j:32 * j + 32],
                                      ring[:, u % RING, b:b + HD], start=gi == 0, stop=gi == GROUPS - 1)
                            if c and j % 2:
                                last.then_inc(sem(f"slot{u % RING}_used"), 1)

                for par in range(2):
                    e = i * 2 + par
                    pe.wait_ge(sem("xe_ready"), e + 1)
                    for h in range(NH):
                        last = nc.tensor.transpose(ps[:, 1, (h + 1) * P:(h + 2) * P],
                                                   pe_in[par][:, h, :, :].rearrange("p a b -> p (a b)"),
                                                   ident[:, :])
                    last.then_inc(sem("pwe_turn"), 1)
                    for gi in range(GROUPS):
                        group(par, gi)
                        if mixed and par and gi < SH_UNITS:
                            pe.wait_ge(sem("pwe_ready"), e + 1)
                            f = SH_EARLY + 2 * gi
                            for q in range(2):
                                sh_gu(f + q, 0)
                                sh_gu(f + q, 1)
                            for q in range(2):
                                for h in range(NH):
                                    sh_down(f + q, h)
                    pe.wait_ge(sem("pwe_ready"), e + 1)
                    pe.wait_ge(sem("y1_ready"), e + 1)
                    for h in range(NH):
                        for c in range(2):
                            last = mm(ps[:, 4 + 2 * h + c, 0:HD], pwe[:, h * P:(h + 1) * P],
                                      e_y[:, c * HD:(c + 1) * HD], start=False, stop=True,
                                      skip_group_check=True)
                    last.then_inc(sem("combined"), 1)

            with pe.Fori(0, MIX // 2) as i:
                experts1(i, 0)
            experts1(MIX // 2, 0, True)
            with pe.Fori(MIX // 2 + 1, E1 // 2) as i:
                experts1(i, SH_UNITS)

            gat(1, 4)

            def dense(tag, u0, experts, unroll, upe, fpu):
                fe = upe * fpu
                body_u, body_f = unroll * upe, unroll * fe
                assert body_u % RING == 0 and body_f % 4 == 0
                mid = [view(scratch, p * N, N) for p in range(4)]
                with pe.Fori(0, experts // unroll) as i:
                    def down(F):
                        U, ft, q = F // fpu, F % fpu, F // fe
                        slot = (u0 + U) % RING
                        pe.wait_ge(sem(f"{tag}_mid"), i * body_f + (F + 1))
                        if F % fe == 0:
                            pe.wait_ge(sem(f"{tag}_yfree"), i * unroll + (q + 1))
                        wd = ring[:, slot, (ft * 12 + KD) * P:(ft * 12 + 12) * P]
                        for h in range(NH):
                            for j in range(2):
                                last = mm(ps[:, 4 + 2 * h + j, 0:HD], mid[F % 4][:, h * P:(h + 1) * P],
                                          wd[:, j * HD:(j + 1) * HD], start=F % fe == 0, stop=F % fe == fe - 1)
                        if ft == fpu - 1:
                            last.then_inc(sem(f"slot{slot}_used"), 1)

                    for F in range(body_f):
                        U, ft = F // fpu, F % fpu
                        slot = (u0 + U) % RING
                        if ft == 0:
                            pe.wait_ge(sem(f"slot{slot}_full"),
                                       i * (16 * body_u // RING) + 16 * ((u0 + U) // RING + 1))
                        for k in range(KD):
                            last = mm(ps[:, F % 4, 0:N], ring[:, slot, (ft * 12 + k) * P:(ft * 12 + k + 1) * P],
                                      xT[:, k, :], start=k == 0, stop=k == KD - 1)
                        last.then_inc(sem(f"{tag}_up"), 1)
                        if F:
                            down(F - 1)
                    down(body_f - 1)

            def scores(act, w, bias):
                for h in range(NH):
                    for k in range(KD):
                        last = mm(ps[:, 3, h * E2:(h + 1) * E2], act[:, k, h * P:(h + 1) * P],
                                  w[:, k * E2:(k + 1) * E2], start=k == 0, stop=k == KD - 1 and bias is None)
                    if bias is not None:
                        last = mm(ps[:, 3, h * E2:(h + 1) * E2], ones[0:1, :], bias, start=False, stop=True)
                last.then_inc(sem("route_scores"), 1)

            def positions():
                for h in range(NH):
                    for hh in range(h + 1):
                        mm(ps[:, 3, h * E2:(h + 1) * E2], tri[:, :] if hh == h else ones[:, :],
                           rt[:, 2, hh, :], start=hh == 0, stop=hh == h)
                for hh in range(NH):
                    last = mm(ps[:, 3, NH * E2:(NH + 1) * E2], ones[:, :], rt[:, 2, hh, :],
                              start=hh == 0, stop=hh == NH - 1)
                last.then_inc(sem("positions"), 1)

            layernorm_T(5)
            normalised(5)
            product_T(U_R2, 0, xT, True, True)
            pe.wait_ge(sem("r2_ready"), 1)
            pe.wait_ge(sem("rows_in"), 32)
            scores(hT, S("wr2"), rw1[:, D:D + E2])
            pe.wait_ge(sem("route_ready"), 1)
            for h in range(NH):
                last = nc.tensor.transpose(ps[0:E2, 2, h * P:(h + 1) * P], rt[:, 5, h, :], ident[:, :])
            last.then_inc(sem("w2T_done"), 1)
            pe.wait_ge(sem("low_tri_set"), 2)
            positions()

            def experts2(t):
                if t:
                    pe.sem_inc(sem("ovw_used"), 1)
                pe.wait_ge(sem("w2T_ready" + t), 1)
                for h in range(NH):
                    for c in range(2):
                        mm(ps[:, 4 + 2 * h + c, 0:HD], wT8[:, h * P:(h + 1) * P],
                           b2r[:, c * HD:(c + 1) * HD], start=True, stop=False, skip_group_check=True)
                pe.wait_ge(sem("onehot2_ready" + t), 1)
                for k in range(KD):
                    for c in range(2):
                        if k:
                            pe.wait_ge(sem(("xsel2_a", "xsel2_v")[c] + t), k)
                        for h in range(NH):
                            last = mm(ps[:, c, :], xn[:, h, k * P:(k + 1) * P],
                                      p2f[:, h, c * 512:(c + 1) * 512], start=h == 0, stop=h == NH - 1)
                        last.then_inc(sem("xsel2_done" + t), 1)
                pe.wait_ge(sem("xsel2_a" + t), KD)
                pe.wait_ge(sem("xsel2_v" + t), KD)

                def unit2(U):
                    return ovw[:, :] if t else ring[:, (U_E2 + U) % RING, :]

                def combine(i):
                    for c in range(2):
                        pe.wait_ge(sem("y2_ready" + t), i * 2 + (c + 1))
                        for h in range(NH):
                            last = mm(ps[:, 4 + 2 * h + c, 0:HD], pwe2[:, h * P:(h + 1) * P],
                                      y2[:, c * HD:(c + 1) * HD], start=False, stop=True,
                                      skip_group_check=True)
                    last.then_inc(sem("combined2" + t), 1)

                def expert(i, first):
                    def down(F):
                        U, ft = F // 3, F % 3
                        pe.wait_ge(sem("mid2" + t), i * FT2 + (F + 1))
                        for c in range(2):
                            b = (ft * 12 + KD) * P + c * HD
                            last = mm(ps[:, 2 + c, 0:HD], mid2[F % 2], unit2(U)[:, b:b + HD],
                                      start=F == 0, stop=F == FT2 - 1)
                            if F == FT2 - 1 and c == 0:
                                last.then_inc(sem("y2_first" + t), 1)
                        if ft == 2:
                            last.then_inc(sem("ovw_used" if t else f"slot{(U_E2 + U) % RING}_used"), 1)

                    for F in range(FT2):
                        U, ft = F // 3, F % 3
                        down_first = F == 1 or F and ft == 0 and t
                        if down_first:
                            down(F - 1)
                        if ft == 0 and t:
                            pe.wait_ge(sem("ovw_full"), i * (16 * UPE2) + 16 * (U + 1))
                        elif ft == 0:
                            pe.wait_ge(sem(f"slot{(U_E2 + U) % RING}_full"),
                                       i * (16 * UPE2 // RING) + 16 * ((U_E2 + U) // RING + 1))
                        if F == 1:
                            pe.wait_ge(sem("pwe2_ready" + t), i + 1)
                        for k in range(KD):
                            b = (ft * 12 + k) * P
                            last = mm(ps[:, F % 2, 0:CAP2], unit2(U)[:, b:b + P],
                                      xsel2[:, k, bass.ds(i * CAP2, CAP2)], start=k == 0, stop=k == KD - 1)
                        last.then_inc(sem("up2" + t), 1)
                        if F == 0:
                            if not first:
                                combine(i - 1)
                            pe.wait_ge(sem("stage2" + t), i + 1)
                            for h in range(NH):
                                last = nc.tensor.transpose(ps[:, 1, (h + 1) * P:(h + 2) * P], pe_in2[:, h, :],
                                                           ident[:, :])
                            last.then_inc(sem("turn2" + t), 1)
                        elif not down_first:
                            down(F - 1)
                    down(FT2 - 1)

                expert(0, True)
                with pe.Fori(1, E2) as i:
                    expert(i, False)
                combine(E2 - 1)

            experts2("")
            overflow(pe, lambda: experts2("_ov"))

            pe.wait_ge(sem("ln_xn"), NH * 7)
            for k in range(KD):
                for h in range(NH):
                    last = mm(feat(0)[:, k, :], xn[:, h, k * P:(k + 1) * P], gcn[:, h, :],
                              start=h == 0, stop=h == NH - 1)
            last.then_inc(sem("agg3_done"), 1)
            pe.wait_ge(sem("agg3_ready"), 1)
            arrived(U_L3G)
            last = product_N(unit(U_L3G), hT, rw1[:, 0:D])
            used(U_L3G, last)

            layernorm_T(7)
            normalised(7)
            scores(xT, S("rw"), None)
            pe.wait_ge(sem("route_ready"), 2)
            positions()

            def sparse3():
                def pair_weights(t, e):
                    return unit(U_E3 + 2 * t + e).rearrange("p (f b n) -> p f b n", f=FT3, b=12)

                def up(t):
                    for e in range(2):
                        arrived(U_E3 + 2 * t + e)
                    for k in range(KD):
                        for e in range(2):
                            c = (2 * t + e) * CAP3
                            last = mm(ps[e * CAP3:(e + 1) * CAP3, t % 2, 0:FT3 * P], xsel3[:, k, c:c + CAP3],
                                      pair_weights(t, e)[:, :, k, :], start=k == 0, stop=k == KD - 1)
                    last.then_inc(sem("e3s_up"), 1)

                def turn(t):
                    pe.wait_ge(sem("e3s_relu"), t + 1)
                    for f in range(FT3):
                        last = nc.tensor.transpose(ps[:, t % 2, f * P:(f + 1) * P], h3[t % 2][:, f * P:(f + 1) * P],
                                                   ident[:, :])
                    last.then_inc(sem("e3s_turn"), 1)

                def down(t):
                    pe.wait_ge(sem("e3s_hT"), t + 1)
                    for c in range(2):
                        for f in range(FT3):
                            for e in range(2):
                                last = mm(ps[e * CAP3:(e + 1) * CAP3, 2 + c, 0:HD],
                                          h3T[:, f, e * CAP3:(e + 1) * CAP3],
                                          unit(U_E3 + 2 * t + e)[:, (f * 12 + KD) * P + c * HD:
                                                                 (f * 12 + KD) * P + (c + 1) * HD],
                                          start=f == 0, stop=f == FT3 - 1)
                                if c and f == FT3 - 1:
                                    used(U_E3 + 2 * t + e, last)

                def scatter(t):
                    pe.wait_ge(sem("y3_a"), t + 1)
                    pe.wait_ge(sem("y3_v"), t + 1)
                    for h in range(NH):
                        for c in range(2):
                            last = mm(ps[:, 4 + 2 * h + c, 0:HD], pw3T[:, t, h * P:(h + 1) * P],
                                      y3[:, c * HD:(c + 1) * HD], start=t == 0, stop=t == PAIRS - 1,
                                      skip_group_check=True)
                    last.then_inc(sem("combined3"), 1)

                pe.wait_ge(sem("onehot3_ready"), 1)
                for k in range(KD):
                    if k >= 2:
                        pe.wait_ge(sem("xsel_odd" if k % 2 else "xsel_even"), KD // 2 + k // 2)
                    for h in range(NH):
                        last = mm(ps[:, k % 2, :], xn[:, h, k * P:(k + 1) * P], p3f[:, h, :],
                                  start=h == 0, stop=h == NH - 1)
                    last.then_inc(sem("xsel_done"), 1)
                pe.wait_ge(sem("xsel_even"), KD)
                pe.wait_ge(sem("xsel_odd"), KD)
                up(0)
                pe.wait_ge(sem("pw3_ready"), 1)
                for t in range(PAIRS):
                    for h in range(NH):
                        last = nc.tensor.transpose(ps[:, 2 + t // 2, (t % 2) * N + h * P:(t % 2) * N + (h + 1) * P],
                                                   p3f[:, h, t * P:(t + 1) * P], ident[:, :])
                last.then_inc(sem("pw3_turn"), 1)
                for t in range(PAIRS):
                    if t >= 2:
                        up(t)
                    elif t == 0:
                        up(1)
                    turn(t)
                    if t:
                        scatter(t - 1)
                    else:
                        pe.wait_ge(sem("pw3T_ready"), 1)
                    down(t)
                scatter(PAIRS - 1)

            either(pe, sparse3, lambda: dense("e3", U_E3, E3, 4, 1, 3))

        @block.scalar
        def _(act):
            A = nc.scalar.activation

            def deviation(n):
                act.wait_ge(sem("ln_var"), n + 1)
                if n == 0:
                    act.wait_ge(sem("ones_set"), 2)
                A(sd[:, :], mv[:, :, 1], ACT.Sqrt, bias=epst[:, 0:1]).then_inc(sem("ln_sd"), 1)

            def take_turned(n):
                act.wait_ge(sem("ln_tp"), turned(n))
                A(xT[:, 0:4, :], feat(0)[:, 0:4, :], ACT.Copy).then_inc(sem("ln_Ta"), 1)

            def layernorm(n):
                deviation(n)
                if n != 6:
                    take_turned(n)

            act.wait_ge(sem("small_in"), 16)
            for n in range(KD):
                if n < KD - 1:
                    act.wait_ge(sem("qg_done"), n + 1)
                else:
                    unit_done(act, U_QG)
                A(qgT[:, n, :], ps[:, 4 + n % 4, :], ACT.Identity, bias=S("bg")[:, n:n + 1]).then_inc(sem("qg_ready"), 1)
                if n == 0:
                    deviation(0)
                if n == 3:
                    act.wait_ge(sem("deg_ready"), 1)
                    A(dis[:, :], deg[:, :], ACT.Sqrt).then_inc(sem("deg_sqrt"), 1)
            take_turned(0)

            for r in range(2):
                for j in range(KD):
                    act.wait_ge(sem("g_done"), KD * r + j + 1)
                    A(view(scratch, 0, REL, KD, N)[:, 0:2, j, :],
                      ps[:, 2 * (j % 2), :].rearrange("p (a b) -> p a b", a=2), ACT.Copy).then_inc(sem("g_copied_a"), 1)
                unit_done(act, (U_RG1, U_RG2)[r] + 3)
                for n in range(KD):
                    last = A(hT[:, n, :], feat(4)[:, n, :], ACT.Relu, bias=S(f"b{r + 1}")[:, n:n + 1])
                last.then_inc(sem("hT_ready"), 1)
                unit_done(act, (U_GT1, U_GT2)[r])
                A(hgT[:, :, :], feat(0), ACT.Copy).then_inc(sem("hg_ready"), 1)
                with act.Fori(0, GATE_CH // BODY_CH) as i:
                    for j in range(BODY_CH):
                        act.wait_ge(sem("gate_sum"), i * BODY_CH + (GATE_CH * r + j + 1))
                        act.wait_ge(sem("gate_sum_v"), i * BODY_CH + (GATE_CH * r + j + 1))
                        A(chunk(j), chunk(j), ACT.Sigmoid).then_inc(sem("gate_sig"), 1)
                act.wait_ge(sem("gate_free"), GATE_CH * (r + 1) + BUFS)
                A(qiT[:, :, :], feat(0), ACT.Copy).then_inc(sem("qi_ready"), 1)
                A(th, feat(0), ACT.Tanh).then_inc(sem("tanh_ready"), 1)
                unit_done(act, (U_GT1, U_GT2)[r] + 2)
                for n in range(KD):
                    last = A(hgT[:, n, :], feat(4)[:, n, :], ACT.Sigmoid, bias=S("bq")[:, n:n + 1])
                    if n % 3 == 2:
                        last.then_inc(sem("alpha_ready"), 1)
                if r == 0:
                    act.wait_ge(sem("hn_nat"), 1)
                    A(xn[:, :, :].rearrange("p h (a b) -> p (h a) b", a=2), ps[:, 0:4, 0:HD], ACT.Copy
                      ).then_inc(sem("hnat_ready"), 1)

            act.wait_ge(sem(f"slot{U_FF0 % RING}_full"), 16 * (U_FF0 // RING + 1))
            A(unit(U_FF0), unit(U_FF0), ACT.Sign).then_inc(sem("sign_ready"), 1)
            layernorm(1)

            def gat(n, lnidx):
                layernorm(lnidx)
                act.wait_ge(sem("ftT_done"), n + 1)
                A(hT[:, :, :], feat(0), ACT.Copy).then_inc(sem("ftT_ready"), 1)
                act.wait_ge(sem("ft_done"), n + 1)
                act.wait_ge(sem("gat_w"), n + 1)
                for h in range(NH):
                    last = A(ft1[:, h, :, 0:HE].rearrange("p (a b) e -> p a b e", a=2),
                             nat(h).rearrange("p a (b e) -> p a b e", e=HE), ACT.Copy)
                last.then_inc(sem("ft_ready"), 1)

                def exponential(gi):
                    act.wait_ge(sem("att_leaky"), n * (HEADS // HG) + gi + 1)
                    act.wait_ge(sem("hmax_ready"), n * (HEADS // HG) + gi + 1)
                    for q in range(HG):
                        for dh in range(NH):
                            last = A(att(gi)[:, q, dh, :], att(gi)[:, q, dh, :], ACT.Exp,
                                     bias=hm[:, gi % 2, 3, q, dh:dh + 1])
                    last.then_inc(sem("att_exp"), 1)

                def copy_turned(gi):
                    for h in range(gi * HG, gi * HG + HG):
                        act.wait_ge(sem("wT_done"), n * HEADS + h + 1)
                        if h >= 2:
                            act.wait_ge(sem("head_done"), n * HEADS + h - 1)
                        A(att_T(h).rearrange("p a b -> p (a b)"), ps[:, 2 + h % 2, :],
                          ACT.Copy).then_inc(sem("wT_ready"), 1)

                NG = HEADS // HG
                act.wait_ge(sem("res_done"), n + 1)
                A(view(qflat, 0, 2 * NH, HD), ps[:, 4:8, 0:HD], ACT.Copy).then_inc(sem("res_ready"), 1)
                for gi in range(NG):
                    exponential(gi)
                    if gi:
                        copy_turned(gi - 1)
                copy_turned(NG - 1)

            gat(0, 2)

            layernorm(3)
            act.wait_ge(sem("score_done"), 1)
            A(sc1[:, :, :].rearrange("p a b -> p (a b)"), ps[:, 3, 0:NH * E1], ACT.Sigmoid
              ).then_inc(sem("score_ready"), 1)
            sg = [view(scratch, 7680 + p * N, N) for p in range(2)]

            def sh_silu(f):
                act.wait_ge(sem("sh_gu"), f + 1)
                if f >= 2:
                    act.wait_ge(sem("sh_act"), f - 1)
                A(sg[f % 2], ps[:, f % 2, 0:N], ACT.Silu).then_inc(sem("sh_silu"), 1)

            def expert1(e, mixed=False):
                act.wait_ge(sem("pwe_turn"), e + 1)
                A(pwe, ps[:, 1, P:3 * P], ACT.Copy).then_inc(sem("pwe_ready"), 1)
                for gi in range(GROUPS):
                    act.wait_ge(sem("e1_gu"), e * GROUPS + (gi + 1))
                    A(e_silu, ps[:, 0, 0:P], ACT.Silu).then_inc(sem("e1_silu"), 1)
                    act.wait_ge(sem("e1_turn"), e * GROUPS + (gi + 1))
                    A(e_hT, ps[:, 1, 0:P], ACT.Copy).then_inc(sem("e1_hT"), 1)
                    if mixed and gi < SH_UNITS:
                        sh_silu(SH_EARLY + 2 * gi)
                        sh_silu(SH_EARLY + 2 * gi + 1)

            for f in range(SH_EARLY):
                sh_silu(f)
            for k in range(0, KD, 2):
                act.wait_ge(sem("xsel_done"), k + 1)
                A(xsel[:, k, :], ps[:, 2 + k % 2, :], ACT.Copy).then_inc(sem("xsel_even"), 1)
            with act.Fori(0, MIX) as i:
                expert1(i)
            expert1(MIX, True)
            with act.Fori(MIX + 1, E1) as i:
                expert1(i)

            gat(1, 4)

            def softmax_exp(n):
                act.wait_ge(sem("route_max"), n)
                for h in range(NH):
                    last = A(rt[:, 1, h, :], rt[:, 0, h, :], ACT.Exp, bias=rsm[:, 0, h:h + 1])
                last.then_inc(sem("route_exp"), 1)

            def dense(tag, experts, unroll, fe):
                body_f = unroll * fe
                mid = [view(scratch, p * N, N) for p in range(4)]
                with act.Fori(0, experts // unroll) as i:
                    for F in range(body_f):
                        act.wait_ge(sem(f"{tag}_up"), i * body_f + (F + 1))
                        A(mid[F % 4], ps[:, F % 4, 0:N], ACT.Relu).then_inc(sem(f"{tag}_mid"), 1)

            layernorm(5)
            unit_done(act, U_R2)
            for n in range(KD):
                last = A(hT[:, n, :], feat(0)[:, n, :], ACT.Relu, bias=S("br1")[:, n:n + 1])
            last.then_inc(sem("r2_ready"), 1)
            softmax_exp(1)

            def experts2(t):
                for k in range(KD):
                    act.wait_ge(sem("xsel2_done" + t), 2 * k + 1)
                    A(xsel2c[:, k, 0, :], ps[:, 0, :], ACT.Copy).then_inc(sem("xsel2_a" + t), 1)
                with act.Fori(0, E2) as i:
                    for F in range(FT2):
                        if F == 1:
                            act.wait_ge(sem("turn2" + t), i + 1)
                            A(pwe2, ps[:, 1, P:3 * P], ACT.Copy).then_inc(sem("pwe2_ready" + t), 1)
                        act.wait_ge(sem("up2" + t), i * FT2 + (F + 1))
                        A(mid2[F % 2], ps[:, F % 2, 0:CAP2], ACT.Relu,
                          bias=S("fb1")[:, bass.ds(i * FT2 + F, 1)]).then_inc(sem("mid2" + t), 1)

            experts2("")
            overflow(act, lambda: experts2("_ov"))
            layernorm(6)
            act.wait_ge(sem("agg3_done"), 1)
            A(hT[:, :, :], feat(0), ACT.Copy).then_inc(sem("agg3_ready"), 1)
            layernorm(7)
            softmax_exp(2)

            def sparse3():
                def relu(t):
                    act.wait_ge(sem("e3s_up"), t + 1)
                    A(h3[t % 2], ps[:, t % 2, 0:FT3 * P], ACT.Relu).then_inc(sem("e3s_relu"), 1)

                for k in range(0, KD, 2):
                    act.wait_ge(sem("xsel_done"), KD + k + 1)
                    A(xsel3[:, k, :], ps[:, 0, :], ACT.Copy).then_inc(sem("xsel_even"), 1)
                relu(0)
                act.wait_ge(sem("pw3_turn"), 1)
                A(pw3T.rearrange("p (a b) n -> p a (b n)", a=2), ps[:, 2:4, :], ACT.Copy
                  ).then_inc(sem("pw3T_ready"), 1)
                for t in range(PAIRS):
                    if t >= 2:
                        relu(t)
                    elif t == 0:
                        relu(1)
                    unit_done(act, U_E3 + 2 * t + 1)
                    A(y3[:, 0:HD], ps[:, 2, 0:HD], ACT.Copy).then_inc(sem("y3_a"), 1)

            either(act, sparse3, lambda: dense("e3", E3, 4, FT3))

        @block.vector
        def _(v):
            link = Chain(v, sem("dve_own"))
            tt, ts, stt = nc.vector.tensor_tensor, nc.vector.tensor_scalar, nc.vector.scalar_tensor_tensor
            copy, red = nc.vector.tensor_copy, nc.vector.tensor_reduce

            def normalise(n):
                for h in range(NH):
                    for j in range(2):
                        last = nc.vector.bn_stats(bnst[:, h, j, :], x[:, h, j * HD:(j + 1) * HD])
                link(last)
                for h in range(NH):
                    last = nc.vector.bn_aggr(mv[:, h, :], bnst[:, h, :, :].rearrange("p a b -> p (a b)"))
                last.then_inc(sem("ln_var"), 1)
                v.wait_ge(sem("ln_sd"), n + 1)
                link(nc.vector.reciprocal(rs[:, :], sd[:, :]))
                for h in range(NH):
                    ts(xn[:, h, :], x[:, h, :], mv[:, h, 0:1], rs[:, h:h + 1], ALU.subtract, ALU.mult
                       ).then_inc(sem("ln_xn"), 1)

            def take_turned(n):
                v.wait_ge(sem("ln_tp"), turned(n))
                copy(xT[:, 4:6, :], feat(0)[:, 4:6, :]).then_inc(sem("ln_Tv"), 1)

            def layernorm(n):
                normalise(n)
                if n != 6:
                    take_turned(n)

            def residual():
                for h in range(NH):
                    last = tt(halves(x, h), nat(h), halves(x, h), ALU.add)
                link(last)

            v.wait_ge(sem("edges_in"), 16)
            link(copy(edf[:, 0:3, :], edi[:, :, :]))
            link(stt(edf[:, 3, :], edf[:, 2, :], float(N), edf[:, 1, :], ALU.mult, ALU.add))
            v.wait_ge(sem("iota_set"), 1)
            link(copy(iota16[:, :], iota[:, :]))
            for c in range(EC):
                if c >= 4:
                    v.wait_ge(sem("onehot_used"), c - 3)
                s_oh, k_oh = onehots(c)
                ts(s_oh, iota16[:, 0:N], edf[:, 0, c:c + 1], None, ALU.is_equal)
                ts(k_oh, iota16[:, :], edf[:, 3, c:c + 1], None, ALU.is_equal).then_inc(sem("onehot_ready"), 1)
            v.wait_ge(sem("onehot_used"), EC)
            for h in range(NH):
                copy(adj[:, h, 0:512], ps[:, 2 * h, :])
                last = copy(adj[:, h, 512:768], ps[:, 2 * h + 1, 0:N])
            last.then_inc(sem("counts_ready"), 1)
            v.wait_ge(sem("counts_ready"), 1)
            link(tt(cT[:, :, :], adj[:, :, 0:N], adj[:, :, N:2 * N], ALU.add))
            tt(cT[:, :, :], cT[:, :, :], adj[:, :, 2 * N:3 * N], ALU.add).then_inc(sem("counts_ready"), 1)
            v.wait_ge(sem("x_in"), 16)
            normalise(0)
            rcnt = view(scratch, 2048, 2, HD)
            v.wait_ge(sem("graph_done"), 1)
            link(ts(rcnt, ps[:, 0:2, 0:HD], 1.0, None, ALU.max))
            link(nc.vector.reciprocal(rcnt, rcnt))
            for h in range(NH):
                last = tt(halves(adj, h), halves(adj, h), rcnt, ALU.mult)
            last.then_inc(sem("adj_ready"), 1)
            v.wait_ge(sem("graph_done"), 2)
            link(copy(cN[:, :, :].rearrange("p a b -> p (a b)"), ps[:, 2, :]))
            ts(far[:, :, :], cN[:, :, :], 0.0, FAR, ALU.is_equal, ALU.mult)
            link(red(deg[:, :], cN[:, :, :], AX.X, ALU.add))
            ts(deg[:, :], deg[:, :], 1.0, None, ALU.add).then_inc(sem("deg_ready"), 1)
            v.wait_ge(sem("deg_sqrt"), 1)
            nc.vector.reciprocal(dis[:, :], dis[:, :]).then_inc(sem("dis_ready"), 1)
            link(copy(gcn[:, :, :], cT[:, :, :]))
            v.wait_ge(sem("ident_set"), 1)
            for h in range(NH):
                last = tt(gcn[:, h, h * P:(h + 1) * P], gcn[:, h, h * P:(h + 1) * P], ident[:, :], ALU.add)
            link(last)
            v.wait_ge(sem("graph_done"), 3)
            for h in range(NH):
                last = stt(gcn[:, h, :], gcn[:, h, :], dis[:, h:h + 1], ps[:, 3, 0:N], ALU.mult, ALU.mult)
            last.then_inc(sem("gcn_ready"), 1)
            take_turned(0)

            for r in range(2):
                for j in range(KD):
                    v.wait_ge(sem("g_done"), KD * r + j + 1)
                    copy(view(scratch, 0, REL, KD, N)[:, 2, j, :], ps[:, 2 * (j % 2) + 1, 0:N]
                         ).then_inc(sem("g_copied_v"), 1)

                def add_row(i, j):
                    v.wait_ge(sem("gate_free"), i * BODY_CH + (GATE_CH * r + j + 1))
                    tt(chunk(j)[:, 0:1, :, :], node_rows(hgT, i, j, 0, 1), query_rows(qgT, i, j, 0, 1), ALU.add
                       ).then_inc(sem("gate_sum_v"), 1)

                def gated_rows(i, last):
                    for j in range(BODY_CH):
                        done = i * BODY_CH + (GATE_CH * r + j + 1)
                        v.wait_ge(sem("gate_sig"), done)
                        tt(chunk(j), chunk(j), query_rows(qTs, i, j, 0, LC), ALU.mult).then_inc(sem("gate_prod"), 1)
                        if not last or j + 2 < BODY_CH:
                            add_row(i + (j + 2) // BODY_CH, (j + 2) % BODY_CH)
                        v.wait_ge(sem("gate_prod"), done)
                        n = paired(j)
                        tt(chunk(j)[:, 0:n, :, :], chunk(j)[:, 0:n, :, :], chunk(j)[:, LC - n:LC, :, :], ALU.add
                           ).then_inc(sem("gate_ready"), 1)

                v.wait_ge(sem("hg_ready"), r + 1)
                v.wait_ge(sem("qg_ready"), KD)
                add_row(0, 0)
                add_row(0, 1)
                with v.Fori(0, GATE_CH // BODY_CH - 1) as i:
                    gated_rows(i, False)
                gated_rows(GATE_CH // BODY_CH - 1, True)
                v.wait_ge(sem("tanh_ready"), r + 1)
                link(tt(th, th, hT[:, :, :], ALU.subtract))
                for a in range(2):
                    v.wait_ge(sem("alpha_ready"), 2 * r + a + 1)
                    b = slice(3 * a, 3 * a + 3)
                    link(tt(th[:, b, :], th[:, b, :], hgT[:, b, :], ALU.mult))
                    tt(hT[:, b, :], hT[:, b, :], th[:, b, :], ALU.add).then_inc(sem("hn_ready"), 1)
            v.wait_ge(sem("hn_nat"), 2)
            residual()

            layernorm(1)
            unit_done(v, U_FF0)
            residual()

            def gat(n, lnidx):
                link(nc.vector.memset(gflat[:, 0:2 * P + 4 * KD], 0.0))
                for q in range(2):
                    pr = slice(q * HE, (q + 1) * HE)
                    copy(bd[pr, 0, pr], S(f"fc{n + 1}")[pr, :])
                    copy(bd[pr, 1, pr], S(f"res{n + 1}")[pr, :])
                    copy(al[pr, :, q], S(f"al{n + 1}")[pr, :])
                    copy(ar[pr, :, q], S(f"ar{n + 1}")[pr, :])
                nc.vector.memset(ft1[:, :, :, HE], 1.0).then_inc(sem("gat_w"), 1)
                layernorm(lnidx)
                NG = HEADS // HG

                v.wait_ge(sem("a2_done"), n + 1)
                copy(a2[:, :, :].rearrange("p a b -> p (a b)"), ps[:, 3, 0:NH * HEADS]).then_inc(sem("a2_ready"), 1)
                v.wait_ge(sem("a2_ready"), n + 1)
                for gi in range(NG):
                    s, m = att(gi), hm[:, gi % 2, :, :, :]
                    v.wait_ge(sem("arow_done"), n * NG + gi + 1)
                    rows = ps[:, 0:2, :].rearrange("p a (b n) -> p (a b) n", b=2)
                    for q in range(HG):
                        for dh in range(NH):
                            last = stt(s[:, q, dh, :], rows[:, q, :], a2[:, dh, gi * HG + q:gi * HG + q + 1],
                                       far[:, dh, :], ALU.add, ALU.add)
                    last.then_inc(sem("arow_taken"), 1)
                    v.wait_ge(sem("arow_taken"), n * NG + gi + 1)
                    if gi >= 2:
                        v.wait_ge(sem("att_exp"), n * NG + gi - 1)
                    red(m[:, 0, :, :], s, AX.X, ALU.max).then_inc(sem("att_max"), 1)
                    v.wait_ge(sem("att_max"), n * NG + gi + 1)
                    sf = s.rearrange("p a b c -> p (a b c)")
                    stt(sf, sf, 0.2, sf, ALU.mult, ALU.max).then_inc(sem("att_leaky"), 1)
                    link(ts(m[:, 1, :, :], m[:, 0, :, :], 0.2, None, ALU.mult))
                    link(tt(m[:, 2, :, :], m[:, 0, :, :], m[:, 1, :, :], ALU.max))
                    ts(m[:, 3, :, :], m[:, 2, :, :], -1.0, None, ALU.mult).then_inc(sem("hmax_ready"), 1)
                v.wait_ge(sem("head_done"), (n + 1) * HEADS)
                v.wait_ge(sem("res_ready"), n + 1)
                t = view(scratch, 0, NH, 2, HD)
                res = view(qflat, 0, NH, 2, HD)
                for dh in range(NH):
                    agg = ps[:, 4 + 2 * dh:6 + 2 * dh, 0:6 * (HE + 1)].rearrange("p a (b e) -> p a b e", e=HE + 1)
                    rd = rden[:, dh, :].rearrange("p (a b) -> p a b", a=2)
                    link(ts(rd, agg[:, :, :, HE], 1e-16, None, ALU.max))
                    link(nc.vector.reciprocal(rd, rd))
                    for a in range(2):
                        last = tt(t[:, dh, a, :].rearrange("p (b e) -> p b e", e=HE), agg[:, a, :, 0:HE],
                                  rd[:, a, :].unsqueeze(2).to_broadcast([P, 6, HE]), ALU.mult)
                    link(last)
                    link(tt(t[:, dh, :, :], t[:, dh, :, :], res[:, dh, :, :], ALU.add))
                    link(stt(halves(x, dh), t[:, dh, :, :], 0.0, halves(x, dh), ALU.max, ALU.add))

            gat(0, 2)

            layernorm(3)
            v.wait_ge(sem("score_ready"), 1)
            v.wait_ge(sem("lt_set"), 1 + NH)
            lt = view(gflat, 0, NH, N)
            jk = view(gflat, 2 * N, 2, NH, 2, N)
            hs = [view(scratch, 6656 + p * N, N) for p in range(4)]
            sg = [view(scratch, 7680 + p * N, N) for p in range(2)]

            def sh_act(f):
                v.wait_ge(sem("sh_silu"), f + 1)
                tt(hs[f % 4], sg[f % 2], ps[:, f % 2, N:2 * N], ALU.mult).then_inc(sem("sh_act"), 1)

            for e in range(E1):
                if e >= 2:
                    v.wait_ge(sem("rank_taken"), e - 1)
                v.wait_ge(sem("srow_done"), e + 1)
                for h in range(NH):
                    row = ps[:, 2 + e % 2, 0:N]
                    ts(jk[:, e % 2, h, 0, :], row, sc1[:, h, e:e + 1], None, ALU.is_gt, ALU.add,
                       accum_out=cnt[:, 0, h, e:e + 1])
                    w = (h + 1) * P
                    last = stt(jk[:, e % 2, h, 1, 0:w], row[:, 0:w], sc1[:, h, e:e + 1], lt[:, h, 0:w], ALU.is_equal, ALU.mult,
                               accum_out=cnt[:, 1, h, e:e + 1])
                last.then_inc(sem("rank_taken"), 1)
                if e >= 4 and e % 4 == 1:
                    sh_act(e // 4 - 1)
            sh_act(SH_EARLY - 1)
            v.wait_ge(sem("rank_taken"), E1)
            link(tt(cnt[:, 2, :, :], cnt[:, 0, :, :], cnt[:, 1, :, :], ALU.add))
            p1 = view(qflat, 0, NH, E1, SLOTS)
            for h in range(NH):
                last = tt(p1[:, h, :, :], iota[:, 0:SLOTS].unsqueeze(1).to_broadcast([P, E1, SLOTS]),
                          cnt[:, 2, h, :].unsqueeze(2).to_broadcast([P, E1, SLOTS]), ALU.is_equal)
            last.then_inc(sem("onehot1_ready"), 1)
            for k in range(1, KD, 2):
                v.wait_ge(sem("xsel_done"), k + 1)
                copy(xsel[:, k, :], ps[:, 2 + k % 2, :]).then_inc(sem("xsel_odd"), 1)
            for h in range(NH):
                last = tt(p1[:, h, :, :], p1[:, h, :, :],
                          sc1[:, h, :].unsqueeze(2).to_broadcast([P, E1, SLOTS]), ALU.mult)
            last.then_inc(sem("pw_ready"), 1)

            def expert1(e, last_unit, mixed=False):
                for gi in range(GROUPS):
                    v.wait_ge(sem("e1_silu"), e * GROUPS + (gi + 1))
                    tt(e_h, e_silu, ps[:, 0, P:2 * P], ALU.mult).then_inc(sem("e1_act"), 1)
                    if mixed and gi < SH_UNITS:
                        sh_act(SH_EARLY + 2 * gi)
                        sh_act(SH_EARLY + 2 * gi + 1)
                v.wait_ge(sem(f"slot{last_unit % RING}_used"),
                          e * (2 * GROUPS // RING) + (last_unit // RING + 1))
                copy(e_y.rearrange("p (a b) -> p a b", a=2), ps[:, 2:4, 0:HD]).then_inc(sem("y1_ready"), 1)

            with v.Fori(0, MIX) as i:
                expert1(i, pair_unit(0, GROUPS - 1) + 1)
            expert1(MIX, pair_unit(MIX, GROUPS - 1) + 1 - MIX * 2 * GROUPS, True)
            with v.Fori(MIX + 1, E1) as i:
                expert1(i, pair_unit(MIX + 1, GROUPS - 1) + 1 - (MIX + 1) * 2 * GROUPS)
            v.wait_ge(sem("combined"), E1)
            residual()

            gat(1, 4)

            def route(n, keep, before):
                v.wait_ge(sem("route_scores"), n)
                link(copy(rt[:, 0, :, :].rearrange("p a b -> p (a b)"), ps[:, 3, 0:NH * E2]))
                link(red(rsm[:, 1, :], rt[:, 0, :, :], AX.X, ALU.max))
                ts(rsm[:, 0, :], rsm[:, 1, :], -1.0, None, ALU.mult).then_inc(sem("route_max"), 1)
                v.wait_ge(sem("route_exp"), n)

                def mask(src):
                    for h in range(NH):
                        a = src[:, h, :].unsqueeze(1).to_broadcast([P, E2, E2])
                        b = src[:, h, :].unsqueeze(2).to_broadcast([P, E2, E2])
                        tt(rk[:, 0, h, :, :], a, b, ALU.is_gt)
                        last = tt(rk[:, 1, h, :, :], a, b, ALU.is_equal)
                    link(last)
                    for h in range(NH):
                        last = tt(rk[:, 1, h, :, :], rk[:, 1, h, :, :], low[:, :, :], ALU.mult)
                    link(last)
                    link(tt(rk[:, 0, :, :, :], rk[:, 0, :, :, :], rk[:, 1, :, :, :], ALU.add))
                    link(red(rt[:, 2, :, :], rk[:, 0, :, :, :].rearrange("p h a b -> p (h a) b"), AX.X, ALU.add))
                    link(ts(rt[:, 2, :, :], rt[:, 2, :, :], float(keep), None, ALU.is_lt))

                v.wait_ge(sem("low_tri_set"), 2)
                if before:
                    mask(rt[:, 0, :, :])
                    link(tt(rt[:, 1, :, :], rt[:, 1, :, :], rt[:, 2, :, :], ALU.mult))
                link(red(rsm[:, 2, :], rt[:, 1, :, :], AX.X, ALU.add))
                link(nc.vector.reciprocal(rsm[:, 3, :], rsm[:, 2, :]))
                last = tt(rt[:, 5, :, :], rt[:, 1, :, :], rsm[:, 3, :].unsqueeze(2).to_broadcast([P, NH, E2]), ALU.mult)
                if before:
                    last.then_inc(sem("route_ready"), 1)
                    v.wait_ge(sem("route_ready"), n)
                else:
                    link(last)
                    mask(rt[:, 5, :, :])
                    tt(rt[:, 5, :, :], rt[:, 5, :, :], rt[:, 2, :, :], ALU.mult).then_inc(sem("route_ready"), 1)
                    v.wait_ge(sem("route_ready"), n)

            def slots(n):
                v.wait_ge(sem("positions"), n)
                link(red(rsm[:, 0, 0:1], ps[:, 3, NH * E2:(NH + 1) * E2], AX.X, ALU.max))
                copy(over[:, n - 1:n], rsm[:, 0, 0:1]).then_inc(sem("most_ready"), 1)
                link(stt(rt[:, 3, :, :].rearrange("p a b -> p (a b)"), rt[:, 2, :, :].rearrange("p a b -> p (a b)"),
                         -1024.0, ps[:, 3, 0:NH * E2], ALU.mult, ALU.add))
                link(ts(rt[:, 3, :, :], rt[:, 3, :, :], 1024.0, None, ALU.add))

            def dense(tag, u0, experts, unroll, upe):
                v.sem_inc(sem(f"{tag}_yfree"), 1)
                with v.Fori(0, experts // unroll) as i:
                    for q in range(unroll):
                        ul = u0 + (q + 1) * upe - 1
                        v.wait_ge(sem(f"slot{ul % RING}_used"), i * (unroll * upe // RING) + (ul // RING + 1))
                        for h in range(NH):
                            last = stt(halves(x, h), nat(h), rt[:, 5, h, bass.ds(i * unroll + q, 1)], halves(x, h),
                                       ALU.mult, ALU.add)
                        last.then_inc(sem(f"{tag}_yfree"), 1)
                        v.wait_ge(sem(f"{tag}_yfree"), i * unroll + (q + 2))

            layernorm(5)
            route(1, 2, True)
            v.wait_ge(sem("w2T_done"), 1)
            copy(wT8[:, :], ps[0:E2, 2, 0:N]).then_inc(sem("w2T_ready"), 1)
            slots(1)
            link(ts(rt[:, 4, :, :], rt[:, 3, :, :], -float(CAP2), None, ALU.add))

            def experts2(t, link):
                q = rt[:, 4 if t else 3, :, :]
                if t:
                    nc.vector.memset(wT8[:, :], 0.0).then_inc(sem("w2T_ready" + t), 1)
                for h in range(NH):
                    last = tt(p2[:, h, :, :], iota[:, 0:CAP2].unsqueeze(1).to_broadcast([P, E2, CAP2]),
                              q[:, h, :].unsqueeze(2).to_broadcast([P, E2, CAP2]), ALU.is_equal)
                last.then_inc(sem("onehot2_ready" + t), 1)
                for k in range(KD):
                    v.wait_ge(sem("xsel2_done" + t), 2 * k + 2)
                    copy(xsel2c[:, k, 1, :], ps[:, 1, :]).then_inc(sem("xsel2_v" + t), 1)
                for h in range(NH):
                    last = tt(p2[:, h, :, :], p2[:, h, :, :],
                              rt[:, 5, h, :].unsqueeze(2).to_broadcast([P, E2, CAP2]), ALU.mult)
                last.then_inc(sem("pw2_ready" + t), 1)
                with v.Fori(0, E2) as i:
                    v.wait_ge(sem("y2_first" + t), i + 1)
                    copy(y2[:, 0:HD], ps[:, 2, 0:HD]).then_inc(sem("y2_ready" + t), 1)
                    ul = U_E2 + UPE2 - 1
                    if t:
                        v.wait_ge(sem("ovw_used"), i * UPE2 + (UPE2 + 1))
                    else:
                        v.wait_ge(sem(f"slot{ul % RING}_used"), i * (UPE2 // RING) + (ul // RING + 1))
                    copy(y2[:, HD:D], ps[:, 3, 0:HD]).then_inc(sem("y2_ready" + t), 1)
                v.wait_ge(sem("combined2" + t), E2)
                for h in range(NH):
                    last = tt(halves(x, h), nat(h), halves(x, h), ALU.add)
                link(last)

            experts2("", link)
            overflow(v, lambda: experts2("_ov", Chain(v, sem("dve_own_ov"))))
            layernorm(6)
            unit_done(v, U_L3G)
            residual()
            layernorm(7)
            route(2, 1, False)
            slots(2)

            def sparse3():
                for h in range(NH):
                    last = tt(p3[:, h, :, :], iota[:, 0:CAP3].unsqueeze(1).to_broadcast([P, E3, CAP3]),
                              rt[:, 3, h, :].unsqueeze(2).to_broadcast([P, E3, CAP3]), ALU.is_equal)
                last.then_inc(sem("onehot3_ready"), 1)
                for k in range(1, KD, 2):
                    v.wait_ge(sem("xsel_done"), KD + k + 1)
                    copy(xsel3[:, k, :], ps[:, 1, :]).then_inc(sem("xsel_odd"), 1)
                for h in range(NH):
                    last = tt(p3[:, h, :, :], p3[:, h, :, :],
                              rt[:, 5, h, :].unsqueeze(2).to_broadcast([P, E3, CAP3]), ALU.mult)
                last.then_inc(sem("pw3_ready"), 1)
                for t in range(PAIRS):
                    v.wait_ge(sem("e3s_turn"), t + 1)
                    copy(h3T, ps[:, t % 2, 0:FT3 * P].rearrange("p (f n) -> p f n", f=FT3)
                         ).then_inc(sem("e3s_hT"), 1)
                    unit_done(v, U_E3 + 2 * t + 1)
                    copy(y3[:, HD:D], ps[:, 3, 0:HD]).then_inc(sem("y3_v"), 1)
                v.wait_ge(sem("combined3"), PAIRS)
                for h in range(NH):
                    last = tt(halves(x, h), nat(h), halves(x, h), ALU.add)
                last.then_inc(sem("e3_yfree"), 1)
                v.wait_ge(sem("e3_yfree"), 1)

            either(v, sparse3, lambda: dense("e3", U_E3, E3, 4, 1))
            nc.vector.memset(rsm[:, :, :], 0.0).then_inc(sem("result"), 1)


def kernel(**inputs):
    import numpy as np
    import concourse.bacc as bacc
    from concourse.bass_utils import run_bass_kernel_spmd

    a = {k: np.asarray(v) for k, v in inputs.items()}

    def rows(w):
        return w.reshape(KD, P, -1).transpose(1, 0, 2).reshape(P, -1)

    def cols(b):
        return b.reshape(-1, P).T

    def twice(w):
        return np.concatenate([w.T, w.T])

    weights = np.empty((UNITS, P, UW), np.float32)

    def put(u, w):
        weights[u] = rows(w)

    wg, wq = a["L0_gnn_Wg"], a["L0_gnn_Wq"]
    put(U_QG, wg[:, D:].T)
    for r, (ur, ug) in enumerate(((U_RG1, U_GT1), (U_RG2, U_GT2))):
        put(ur, a[f"L0_gnn_W_root{r + 1}"])
        for rel in range(REL):
            put(ur + 1 + rel, a[f"L0_gnn_W_rel{r + 1}"][rel])
        put(ug, wg[:, :D].T)
        put(ug + 1, wq[:, :D].T)
        put(ug + 2, wq[:, D:].T)
    put(U_FF0, a["L0_ffn_weight"].T)

    def up_blocks(w, f):
        return w.reshape(w.shape[0], -1, f, P, KD, P).transpose(0, 1, 5, 2, 4, 3)

    def down_blocks(w, f):
        return w.reshape(w.shape[0], KD, P, -1, f, P).transpose(0, 3, 5, 4, 1, 2)

    shared = np.empty((SH_FT // 2, P, UW), np.float32)
    o = shared.reshape(1, -1, P, 2, 18, P)
    o[:, :, :, :, 0:6] = up_blocks(a["L1_ffn_Ws_g"][None], 2)
    o[:, :, :, :, 6:12] = up_blocks(a["L1_ffn_Ws_u"][None], 2)
    o[:, :, :, :, 12:18] = down_blocks(a["L1_ffn_Ws_d"][None], 2)
    for f in range(0, SH_FT, 2):
        weights[shared_unit(f)] = shared[f // 2]
    experts = np.empty((E1, GROUPS, 2, P, UB, P), np.float32)
    for i, w in enumerate((a["L1_ffn_Wg"], a["L1_ffn_Wu"])):
        experts[:, :, :, :, 0:24].reshape(E1, GROUPS, 2, P, 3, 4, 2, P)[..., i, :] = \
            w.reshape(E1, GROUPS, 4, P, 2, 3, P).transpose(0, 1, 4, 6, 5, 2, 3)
    experts[:, :, :, :, 24:36] = a["L1_ffn_Wd"].reshape(E1, KD, P, GROUPS, 2, 2, P).transpose(
        0, 3, 4, 6, 5, 1, 2).reshape(E1, GROUPS, 2, P, 12, P)
    for e in range(E1):
        for g in range(GROUPS):
            weights[pair_unit(e, g):pair_unit(e, g) + 2] = experts[e, g].reshape(2, P, UW)
    put(U_R2, a["L2_ffn_Wr1"].T)
    o = weights[U_E2:U_L3G].reshape(E2, -1, P, 3, 12, P)
    o[:, :, :, :, 0:6] = up_blocks(a["L2_ffn_W1"], 3)
    o[:, :, :, :, 6:12] = down_blocks(a["L2_ffn_W2"], 3)
    put(U_L3G, a["L3_gnn_W"])
    o = weights[U_E3:UNITS].reshape(E3, 1, P, 3, 12, P)
    o[:, :, :, :, 0:6] = up_blocks(a["L3_ffn_wi"].transpose(0, 2, 1), 3)
    o[:, :, :, :, 6:12] = down_blocks(a["L3_ffn_wo"].transpose(0, 2, 1), 3)

    small = np.concatenate([
        cols(a["L0_gnn_b1"]), cols(a["L0_gnn_b2"]), cols(a["L0_gnn_bg"]), cols(a["L0_gnn_bq"]),
        cols(a["L2_ffn_br1"]), cols(a["L2_ffn_b1"].reshape(-1)),
        rows(a["L1_ffn_gate_weight"].T), rows(a["L2_ffn_Wr2"].T), rows(a["L3_ffn_router_w"]),
        twice(a["L1_gnn_W_fc"]), twice(a["L1_gnn_W_res"]), cols(a["L1_gnn_attn_l"].reshape(-1)),
        cols(a["L1_gnn_attn_r"].reshape(-1)),
        twice(a["L2_gnn_W"]), twice(a["L2_gnn_W_res"]), cols(a["L2_gnn_attn_l"].reshape(-1)),
        cols(a["L2_gnn_attn_r"].reshape(-1))], axis=1)
    arrays = {
        "weights": weights,
        "small": small,
        "edges": np.stack([a["src"], a["dst"], a["edge_type_3"]]).reshape(3, P, EC).transpose(1, 0, 2),
        "x": a["x"].reshape(NH, P, D).transpose(1, 0, 2),
        "qT": a["L0_gnn_query_embs"].reshape(B * L, KD, P).transpose(2, 1, 0),
        "rows8": a["L2_ffn_b2"],
        "row1": np.concatenate([a["L3_gnn_b"], a["L2_ffn_br2"]])[None],
    }
    nc = bacc.Bacc("TRN2", target_bir_lowering=False, num_devices=1)
    arrays = {f"in_{k}": np.ascontiguousarray(v) for k, v in arrays.items()}
    aps = [nc.dram_tensor(k, v.shape, mybir.dt.from_np(v.dtype), kind="ExternalInput").ap() for k, v in arrays.items()]
    out = nc.dram_tensor("out", (P, NH, D), F32, kind="ExternalOutput").ap()
    build(nc, *aps, out)
    r = run_bass_kernel_spmd(nc, [arrays], core_ids=[0])
    return r.results[0]["out"].transpose(1, 0, 2).reshape(N, D)
```
